# Optimizing a Trainium2 kernel written in Bass

```python
import numpy as np
import jax
import jax.numpy as jnp

def _softmax(x, axis=-1):
    return jax.nn.softmax(x, axis=axis)

def _gelu(x):
    return jax.nn.gelu(x, approximate=True)

def _silu(x):
    return jax.nn.silu(x)

def _sigmoid(x):
    return jax.nn.sigmoid(x)

def _layernorm(x, axis=-1, eps=1e-05):
    m = jnp.mean(x, axis=axis, keepdims=True)
    v = jnp.var(x, axis=axis, keepdims=True)
    return (x - m) / jnp.sqrt(v + eps)

def _scatter_add(tgt, idx, src, axis=0):
    return tgt.at[idx].add(src)

def _segment_sum(src, seg, n):
    return jax.ops.segment_sum(src, seg, n)
kernel_name = 'mk_gnn_ffn_d1_gnn_r8_346596'

def setup_inputs(seed: int=0):
    np.random.seed(seed)
    _w = jnp.asarray

    def _rec_inputs():
        import jax
        import jax.numpy as jnp
        _gk = jax.random.key(seed)
        x = -6.415e-05 + 1 * jax.random.normal(jax.random.fold_in(_gk, 1), (2500, 512), jnp.float32)
        src = jax.random.randint(jax.random.fold_in(_gk, 2), (40000,), 0, 2500, jnp.int32)
        dst = jax.random.randint(jax.random.fold_in(_gk, 3), (40000,), 0, 2500, jnp.int32)
        _o = jnp.argsort(dst, stable=True)
        src = src[_o]
        dst = dst[_o]
        return (x, src, dst)
    x, src, dst = _rec_inputs()

    def _L0_gnn_setup():
        import jax, jax.numpy as jnp
        import numpy as np
        N = 2500
        E_RAND = 17500
        D_IN = 512
        D_OUT = 512
        SLOPE = 0.2
        key = jax.random.key(seed)
        k1, k2, k3, k4 = jax.random.split(key, 4)
        nodes = jax.random.normal(k1, (N, D_IN), dtype=jnp.float32)
        ei = jax.random.randint(k2, (2, E_RAND), 0, N, dtype=jnp.int64)
        loops = jnp.arange(N, dtype=jnp.int64)
        edge_index = jnp.concatenate([ei, jnp.stack([loops, loops])], axis=1)
        W = jax.random.normal(k3, (D_IN, D_OUT), dtype=jnp.float32) * (1.0 / np.sqrt(D_IN))
        b_w = jnp.zeros((D_OUT,), dtype=jnp.float32)
        a = jax.random.normal(k4, (2 * D_OUT,), dtype=jnp.float32) * (1.0 / np.sqrt(2 * D_OUT))
        b_a = jnp.zeros((), dtype=jnp.float32)
        return {'nodes': nodes, 'edge_index': edge_index, 'W': W, 'b_w': b_w, 'a': a, 'b_a': b_a}
    _L0_gnn_all = _L0_gnn_setup()
    _L0_gnn_in = {k: v for k, v in _L0_gnn_all.items() if k in ('W', 'b_w', 'a', 'b_a')}
    del _L0_gnn_all

    def _L0_ffn_setup():
        import jax, jax.numpy as jnp
        import numpy as np
        NUM_EXPERTS = 8
        TOP_K = 2
        HIDDEN = 512
        INTERMEDIATE = 256
        BATCH, SEQ = (8, 256)
        key = jax.random.key(seed)
        ks = jax.random.split(key, 7)
        s_in = 1.0 / np.sqrt(HIDDEN)
        s_mid = 1.0 / np.sqrt(INTERMEDIATE)
        return {'x': jax.random.normal(ks[0], (BATCH, SEQ, HIDDEN), jnp.float32), 'Wg': jax.random.normal(ks[1], (HIDDEN, NUM_EXPERTS), jnp.float32) * s_in, 'bg': jnp.zeros((NUM_EXPERTS,), jnp.float32), 'W1': jax.random.normal(ks[2], (NUM_EXPERTS, HIDDEN, INTERMEDIATE), jnp.float32) * s_in, 'b1': jnp.zeros((NUM_EXPERTS, INTERMEDIATE), jnp.float32), 'W2': jax.random.normal(ks[3], (NUM_EXPERTS, INTERMEDIATE, HIDDEN), jnp.float32) * s_mid, 'b2': jnp.zeros((NUM_EXPERTS, HIDDEN), jnp.float32)}
    _L0_ffn_all = _L0_ffn_setup()
    _L0_ffn_in = {k: v for k, v in _L0_ffn_all.items() if k in ('Wg', 'bg', 'W1', 'b1', 'W2', 'b2')}
    del _L0_ffn_all
    return {'x': x, 'src': src, 'dst': dst, 'L0_gnn_W': _L0_gnn_in['W'], 'L0_gnn_b_w': _L0_gnn_in['b_w'], 'L0_gnn_a': _L0_gnn_in['a'], 'L0_gnn_b_a': _L0_gnn_in['b_a'], 'L0_ffn_Wg': _L0_ffn_in['Wg'], 'L0_ffn_bg': _L0_ffn_in['bg'], 'L0_ffn_W1': _L0_ffn_in['W1'], 'L0_ffn_b1': _L0_ffn_in['b1'], 'L0_ffn_W2': _L0_ffn_in['W2'], 'L0_ffn_b2': _L0_ffn_in['b2']}

def reference(x, src, dst, L0_gnn_W, L0_gnn_b_w, L0_gnn_a, L0_gnn_b_a, L0_ffn_Wg, L0_ffn_bg, L0_ffn_W1, L0_ffn_b1, L0_ffn_W2, L0_ffn_b2):
    import jax
    import jax.numpy as jnp

    def _L0_gnn_ref(nodes, edge_index, W, b_w, a, b_a):
        import jax, jax.numpy as jnp
        import numpy as np
        N = 2500
        E_RAND = 17500
        D_IN = 512
        D_OUT = 512
        SLOPE = 0.2
        h = nodes @ W + b_w
        src = edge_index[0]
        dst = edge_index[1]
        s_dst = h @ a[:D_OUT]
        s_src = h @ a[D_OUT:]
        e = jax.nn.leaky_relu(s_dst[dst] + s_src[src] + b_a, negative_slope=SLOPE)
        w = jnp.exp(e)
        denom = jax.ops.segment_sum(w, dst, num_segments=N)
        alpha = w / denom[dst]
        out = jax.ops.segment_sum(alpha[:, None] * h[src], dst, num_segments=N)
        return out

    def _L0_ffn_ref(x, Wg, bg, W1, b1, W2, b2):
        import jax, jax.numpy as jnp
        import numpy as np
        NUM_EXPERTS = 8
        TOP_K = 2
        HIDDEN = 512
        INTERMEDIATE = 256
        BATCH, SEQ = (8, 256)
        B, S, H = x.shape
        xf = x.reshape(B * S, H)
        logits = xf @ Wg + bg
        probs = jax.nn.softmax(logits, axis=-1)
        _, top_idx = jax.lax.top_k(probs, TOP_K)
        mask = jnp.any(top_idx[:, :, None] == jnp.arange(NUM_EXPERTS)[None, None, :], axis=1)
        comb = probs * mask.astype(probs.dtype)
        out = jnp.zeros_like(xf)
        for e in range(NUM_EXPERTS):
            h = jax.nn.gelu(xf @ W1[e] + b1[e])
            y = h @ W2[e] + b2[e]
            out = out + comb[:, e:e + 1] * y
        return out.reshape(B, S, H)
    edge_index = jnp.stack([src, dst])
    x = x + _L0_gnn_ref(_layernorm(x, axis=-1), edge_index, L0_gnn_W, L0_gnn_b_w, L0_gnn_a, L0_gnn_b_a)
    x = x + _L0_ffn_ref(_layernorm(x, axis=-1)[None], L0_ffn_Wg, L0_ffn_bg, L0_ffn_W1, L0_ffn_b1, L0_ffn_W2, L0_ffn_b2)[0]
    return x

_drawn_inputs = setup_inputs


def setup_inputs(seed=0):
    import zlib

    import numpy as np

    out = dict(_drawn_inputs(seed))
    spreads = {'L0_gnn_b_w': (0.0, 0.1),
     'L0_ffn_bg': (0.0, 0.1),
     'L0_ffn_b1': (0.0, 0.295),
     'L0_ffn_b2': (0.0, 0.1)}
    factors = {}
    for name, (base, spread) in spreads.items():
        noise = np.random.default_rng([zlib.crc32(name.encode()), seed]).standard_normal(out[name].shape)
        drawn = base * np.exp(spread * noise) if base else spread * noise
        out[name] = jnp.asarray(drawn.astype(out[name].dtype))
    for name, factor in factors.items():
        out[name] = (out[name] * factor).astype(out[name].dtype)
    return out
```

```python
from contextlib import ExitStack

import concourse.bass as bass
from concourse import mybir

P = 128
F32 = mybir.dt.float32
F32R = mybir.dt.float32r
BF16 = mybir.dt.bfloat16
I32 = mybir.dt.int32
I16 = mybir.dt.int16
ALU = mybir.AluOpType
ACT = mybir.ActivationFunctionType
AX = mybir.AxisListType

EPS = 1e-5
SLOPE = 0.2
FINITE = 3.0e38


def gnn_moe_kernel(nc, x, src, dst, gnn_W, gnn_b_w, gnn_a, gnn_b_a, Wg, bg, W1, b1, W2, b2, out):
    N, D = x.shape
    E = src.shape[0]
    KT = D // P
    NT = -(-N // P)
    LAST = N - (NT - 1) * P
    NTN = NT * P
    CH = -(-E // P)
    CJ = -(-CH // P)
    GC = 2
    RING = 10
    NG = -(-CH // (RING * GC)) * RING
    SR = 5
    BACK = 3
    HD = D // 2
    HALF = HD + 1
    ROW = 2 * HALF + 2
    ONE, S_SRC = HD, 2 * HALF - 1

    NX, F = W1.shape[0], W1.shape[2]
    HF = F // P
    ITEMS = 2 * NT
    TILES = (2 * N + NX * (P - 1)) // P
    YR = 4
    SKIP = 4 * NTN

    table = nc.dram_tensor("node_table", [NTN, ROW], F32).ap()
    xn_table = nc.dram_tensor("xn_table", [NTN, D], F32).ap()
    y_table = nc.dram_tensor("y_table", [2 * NTN, D], F32).ap()

    with ExitStack() as ctx:
        def sb(name, shape, dt):
            return ctx.enter_context(nc.sbuf_tensor(name, shape, dt))

        def sem(name):
            return ctx.enter_context(nc.semaphore(name))

        acc = sb("acc", [P, NT, 2, HALF], F32)
        rden = sb("rden", [P, NT], F32)
        x_in = sb("x_in", [P, 2, 2, D], F32)
        xn = sb("xn", [P, 2, 2, D], F32)
        ident = sb("ident", [P, P], F32)
        stats = sb("stats", [P, 2, 2, 6], F32)
        mv = sb("mv", [P, 2, 2, 2], F32)
        std = sb("std", [P, 2, 2], F32)
        rstd = sb("rstd", [P, 2, 2], F32)
        spare = sb("spare", [P, 3], F32)
        start = sb("start", [P, 5], F32)
        eps = sb("eps", [P, 1], F32)
        graph = ctx.enter_context(ExitStack())

        def sg(name, shape, dt):
            return graph.enter_context(nc.sbuf_tensor(name, shape, dt))

        rows = sg("rows", [P, RING, GC, ROW], F32)
        sdst_b = sg("sdst_b", [P, NTN], F32)
        node_id = sg("node_id", [P, NTN], I16)
        ba_b = sg("ba_b", [P, 1], F32)
        cst = sg("cst", [P, 1], F32)
        cst2 = sg("cst2", [P, 2], F32)
        srcT = sg("srcT", [P, NG * GC], I32)
        dstT = sg("dstT", [P, NG * GC], F32)
        idx = sg("idx", [P, RING, GC], I32)
        ch_mm = sg("ch_mm", [P, 2, CJ], F32)
        win_f = sg("win_f", [1, 2, NG], F32)
        win_i = sg("win_i", [1, 2, NG], I32)
        win_n = sg("win_n", [1, 3, NG], F32)
        zero_r = sg("zero_r", [1, NG], F32)
        win_w = sg("win_w", [1, 2, NG + BACK], F32)
        window = sg("window", [1, NG + BACK], I32)
        E1 = sg("E1", [P, 3, GC, P], F32)
        E2 = sg("E2", [P, 3, GC, P], F32)
        Wt = sg("Wt", [P, 3, GC, P], F32)
        S = sg("S", [P, SR + 1, GC, P], F32)

        xT = sg("xT", [P, 2, 2, KT, 2 * P], F32R)
        Wb = sg("Wb", [P, 2, KT, D], F32R)
        Wf = sg("Wf", [P, KT, D], F32)
        bw_b = sg("bw_b", [P, D], F32)
        a_b = sg("a_b", [P, 2, D], F32)
        junk = sg("junk", [P, 2, D], F32)
        s_dot = sg("s_dot", [P, 2, 2], F32)
        edge_i = sg("edge_i", [P, 2, CJ, P], I32)
        edge_f = sg("edge_f", [P, 2, CJ, P], F32)
        wa = sg("wa", [P, KT], F32)
        wa_hl = sg("wa_hl", [P, 2, KT], F32R)
        wa_rep = sg("wa_rep", [P, 2, KT, P], F32R)
        graph.close()

        expert_of = sb("expert_of", [1, TILES + 4], I32)
        src_row = sb("src_row", [P, TILES], I32)
        dst_row = sb("dst_row", [P, TILES], I32)
        prob = sb("prob", [P, 2, NT], F32)
        b1_b = sb("b1_b", [P, NX, F], F32)
        b2_b = sb("b2_b", [P, NX, D], F32)

        routing = ctx.enter_context(ExitStack())

        def sr(name, shape, dt):
            return routing.enter_context(nc.sbuf_tensor(name, shape, dt))

        xnT = sr("xnT", [P, 2, 2, KT * P], F32)
        Wg_sb = sr("Wg_sb", [P, KT, NX], F32)
        bg_b = sr("bg_b", [P, NX], F32)
        count_i = sr("count_i", [P, P], I32)
        count = sr("count", [P, P], F32)
        part_i = sr("part_i", [P, 1], I32)
        part1 = sr("part1", [P, 1], F32)
        beyond = sr("beyond", [P, TILES], I32)
        valid = sr("valid", [P, 2, NT], F32)
        below = sr("below", [P, P], F32)
        all_1 = sr("all_1", [P, P], F32)
        score = sr("score", [P, NT, NX], F32)
        pr = sr("pr", [P, NT, NX], F32)
        pick = sr("pick", [P, NT, NX], F32)
        red = sr("red", [P, NT], F32)
        choice = sr("choice", [P, NX, 2, NT], F32)
        rank = sr("rank", [P, NX, ITEMS], F32)
        zeros = sr("zeros", [P, NX * ITEMS], F32)
        per = sr("per", [P, 8, NX], F32)
        per_i = sr("per_i", [P, NX], I32)
        pos = sr("pos", [P, ITEMS], F32)
        pos_i = sr("pos_i", [P, 3, ITEMS], I32)
        pos_f = sr("pos_f", [P, 2, ITEMS], F32)
        hot_r = sr("hot_r", [P, ITEMS, P], BF16)
        hot_t = sr("hot_t", [P, ITEMS, TILES], F32)
        hot_v = sr("hot_v", [P, 2, ITEMS, TILES], BF16)
        inv = sr("inv", [P, 3, TILES], F32)
        ends = sr("ends", [1, TILES, NX], F32)
        end_n = sr("end_n", [1, TILES], F32)
        routing.close()

        xg = sb("xg", [P, YR, D], F32)
        gi = sb("gi", [P, YR, 1], I32)
        si = sb("si", [P, YR, 1], I32)
        xgT = sb("xgT", [P, 2, KT * P], F32)
        hid = sb("hid", [P, 2, F], F32)
        act_h = sb("act_h", [P, 2, F], F32)
        hidT = sb("hidT", [P, 2, HF * P], F32)
        y = sb("y", [P, YR, D], F32)
        ya = sb("ya", [P, YR, D], F32)
        yb = sb("yb", [P, YR, D], F32)
        late = YR * (4 * D + 2) + 2 * KT * P + 4 * F + 2 * HF * P + NX * (F + D) + 2 * NT + 3 * TILES + 4
        early = RING * GC * (ROW + 1) + NTN + NTN // 2 + 2 * NG * GC + 11 * NG + (9 + SR + 1) * GC * P
        gap = sb("gap", [P, max(1, early - late + 128)], F32)
        W1_e = sb("W1_e", [P, NX, KT, F], F32)
        W2_e = sb("W2_e", [P, NX, HF, D], F32)

        pair = [ctx.enter_context(nc.psum_tensor(f"ps{i}", [P, 2, 512], F32)) for i in range(4)]
        ps = [pair[i // 2][:, i % 2, :] for i in range(8)]
        psT = [[ps[2 * s], ps[2 * s + 1]] for s in range(2)]
        ps_h, ps_edge, ps_d = [ps[4], ps[5]], ps[6], ps[7]
        ps_agg = pair[0:3]
        ps_logit, ps_sum, ps_inv = ps[4], ps[5], ps[6]
        ps_x, ps_hT, ps_hid, ps_y = ps[0], ps[1], [ps[2], ps[3]], [ps[4], ps[5]]

        def halves(ap):
            return ap.rearrange("p (a d) -> p a d", a=2)

        def features(t):
            return acc[:, bass.ds(t, 1), :, 0:HD].rearrange("p t a d -> p (t a) d")

        ld_x = [[sem(f"ld_x{s}{j}") for j in range(2)] for s in range(2)]
        ld_W, ld_edge, ld_par = sem("ld_W"), sem("ld_edge"), sem("ld_par")
        pads, ident_ok, ids_ok, zeros_ok = sem("pads"), sem("ident_ok"), sem("ids_ok"), sem("zeros_ok")
        dv = sem("dv_setup")
        W_hi, W_ok, wa_ok, edges_f, edges_ps, edges_ok = (sem(n) for n in (
            "W_hi", "W_ok", "wa_ok", "edges_f", "edges_ps", "edges_ok"))
        mm_ps, win_ok, mm_ok = sem("mm_ps"), sem("win_ok"), sem("mm_ok")
        stats_ok, std_ok, rstd_ok, xn_ok = (sem(n) for n in ("stats_ok", "std_ok", "rstd_ok", "xn_ok"))
        xT_ps, xT_hi, xT_lo = sem("xT_ps"), sem("xT_hi"), sem("xT_lo")
        h_ps, row_ok, d_ps, d_ok = (sem(n) for n in ("h_ps", "row_ok", "d_ps", "d_ok"))
        dot_ok, s_ok = sem("dot_ok"), sem("s_ok")
        st_row = [[sem(f"st_row{s}{j}") for j in range(2)] for s in range(2)]
        idx_ok = sem("idx_ok")
        got = [sem(f"got{r}") for r in range(RING)]
        exp_ok = sem("exp_ok")
        max_ok = [sem("max_ok0"), sem("max_ok1")]
        S_ok, agg_ok = sem("S_ok"), sem("agg_ok")
        xexp_ok, xmax_ok, xS_ok, xagg_ok = (sem(n) for n in ("xexp_ok", "xmax_ok", "xS_ok", "xagg_ok"))
        acc_ok, added, xadded = sem("acc_ok"), sem("added"), sem("xadded")
        ld_x2 = [[sem(f"ld_x2_{s}{j}") for j in range(2)] for s in range(2)]
        st_xn = [[sem(f"st_xn_{s}{j}") for j in range(2)] for s in range(2)]
        ld_late, ld_W1, ld_W2 = sem("ld_late"), sem("ld_W1"), sem("ld_W2")
        x1_ok, stats2_ok, aggr2_ok, std2_ok, rstd2_ok, xn2_ok = (sem(n) for n in (
            "x1_ok", "stats2_ok", "aggr2_ok", "std2_ok", "rstd2_ok", "xn2_ok"))
        xnT_ps, xnT_ok, logit_ps = sem("xnT_ps"), sem("xnT_ok"), sem("logit_ps")
        shift_ok, exp2_ok, cnt_ok, cnt_ps = sem("shift_ok"), sem("exp2_ok"), sem("cnt_ok"), sem("cnt_ps")
        hot_ok, inv_ps, routed = sem("hot_ok"), sem("inv_ps"), sem("routed")
        consts_ok = sem("consts_ok")
        gi_ok, si_ok = sem("gi_ok"), sem("si_ok")
        got_x = [sem(f"got_x{r}") for r in range(YR)]
        put_y = [sem(f"put_y{r}") for r in range(YR)]
        x_ps, xgT_ok, hid_ps, hid_ok, gelu_ok, hidT_ps, hidT_ok, y_ps, y_ok = (sem(n) for n in (
            "x_ps", "xgT_ok", "hid_ps", "hid_ok", "gelu_ok", "hidT_ps", "hidT_ok", "y_ps", "y_ok"))
        ld_ya = [sem(f"ld_ya{r}") for r in range(YR)]
        ld_yb = [sem(f"ld_yb{r}") for r in range(YR)]
        fin_a, fin_b, st_out = sem("fin_a"), sem("fin_b"), sem("st_out")

        def experts(eng, regs, i):
            eng.load(regs, expert_of[0:1, bass.ds(i, len(regs))])

        def expert_in(eng, reg):
            return nc.s_assert_within(eng.snap(reg), 0, NX - 1,
                                      skip_runtime_bounds_check_because="the table's words are built so")

        def over_tiles(eng, regs, step):
            def some(i, n, at):
                experts(eng, regs[0:n + 2], i)
                for k in range(n):
                    step(at + k, i + k, regs[k + 2] if at + k < TILES else None, regs[k] if at + k >= 2 else None)
            some(0, 4, 0)
            some(4, 4, 4)
            body = TILES // 4
            with eng.Fori(2, body) as b:
                some(4 * b, 4, 4)
            for i in range(4 * body, TILES + 2):
                some(i, 1, i)


        def window_words(eng, regs, i, back=0):
            eng.load(regs, window[0:1, bass.ds(RING * i + BACK - back, len(regs))])

        def field(word, shift, mask, most):
            return nc.s_assert_within((word >> shift) & mask if shift else word & mask, 0, most,
                                      skip_runtime_bounds_check_because="the table's words are built so")

        def tile_in(word):
            return field(word, 0, 31, NT - 1)

        def extra_in(word):
            return field(word, 5, 31, NT - 1)

        def before_in(word):
            return field(word, 10, 4095, NG * NT)

        def tile_of(value):
            return nc.s_assert_within(value, 0, NT - 1, skip_runtime_bounds_check_because="a tile of the window")

        block = ctx.enter_context(nc.Block())

        @block.sync
        def _(sp):
            def load_x(u, s, j):
                if u is not None:
                    tile = x[0:(NT - 1) * P, :].rearrange("(t p) d -> t p d", p=P)[bass.ds(2 * u + j, 1)]
                    sp.dma_start(x_in[:, s, j, :], tile.rearrange("t p d -> (t p) d")).then_inc(ld_x[s][j], 16)
                else:
                    sp.dma_start(x_in[0:LAST, s, j, :], x[(NT - 1) * P:N, :]).then_inc(ld_x[s][j], 16)

            def store_rows(u, s, i):
                sp.wait_ge(s_ok, u + 1)
                for j in range(2):
                    sp.wait_ge(row_ok, 2 * u + j + 1)
                    sp.dma_start(table[bass.ds((2 * u + j) * P, P), :], rows[:, s, j, :])\
                        .then_inc(st_row[s][j], 16)

            load_x(0, 0, 0)
            load_x(0, 0, 1)
            sp.dma_start(Wf[:, :, :], gnn_W.rearrange("(k p) n -> p k n", p=P)).then_inc(ld_W, 16)
            load_x(1, 1, 0)
            load_x(1, 1, 1)
            full = (CH - 1) * P if E % P else E
            sp.wait_ge(pads, 1)
            for k, e in enumerate((src, dst)):
                jf = full // (P * P)
                sp.dma_start(edge_i[:, k, 0:jf, :], e[0:jf * P * P].rearrange("(j q i) -> q j i", q=P, i=P))\
                    .then_inc(ld_edge, 16)
                q = (full - jf * P * P) // P
                sp.dma_start(edge_i[0:q, k, jf, :], e[jf * P * P:full].rearrange("(q i) -> q i", i=P))\
                    .then_inc(ld_edge, 16)
                sp.dma_start(edge_i[q:q + 1, k, jf, 0:E - full], e[full:E].rearrange("(q i) -> q i", q=1))\
                    .then_inc(ld_edge, 16)
            sp.dma_start(bw_b[:, :], gnn_b_w.partition_broadcast(P)).then_inc(ld_par, 16)
            sp.dma_start(a_b[:, :, :].rearrange("p a d -> p (a d)"), gnn_a.partition_broadcast(P)).then_inc(ld_par, 16)
            sp.dma_start(ba_b[:, :], gnn_b_a.partition_broadcast(P)).then_inc(ld_par, 16)

            def step(u, s, i, ahead):
                if ahead:
                    for j in range(2):
                        sp.wait_ge(xn_ok, 2 * u + j + 1)
                        load_x(*((u + 2, s, j) if ahead == 1 or j == 0 else (None, s, j)))
                store_rows(u, s, i)

            with sp.Fori(0, 3) as i:
                for s in range(2):
                    step(2 * i + s, s, i, 1)
            step(6, 0, 3, 1)
            step(7, 1, 3, 2)
            step(8, 0, 4, 0)
            step(9, 1, 4, 0)

            sp.wait_ge(d_ok, NT // 2)
            sp.wait_ge(wa_ok, 1)
            sp.wait_ge(win_ok, 2)
            sp.wait_ge(row_ok, NT)
            sp.wait_ge(s_ok, NT // 2)
            with sp.Fori(0, NX) as e:
                sp.wait_ge(agg_ok, NG // (NX + 1) * e + 1)
                sp.dma_start(W1_e[:, bass.ds(e, 1), :, :].rearrange("p e k f -> p (e k) f"),
                             W1.rearrange("e (k p) f -> p e k f", p=P)[:, bass.ds(e, 1)]
                             .rearrange("p e k f -> p (e k) f")).then_inc(ld_W1, 16)
                sp.dma_start(W2_e[:, bass.ds(e, 1), :, :].rearrange("p e k d -> p (e k) d"),
                             W2.rearrange("e (k p) d -> p e k d", p=P)[:, bass.ds(e, 1)]
                             .rearrange("p e k d -> p (e k) d")).then_inc(ld_W2, 16)

            def load_x2(u, s, j, last=False):
                if last:
                    sp.dma_start(x_in[0:LAST, s, j, :], x[(NT - 1) * P:N, :]).then_inc(ld_x2[s][j], 16)
                else:
                    tile = x[0:(NT - 1) * P, :].rearrange("(t p) d -> t p d", p=P)[bass.ds(2 * u + j, 1)]
                    sp.dma_start(x_in[:, s, j, :], tile.rearrange("t p d -> (t p) d")).then_inc(ld_x2[s][j], 16)

            def store_xn(u, s):
                for j in range(2):
                    sp.wait_ge(xn2_ok, 2 * u + j + 1)
                    sp.dma_start(xn_table[bass.ds((2 * u + j) * P, P), :], xn[:, s, j, :]).then_inc(st_xn[s][j], 16)

            def x_step(u, s, last=False):
                for j in range(2):
                    sp.wait_ge(x1_ok, 2 * u + j + 1)
                    load_x2(u + 2, s, j, last and j == 1)
                store_xn(u, s)

            for u in range(2):
                for j in range(2):
                    load_x2(u, u, j)
            sp.wait_ge(acc_ok, 1)
            sp.dma_start(Wg_sb[:, :, :], Wg.rearrange("(k p) e -> p k e", p=P)).then_inc(ld_late, 16)
            sp.dma_start(bg_b[:, :], bg.partition_broadcast(P)).then_inc(ld_late, 16)
            sp.dma_start(b1_b[:, :, :].rearrange("p e f -> p (e f)"),
                         b1.rearrange("e f -> (e f)").partition_broadcast(P)).then_inc(ld_late, 16)
            sp.dma_start(b2_b[:, :, :].rearrange("p e d -> p (e d)"),
                         b2.rearrange("e d -> (e d)").partition_broadcast(P)).then_inc(ld_late, 16)
            with sp.Fori(0, 3) as i:
                for s in range(2):
                    x_step(2 * i + s, s)
            x_step(NT // 2 - 4, 0)
            x_step(NT // 2 - 3, 1, last=True)
            store_xn(NT // 2 - 2, 0)
            store_xn(NT // 2 - 1, 1)

            for r in range(YR):
                sp.wait_ge(put_y[r], 16 * ((TILES - r + YR - 1) // YR))

            def load_y(t, r, i, rows_):
                sp.wait_ge(fin_a, t + 1 - YR) if not (isinstance(t, int) and t < YR) else None
                for slot, (into, ld) in enumerate(((ya, ld_ya[r]), (yb, ld_yb[r]))):
                    if slot and not (isinstance(t, int) and t < YR):
                        sp.wait_ge(fin_b, t + 1 - YR)
                    sp.dma_start(into[0:rows_, r, :], y_table[bass.ds(slot * NTN + t * P, rows_), :]).then_inc(ld, 16)

            for r in range(YR):
                load_y(r, r, 0, P)
            with sp.Fori(1, NT // YR - 1) as i:
                for r in range(YR):
                    load_y(YR * i + r, r, i, P)
            for r in range(YR):
                load_y(NT - YR + r, r, NT // YR - 1, P if r < YR - 1 else LAST)

        @block.gpsimd
        def _(pool):
            nc.gpsimd.memset(edge_i[:, 0, :, :], 0)
            nc.gpsimd.memset(edge_i[:, 1, :, :], 4095).then_inc(pads, 1)
            nc.gpsimd.memset(ident[:, :], 0.0).then_inc(zeros_ok, 1)
            pool.wait_ge(zeros_ok, 1)
            nc.gpsimd.affine_select(out=ident[:, :], in_=ident[:, :], compare_op=ALU.not_equal, fill=1.0, base=0,
                                    pattern=[[-1, P]], channel_multiplier=1).then_inc(ident_ok, 1)
            nc.gpsimd.memset(rows[:, 0:2, :, ONE:ONE + 1], 1.0)
            nc.gpsimd.memset(rows[:, 0:2, :, ROW - 1:ROW], 0.0).then_inc(pads, 1)
            nc.gpsimd.iota(node_id[:, :], pattern=[[1, NTN]], base=0, channel_multiplier=0)
            nc.gpsimd.memset(acc[:, :, :, :], 0.0).then_inc(ids_ok, 1)

            def copy_idx(g, r):
                nc.gpsimd.tensor_copy(idx[:, r, :], srcT[:, bass.ds(GC * g, GC)]).then_inc(idx_ok, 1)

            def gather(g, r, last=False):
                pool.wait_ge(idx_ok, g + 1)
                if not (isinstance(g, int) and g < RING):
                    pool.wait_ge(agg_ok, g - RING + 2)
                if not last:
                    copy_idx(g + 1, (r + 1) % RING)
                for c in range(GC):
                    nc.gpsimd.indirect_dma_start(
                        out=rows[:, r, c, :], out_offset=None, in_=table,
                        in_offset=bass.IndirectOffsetOnAxis(ap=idx[:, r, c:c + 1], axis=0)).then_inc(got[r], 16)

            pool.wait_ge(edges_ok, 2)
            for s in range(2):
                for j in range(2):
                    pool.wait_ge(st_row[s][j], 16 * NT // 4)
            copy_idx(0, 0)
            for r in range(RING):
                if r == RING - 1:
                    pool.wait_ge(agg_ok, 1)
                gather(r, r)
            with pool.Fori(1, NG // RING - 1) as i:
                for r in range(RING):
                    gather(RING * i + r, r)
            for r in range(RING):
                gather(NG - RING + r, r, last=r == RING - 1)

            pool.wait_ge(acc_ok, 1)
            nc.gpsimd.iota(count_i[:, :], pattern=[[1, P]], base=0, channel_multiplier=0)
            nc.gpsimd.iota(part_i[:, :], pattern=[[0, 1]], base=1, channel_multiplier=1)
            nc.gpsimd.iota(beyond[:, :], pattern=[[P, TILES]], base=SKIP, channel_multiplier=1)
            nc.gpsimd.memset(all_1[:, :], 1.0)
            nc.gpsimd.memset(zeros[:, :], 0.0)
            nc.gpsimd.memset(below[:, :], 1.0)
            nc.gpsimd.memset(expert_of[:, :], 0)
            nc.gpsimd.memset(valid[:, :, :], 1.0).then_inc(consts_ok, 1)
            pool.wait_ge(consts_ok, 1)
            nc.gpsimd.affine_select(out=below[:, :], in_=below[:, :], compare_op=ALU.is_gt, fill=0.0, base=0,
                                    pattern=[[1, P]], channel_multiplier=-1)
            nc.gpsimd.affine_select(out=valid[:, :, :], in_=valid[:, :, :], compare_op=ALU.is_ge, fill=0.0,
                                    base=N - 1, pattern=[[0, 2], [-P, NT]], channel_multiplier=-1)\
                .then_inc(consts_ok, 1)

            def copy_gi(i, r):
                nc.gpsimd.tensor_copy(gi[:, r, :], src_row[:, bass.ds(i, 1)]).then_inc(gi_ok, 1)

            def copy_si(i, r):
                nc.gpsimd.tensor_copy(si[:, r, :], dst_row[:, bass.ds(i, 1)]).then_inc(si_ok, 1)

            def row_step(i, r, b):
                peeled = isinstance(i, int)
                if not (peeled and i >= TILES):
                    pool.wait_ge(gi_ok, i + 1)
                if not (peeled and i < YR):
                    pool.wait_ge(si_ok, i - YR + 1)
                    pool.wait_ge(y_ok, i - YR + 1)
                if not (peeled and i + 1 >= TILES):
                    if not (peeled and i + 1 < YR):
                        pool.wait_ge(x_ps, i + 2 - YR)
                    copy_gi(i + 1, (r + 1) % YR)
                if not (peeled and (i + 1 < YR or i + 1 >= TILES + YR)):
                    if not (peeled and i + 1 < 2 * YR):
                        n = (i + 1) // YR - 1 if peeled else b + (r + 1) // YR - 1
                        pool.wait_ge(put_y[(r + 1) % YR], 16 * n)
                    copy_si(i + 1 - YR, (r + 1) % YR)
                if not (peeled and i >= TILES):
                    nc.gpsimd.indirect_dma_start(
                        out=xg[:, r, :], out_offset=None, in_=xn_table,
                        in_offset=bass.IndirectOffsetOnAxis(ap=gi[:, r, :], axis=0)).then_inc(got_x[r], 16)
                if not (peeled and i < YR):
                    nc.gpsimd.indirect_dma_start(
                        out=y_table, out_offset=bass.IndirectOffsetOnAxis(ap=si[:, r, :], axis=0),
                        in_=y[:, r, :], in_offset=None, bounds_check=2 * NTN - 1, oob_is_err=False)\
                        .then_inc(put_y[r], 16)

            pool.wait_ge(routed, 1)
            for s in range(2):
                for j in range(2):
                    pool.wait_ge(st_xn[s][j], 16 * NT // 4)
            copy_gi(0, 0)
            first, body = 2 * YR, (TILES - 1 - 2 * YR) // YR
            for i in range(first):
                row_step(i, i % YR, i // YR)
            with pool.Fori(2, 2 + body) as b:
                for r in range(YR):
                    row_step(YR * b + r, r, b)
            for i in range(first + YR * body, TILES + YR):
                row_step(i, i % YR, i // YR)

        @block.tensor
        def _(pe):
            regs = [pe.alloc_register(f"pe_window{k}") for k in range(RING)]
            pe.wait_ge(ident_ok, 1)

            def edge_columns(k):
                for j in range(CJ):
                    m = pe.transpose(ps_edge[:, j * P:(j + 1) * P], edge_f[:, k, j, :], ident[:, :])
                m.then_inc(edges_ps, 1)

            def transposes(u, s):
                for j in range(2):
                    pe.wait_ge(xn_ok, 2 * u + j + 1)
                    for k in range(KT):
                        m = pe.transpose(psT[s][k // 2][:, (k % 2) * 2 * P + j * P:(k % 2) * 2 * P + (j + 1) * P],
                                         xn[:, s, j, k * P:(k + 1) * P], ident[:, :])
                m.then_inc(xT_ps, 1)

            def products(u, s, first):
                pe.wait_ge(xT_lo, u + 1)
                three = [(0, 0), (1, 0), (0, 1)]
                for j in range(2):
                    if not first:
                        pe.wait_ge(row_ok, 2 * u + j - 1)
                    n = 0
                    for k in range(KT):
                        for a, b in three:
                            m = pe.matmul(ps_h[j][:, :], xT[:, s, a, k, j * P:(j + 1) * P], Wb[:, b, k, :],
                                          start=(n == 0), stop=(n == 3 * KT - 1))
                            n += 1
                    m.then_inc(h_ps, 1)
                if first:
                    pe.wait_ge(wa_ok, 1)
                else:
                    pe.wait_ge(d_ok, u)
                n = 0
                for k in range(KT):
                    for a, b in three:
                        m = pe.matmul(ps_d[:, 0:2 * P], wa_rep[:, b, k, :], xT[:, s, a, k, :],
                                      start=(n == 0), stop=(n == 3 * KT - 1))
                        n += 1
                m.then_inc(d_ps, 1)

            transposes(0, 0)
            transposes(1, 1)
            pe.wait_ge(W_ok, 1)
            products(0, 0, True)
            pe.wait_ge(edges_f, 1)
            edge_columns(0)
            transposes(2, 0)
            products(1, 1, False)
            pe.wait_ge(edges_ok, 1)
            edge_columns(1)
            with pe.Fori(1, NT // 4 - 1) as i:
                transposes(2 * i + 1, 1)
                products(2 * i, 0, False)
                transposes(2 * i + 2, 0)
                products(2 * i + 1, 1, False)
            transposes(NT // 2 - 1, 1)
            products(NT // 2 - 2, 0, False)
            pe.wait_ge(mm_ok, 1)
            for k in range(2):
                for j in range(CJ):
                    m = pe.transpose(psT[0][k][0:1, j * P:(j + 1) * P], ch_mm[:, k, j:j + 1], ident[:, :])
            m.then_inc(mm_ps, 1)
            products(NT // 2 - 1, 1, False)

            def sums(q, w, r):
                for c in range(GC):
                    for a in range(2):
                        m = pe.matmul(ps_agg[q][:, a, 0:HALF], S[:, w, c, :], rows[:, r, c, a * HALF:(a + 1) * HALF],
                                      start=(c == 0), stop=(c == GC - 1))
                return m

            def group(g, r, i):
                pe.wait_ge(S_ok, g + 1)
                if not (isinstance(g, int) and g < 2):
                    pe.wait_ge(added, g - 1)
                sums(r % 2, r % SR, r).then_inc(agg_ok, 1)
                word = pe.snap(regs[r])
                extra = pe.snap(extra_in(word))
                with pe.If(extra > 0):
                    before = pe.snap(before_in(word))
                    with pe.Fori(0, extra) as n:
                        pe.wait_ge(xS_ok, before + n + 2)
                        pe.wait_ge(xadded, before + n + 1)
                        sums(2, SR, r).then_inc(xagg_ok, 1)

            pe.wait_ge(row_ok, NT)
            pe.wait_ge(s_ok, NT // 2)
            pe.wait_ge(d_ok, NT // 2)
            pe.wait_ge(win_ok, 2)
            window_words(pe, regs, 0)
            for r in range(RING):
                group(r, r, 0)
            with pe.Fori(1, NG // RING) as i:
                window_words(pe, regs, i)
                for r in range(RING):
                    group(RING * i + r, r, i)

            def normal_T(u, s):
                for j in range(2):
                    pe.wait_ge(xn2_ok, 2 * u + j + 1)
                    if j == 0 and not (isinstance(u, int) and u < 2):
                        pe.wait_ge(xnT_ok, u - 1)
                    for k in range(KT):
                        m = pe.transpose(psT[s][j][:, k * P:(k + 1) * P], xn[:, s, j, k * P:(k + 1) * P], ident[:, :])
                m.then_inc(xnT_ps, 1)

            def logits(u, s):
                pe.wait_ge(xnT_ok, u + 1)
                for j in range(2):
                    for k in range(KT):
                        m = pe.matmul(ps_logit[:, bass.ds((2 * u + j) * NX, NX)], xnT[:, s, j, k * P:(k + 1) * P],
                                      Wg_sb[:, k, :], start=(k == 0), stop=(k == KT - 1))
                m.then_inc(logit_ps, 1)

            pe.wait_ge(acc_ok, 1)
            pe.wait_ge(ld_late, 16 * 4)
            normal_T(0, 0)

            def two_steps(i):
                normal_T(2 * i + 1, 1)
                logits(2 * i, 0)
                normal_T(2 * i + 2, 0)
                logits(2 * i + 1, 1)

            two_steps(0)
            with pe.Fori(1, NT // 4 - 1) as i:
                two_steps(i)
            normal_T(NT // 2 - 1, 1)
            logits(NT // 2 - 2, 0)
            logits(NT // 2 - 1, 1)
            pe.wait_ge(cnt_ok, 1)
            pe.wait_ge(consts_ok, 2)
            pe.matmul(ps_sum[:, 0:NX], below[:, :], per[:, 0, :], start=True, stop=True)
            pe.matmul(ps_sum[:, NX:2 * NX], all_1[:, :], per[:, 0, :], start=True, stop=True).then_inc(cnt_ps, 1)
            pe.wait_ge(hot_ok, 1)
            for v in range(2):
                for t in range(ITEMS):
                    m = pe.matmul(ps_inv[:, v * TILES:(v + 1) * TILES], hot_r[:, t, :], hot_v[:, v, t, :],
                                  start=(t == 0), stop=(t == ITEMS - 1))
            m.then_inc(inv_ps, 1)

            def tile_step(i, n, e_new, e_old):
                s, r, peeled = i % 2, i % YR, isinstance(n, int)
                if e_old is not None:
                    pe.wait_ge(gelu_ok, n - 1)
                    if not (peeled and n < 3):
                        pe.wait_ge(hidT_ok, n - 2)
                    for k in range(HF):
                        m = pe.transpose(ps_hT[:, k * P:(k + 1) * P], act_h[:, s, k * P:(k + 1) * P], ident[:, :])
                    m.then_inc(hidT_ps, 1)
                if e_new is not None:
                    pe.wait_ge(got_x[r], tile_count(n, i))
                    if not (peeled and n < 1):
                        pe.wait_ge(xgT_ok, n)
                    for k in range(KT):
                        m = pe.transpose(ps_x[:, k * P:(k + 1) * P], xg[:, r, k * P:(k + 1) * P], ident[:, :])
                    m.then_inc(x_ps, 1)
                if e_old is not None:
                    e = expert_in(pe, e_old)
                    pe.wait_ge(hidT_ok, n - 1)
                    if not (peeled and n < 4):
                        pe.wait_ge(y_ok, n - 3)
                    for k in range(HF):
                        m = pe.matmul(ps_y[s][:, :], hidT[:, s, k * P:(k + 1) * P],
                                      W2_e[:, bass.ds(e, 1), k, :].rearrange("p e d -> p (e d)"),
                                      start=(k == 0), stop=(k == HF - 1))
                    m.then_inc(y_ps, 1)
                if e_new is not None:
                    e = expert_in(pe, e_new)
                    pe.wait_ge(xgT_ok, n + 1)
                    if not (peeled and n < 2):
                        pe.wait_ge(hid_ok, n - 1)
                    for k in range(KT):
                        m = pe.matmul(ps_hid[s][:, 0:F], xgT[:, s, k * P:(k + 1) * P],
                                      W1_e[:, bass.ds(e, 1), k, :].rearrange("p e f -> p (e f)"),
                                      start=(k == 0), stop=(k == KT - 1))
                    m.then_inc(hid_ps, 1)

            def tile_count(n, i):
                return 16 * (n // YR + 1) if isinstance(n, int) else 4 * (n - i % YR) + 16

            pe.wait_ge(routed, 1)
            pe.wait_ge(ld_W1, 16 * NX)
            pe.wait_ge(ld_W2, 16 * NX)
            pe_experts = [pe.alloc_register(f"pe_expert{k}") for k in range(6)]
            over_tiles(pe, pe_experts, tile_step)

        @block.scalar
        def _(act):
            regs = [act.alloc_register(f"act_window{k}") for k in range(RING + 1)]
            def std_of(u, s):
                act.wait_ge(stats_ok, u + 1)
                nc.scalar.activation(std[:, s, :], mv[:, s, :, 1], ACT.Sqrt, bias=eps[:, :]).then_inc(std_ok, 1)

            def high_xT(u, s):
                act.wait_ge(xT_ps, u + 1)
                if not (isinstance(u, int) and u < 2):
                    act.wait_ge(d_ps, u - 1)
                for b in range(2):
                    m = nc.scalar.activation(xT[:, s, 0, 2 * b:2 * b + 2, :].rearrange("p k n -> p (k n)"),
                                             psT[s][b][:, :], ACT.Copy)
                m.then_inc(xT_hi, 1)

            def s_dst(u):
                act.wait_ge(d_ps, u + 1)
                nc.scalar.activation(sdst_b[:, bass.ds(2 * P * u, 2 * P)], ps_d[:, 0:2 * P], ACT.Copy).then_inc(d_ok, 1)

            std_of(0, 0)
            act.wait_ge(ld_W, 16)
            nc.scalar.activation(Wb[:, 0, :, :], Wf[:, :, :], ACT.Copy).then_inc(W_hi, 1)
            high_xT(0, 0)
            std_of(1, 1)

            def step(u, s, i, ahead):
                if ahead:
                    high_xT(u + 1, 1 - s)
                    if ahead > 1:
                        std_of(u + 2, s)
                s_dst(u)

            step(0, 0, 0, 2)
            with act.Fori(0, NT // 4 - 2) as i:
                step(2 * i + 1, 1, i, 2)
                step(2 * i + 2, 0, i + 1, 2)
            step(NT // 2 - 3, 1, NT // 4 - 2, 2)
            step(NT // 2 - 2, 0, NT // 4 - 1, 1)
            step(NT // 2 - 1, 1, NT // 4 - 1, 0)

            def weights(q, r, tile):
                for k, (e, scale) in enumerate(((E1, 1.0), (E2, SLOPE))):
                    for c in range(GC):
                        bias = rows[:, r, c, S_SRC + k:S_SRC + k + 1]
                        m = nc.scalar.activation(e[:, q, c, :], sdst_b[:, bass.ds(tile * P, P)], ACT.Exp,
                                                 bias=bias, scale=scale)
                return m

            def extras(r):
                word = act.snap(regs[r])
                extra = act.snap(extra_in(word))
                with act.If(extra > 0):
                    tile, before = act.snap(tile_in(word)), act.snap(before_in(word))
                    with act.Fori(0, extra) as n:
                        act.wait_ge(xmax_ok, before + n + 1)
                        weights(2, (r - 1) % RING, tile_of(tile + n + 1)).then_inc(xexp_ok, 1)

            def group(r, i):
                tile = act.snap(tile_in(act.snap(regs[r + 1])))
                act.wait_ge(max_ok[r % 2], RING // 2 * i + r // 2 + 1)
                act.wait_ge(got[r], 16 * GC * (i + 1))
                weights(r % 2, r, tile).then_inc(exp_ok, 1)
                extras(r)

            act.wait_ge(d_ok, NT // 2)
            act.wait_ge(win_ok, 2)
            act.wait_ge(wa_ok, 1)
            nc.scalar.activation(spare[:, 2:3], cst2[:, 0:1], ACT.Exp)
            with act.Fori(0, NG // RING) as i:
                window_words(act, regs, i, 1)
                for r in range(RING):
                    group(r, i)
            extras(RING)

            def std2_of(u, s):
                act.wait_ge(aggr2_ok, u + 1)
                nc.scalar.activation(std[:, s, :], mv[:, s, :, 1], ACT.Sqrt, bias=eps[:, :]).then_inc(std2_ok, 1)

            def xnT_of(u, s):
                act.wait_ge(xnT_ps, u + 1)
                if not (isinstance(u, int) and u < 2):
                    act.wait_ge(logit_ps, u - 1)
                for j in range(2):
                    m = nc.scalar.activation(xnT[:, s, j, :], psT[s][j][:, :], ACT.Copy)
                m.then_inc(xnT_ok, 1)

            act.wait_ge(acc_ok, 1)
            std2_of(0, 0)

            def two_steps(i):
                std2_of(2 * i + 1, 1)
                xnT_of(2 * i, 0)
                std2_of(2 * i + 2, 0)
                xnT_of(2 * i + 1, 1)

            two_steps(0)
            with act.Fori(1, NT // 4 - 1) as i:
                two_steps(i)
            std2_of(NT // 2 - 1, 1)
            xnT_of(NT // 2 - 2, 0)
            xnT_of(NT // 2 - 1, 1)
            act.wait_ge(shift_ok, 1)
            nc.scalar.activation(pr[:, :, :], score[:, :, :], ACT.Exp).then_inc(exp2_ok, 1)

            def tile_step(i, n, e_new, e_old):
                s = i % 2
                if e_new is not None:
                    act.wait_ge(x_ps, n + 1)
                    if not (isinstance(n, int) and n < 2):
                        act.wait_ge(hid_ps, n - 1)
                    nc.scalar.activation(xgT[:, s, :], ps_x[:, :], ACT.Copy).then_inc(xgT_ok, 1)
                    act.wait_ge(hid_ok, n + 1)
                    if not (isinstance(n, int) and n < 2):
                        act.wait_ge(hidT_ps, n - 1)
                    nc.scalar.activation(act_h[:, s, :], hid[:, s, :], ACT.Gelu_apprx_tanh).then_inc(gelu_ok, 1)

            act.wait_ge(routed, 1)
            for i in range(4):
                tile_step(i, i, True, i >= 2)
            with act.Fori(1, TILES // 4) as b:
                for k in range(4):
                    tile_step(k, 4 * b + k, True, True)
            for i in range(TILES // 4 * 4, TILES):
                tile_step(i, i, True, True)

            def store_out(t, rows_):
                act.wait_ge(fin_b, t + 1)
                act.dma_start(out[bass.ds(t * P, rows_), :].rearrange("p (a d) -> p a d", a=2),
                              features(t)[0:rows_]).then_inc(st_out, 16)

            with act.Fori(0, NT - 1) as t:
                store_out(t, P)
            store_out(NT - 1, LAST)
            act.wait_ge(st_out, 16 * NT)

        @block.vector
        def _(dve):
            regs = [dve.alloc_register(f"dve_window{k}") for k in range(RING + BACK)]
            n_dv = [0]

            def link(ins):
                n_dv[0] += 1
                ins.then_inc(dv, 1)
                dve.wait_ge(dv, n_dv[0])

            nc.vector.memset(zero_r[:, :], 0.0)
            for k, count_ in enumerate((max_ok[0], max_ok[1], xmax_ok, xS_ok, xadded)):
                nc.vector.memset(start[:, k:k + 1], 0.0).then_inc(count_, 1)
            link(nc.vector.memset(eps[:, :], EPS))

            def normal(u, s):
                for j in range(2):
                    dve.wait_ge(ld_x[s][j], 16 * (u // 2 + 1) if isinstance(u, int) else u * 8 + 16 - 8 * s)
                    nc.vector.bn_stats(stats[:, s, j, :], x_in[:, s, j, :]).then_inc(rstd_ok, 1)
                dve.wait_ge(rstd_ok, 3 * u + 2)
                nc.vector.memset(spare[:, s:s + 1], 0.0)
                for j in range(2):
                    m = nc.vector.bn_aggr(mv[:, s, j, :], stats[:, s, j, :])
                m.then_inc(stats_ok, 1)
                dve.wait_ge(std_ok, u + 1)
                nc.vector.reciprocal(rstd[:, s, :], std[:, s, :]).then_inc(rstd_ok, 1)
                dve.wait_ge(rstd_ok, 3 * u + 3)
                for j in range(2):
                    if not (isinstance(u, int) and u < 2):
                        dve.wait_ge(xT_ps, u - 1)
                    nc.vector.tensor_scalar(xn[:, s, j, :], x_in[:, s, j, :], mv[:, s, j, 0:1], rstd[:, s, j:j + 1],
                                            ALU.subtract, ALU.mult).then_inc(xn_ok, 1)

            def low_xT(u, s):
                dve.wait_ge(xT_hi, u + 1)
                for b in range(2):
                    m = nc.vector.tensor_tensor(xT[:, s, 1, 2 * b:2 * b + 2, :].rearrange("p k n -> p (k n)"),
                                                psT[s][b][:, :],
                                                xT[:, s, 0, 2 * b:2 * b + 2, :].rearrange("p k n -> p (k n)").bitcast(F32),
                                                ALU.subtract)
                m.then_inc(xT_lo, 1)

            def node_rows(u, s, i):
                for j in range(2):
                    dve.wait_ge(h_ps, 2 * u + j + 1)
                    if not (isinstance(u, int) and u < 2):
                        dve.wait_ge(st_row[s][j], 16 * i)
                    nc.vector.tensor_tensor(halves(rows[:, s, j, 0:2 * HALF])[:, :, 0:HD], halves(ps_h[j]),
                                            halves(bw_b[:, :]), ALU.add).then_inc(row_ok, 1)
                for j in range(2):
                    dve.wait_ge(row_ok, 2 * u + j + 1)
                    m = nc.vector.tensor_tensor_reduce(halves(junk[:, j, :]), halves(rows[:, s, j, 0:2 * HALF])[:, :, 0:HD],
                                                       halves(a_b[:, 1, :]), 1.0, 0.0, ALU.mult, ALU.add,
                                                       s_dot[:, s, j:j + 1])
                m.then_inc(dot_ok, 1)
                dve.wait_ge(dot_ok, u + 1)
                for k, scale in enumerate((1.0, SLOPE)):
                    m = nc.vector.tensor_scalar(rows[:, s, :, S_SRC + k:S_SRC + k + 1],
                                                s_dot[:, s, :].unsqueeze(2), scale, cst2[:, k:k + 1], ALU.mult, ALU.add)
                m.then_inc(s_ok, 1)

            normal(0, 0)
            normal(1, 1)
            dve.wait_ge(W_hi, 1)
            nc.vector.tensor_tensor(Wb[:, 1, :, :], Wf[:, :, :], Wb[:, 0, :, :].bitcast(F32), ALU.subtract).then_inc(W_ok, 1)
            low_xT(0, 0)
            dve.wait_ge(ld_par, 48)
            for k in range(KT):
                link(nc.vector.tensor_tensor_reduce(junk[:, 0, :], Wf[:, k, :], a_b[:, 0, :], 1.0, 0.0, ALU.mult,
                                                    ALU.add, wa[:, k:k + 1]))
            link(nc.vector.tensor_copy(wa_hl[:, 0, :], wa[:, :]))
            link(nc.vector.tensor_tensor(wa_hl[:, 1, :], wa[:, :], wa_hl[:, 0, :].bitcast(F32), ALU.subtract))
            for a in range(2):
                m = nc.vector.tensor_copy(wa_rep[:, a, :, :],
                                          wa_hl[:, a, :].bitcast(F32).unsqueeze(2).to_broadcast([P, KT, P]))
            m.then_inc(wa_ok, 1)
            link(nc.vector.tensor_tensor_reduce(junk[:, 0, :], bw_b[:, :], a_b[:, 0, :], 1.0, 0.0, ALU.mult,
                                                ALU.add, cst[:, :]))
            link(nc.vector.tensor_tensor(cst2[:, 0:1], cst[:, :], ba_b[:, :], ALU.add))
            link(nc.vector.tensor_scalar(cst2[:, 1:2], cst2[:, 0:1], SLOPE, None, ALU.mult))
            dve.wait_ge(ld_edge, 16 * 6)
            nc.vector.tensor_copy(edge_f[:, :, :, :], edge_i[:, :, :, :]).then_inc(edges_f, 1)
            dve.wait_ge(pads, 2)

            def step(u, s, i, ahead):
                if ahead:
                    low_xT(u + 1, 1 - s)
                    if ahead > 1:
                        normal(u + 2, s)
                node_rows(u, s, i)

            step(0, 0, 0, 2)
            dve.wait_ge(edges_f, 1)
            nc.vector.tensor_reduce(ch_mm[:, 0, :], edge_f[:, 1, :, :], AX.X, ALU.min)
            nc.vector.tensor_reduce(ch_mm[:, 1, :], edge_f[:, 1, :, :], AX.X, ALU.max).then_inc(mm_ok, 1)
            dve.wait_ge(edges_ps, 1)
            nc.vector.tensor_copy(srcT[:, :], ps_edge[:, 0:NG * GC]).then_inc(edges_ok, 1)
            step(1, 1, 0, 2)
            dve.wait_ge(edges_ps, 2)
            nc.vector.tensor_copy(dstT[:, :], ps_edge[:, 0:NG * GC]).then_inc(edges_ok, 1)
            step(2, 0, 1, 2)
            with dve.Fori(1, NT // 4 - 2) as i:
                step(2 * i + 1, 1, i, 2)
                step(2 * i + 2, 0, i + 1, 2)
            step(NT // 2 - 3, 1, NT // 4 - 2, 2)
            step(NT // 2 - 2, 0, NT // 4 - 1, 1)
            dve.wait_ge(mm_ps, 1)
            for k in range(2):
                link(nc.vector.tensor_reduce(win_f[:, k, :],
                                             psT[0][k][0:1, 0:NG * GC].rearrange("o (g c) -> o g c", c=GC),
                                             AX.X, (ALU.min, ALU.max)[k]))
            link(nc.vector.tensor_scalar(win_i[:, :, :], win_f[:, :, :], float(N - 1), None, ALU.min))
            link(nc.vector.tensor_single_scalar(win_i[:, :, :], win_i[:, :, :], 7, ALU.arith_shift_right))
            link(nc.vector.tensor_tensor(win_n[:, 0, :], win_i[:, 1, :], win_i[:, 0, :], ALU.subtract))
            link(nc.vector.tensor_tensor_scan(win_n[:, 1, :], win_n[:, 0, :], zero_r[:, :], 0.0, ALU.add, ALU.add))
            link(nc.vector.memset(win_w[:, :, :], 0.0))
            nc.vector.scalar_tensor_tensor(out=win_w[:, 0, BACK:NG + BACK], in0=win_n[:, 0, :], scalar=32.0,
                                           in1=win_i[:, 0, :], op0=ALU.mult, op1=ALU.add)
            link(nc.vector.tensor_copy(win_w[:, 1, BACK + 1:NG + BACK], win_n[:, 1, 0:NG - 1]))
            nc.vector.scalar_tensor_tensor(out=window[:, :], in0=win_w[:, 1, :], scalar=1024.0, in1=win_w[:, 0, :],
                                           op0=ALU.mult, op1=ALU.add).then_inc(win_ok, 2)

            step(NT // 2 - 1, 1, NT // 4 - 1, 0)

            def largest(q):
                return nc.vector.scalar_tensor_tensor(out=Wt[:, q, :, :], in0=E1[:, q, :, :], scalar=FINITE,
                                                      in1=E2[:, q, :, :], op0=ALU.min, op1=ALU.max)

            def masked(q, w, g, tile):
                for c in range(GC):
                    m = nc.vector.scalar_tensor_tensor(
                        out=S[:, w, c, :], in0=node_id[:, bass.ds(tile * P, P)], scalar=dstT[:, bass.ds(GC * g + c, 1)],
                        in1=Wt[:, q, c, :], op0=ALU.is_equal, op1=ALU.mult)
                return m

            def add(q, tile, count):
                a = acc[:, bass.ds(tile, 1), :, :].rearrange("p t a d -> p (t a) d")
                nc.vector.tensor_tensor(a, a, ps_agg[q][:, :, 0:HALF], ALU.add).then_inc(count, 1)

            def settle(sem_, at):
                dve.wait_ge(sem_, at)
                nc.vector.memset(spare[:, 0:1], 0.0)

            def weigh_extra(g, tile, at):
                dve.wait_ge(xS_ok, at)
                dve.wait_ge(xexp_ok, at)
                largest(2).then_inc(xmax_ok, 1)
                dve.wait_ge(xmax_ok, at + 1)
                masked(2, SR, g, tile).then_inc(xS_ok, 1)

            def add_extra(n_added, tile, at):
                dve.wait_ge(added, n_added)
                dve.wait_ge(xagg_ok, at)
                add(2, tile, xadded)
                settle(xadded, at + 1)

            def extras(g, n_added, last, word):
                if last is not None:
                    last_extra = extra_in(last)
                    with dve.If(last_extra > 0):
                        add_extra(n_added, tile_of(tile_in(last) + last_extra), before_in(last) + last_extra)
                if word is not None:
                    extra = dve.snap(extra_in(word))
                    with dve.If(extra > 0):
                        tile, before = dve.snap(tile_in(word)), dve.snap(before_in(word))
                        weigh_extra(g, tile_of(tile + 1), before + 1)
                        with dve.If(extra > 1):
                            with dve.Fori(1, extra) as n:
                                add_extra(n_added, tile_of(tile + n), before + n)
                                weigh_extra(g, tile_of(tile + n + 1), before + n + 1)

            def step_of_group(g, r, i, first=False, words=None):
                words_at = r + BACK
                word = lambda back: dve.snap(regs[words_at - back])
                r %= RING
                if words is None:
                    dve.wait_ge(exp_ok, g + 1)
                    if not (first and r < 2):
                        dve.wait_ge(S_ok, g - 1)
                    largest(r % 2).then_inc(max_ok[r % 2], 1)
                if not (first and r < 3):
                    tile = dve.snap(tile_in(word(3)))
                    if not (first and r < 4):
                        dve.wait_ge(added, g - 3)
                    dve.wait_ge(agg_ok, g - 2)
                    add((r - 3) % 2, tile, added)
                if words is None or words < 1:
                    if not (first and r < 1):
                        tile = dve.snap(tile_in(word(1)))
                        dve.wait_ge(max_ok[(r - 1) % 2], RING // 2 * i + (r + 1) // 2 + 1)
                        masked((r - 1) % 2, (r - 1) % SR, g - 1, tile).then_inc(S_ok, 1)
                n_added = g - 2 if not (first and r < 3) else 0
                if first and r < 2:
                    if r == 1:
                        extras(g - 1, n_added, None, word(1))
                elif words is None or words < 1:
                    either = dve.snap((word(2) | word(1)) & (31 << 5))
                    with dve.If(either > 0):
                        extras(g - 1, n_added, word(2), word(1))
                elif words < 2:
                    extras(g - 1, n_added, word(2), None)

            dve.wait_ge(win_ok, 2)
            dve.wait_ge(ids_ok, 1)
            dve.wait_ge(edges_ok, 2)
            window_words(dve, regs, 0, BACK)
            for r in range(RING):
                step_of_group(r, r, 0, first=True)
            with dve.Fori(1, NG // RING) as i:
                window_words(dve, regs, i, BACK)
                for r in range(RING):
                    step_of_group(RING * i + r, r, i)
            for k in range(BACK):
                step_of_group(NG + k, RING + k, NG // RING, words=k)
            dve.wait_ge(added, NG)
            last_word = dve.snap(regs[RING + BACK - 1])
            settle(xadded, before_in(last_word) + extra_in(last_word) + 1)
            dve.wait_ge(agg_ok, NG)
            den = acc[:, :, 0, ONE]
            link(nc.vector.tensor_single_scalar(rden[:, :], den, 0.0, ALU.is_equal))
            link(nc.vector.tensor_tensor(rden[:, :], rden[:, :], den, ALU.add))
            link(nc.vector.reciprocal(rden[:, :], rden[:, :]))
            nc.vector.memset(spare[:, 0:1], 0.0).then_inc(acc_ok, 1)

            def x1_of(u, s):
                for j in range(2):
                    a = features(2 * u + j)
                    dve.wait_ge(ld_x2[s][j], 16 * (u // 2 + 1) if isinstance(u, int) else u * 8 + 16 - 8 * s)
                    nc.vector.scalar_tensor_tensor(out=a, in0=a, scalar=rden[:, bass.ds(2 * u + j, 1)],
                                                   in1=halves(x_in[:, s, j, :]), op0=ALU.mult, op1=ALU.add).then_inc(x1_ok, 1)
                if not (isinstance(u, int) and u < 1):
                    dve.wait_ge(xn2_ok, 2 * u - 2)
                dve.wait_ge(x1_ok, 2 * u + 2)
                nc.vector.memset(spare[:, 0:1], 0.0)
                for j in range(2):
                    a = features(2 * u + j)
                    m = nc.vector.bn_stats(stats[:, s, j, :], a)
                m.then_inc(stats2_ok, 1)
                dve.wait_ge(stats2_ok, u + 1)
                nc.vector.memset(spare[:, 1:2], 0.0)
                for j in range(2):
                    m = nc.vector.bn_aggr(mv[:, s, j, :], stats[:, s, j, :])
                m.then_inc(aggr2_ok, 1)

            def normal2(u, s):
                dve.wait_ge(std2_ok, u + 1)
                nc.vector.reciprocal(rstd[:, s, :], std[:, s, :]).then_inc(rstd2_ok, 1)
                dve.wait_ge(rstd2_ok, u + 1)
                if not (isinstance(u, int) and u < 2):
                    dve.wait_ge(xnT_ps, u - 1)
                for j in range(2):
                    if not (isinstance(u, int) and u < 2):
                        dve.wait_ge(st_xn[s][j], 16 * (u // 2) if isinstance(u, int) else u * 8 - 8 * s)
                    a = features(2 * u + j)
                    nc.vector.tensor_scalar(halves(xn[:, s, j, :]), a, mv[:, s, j, 0:1], rstd[:, s, j:j + 1],
                                            ALU.subtract, ALU.mult).then_inc(xn2_ok, 1)

            x1_of(0, 0)

            def two_steps(i):
                x1_of(2 * i + 1, 1)
                normal2(2 * i, 0)
                x1_of(2 * i + 2, 0)
                normal2(2 * i + 1, 1)

            two_steps(0)
            with dve.Fori(1, NT // 4 - 1) as i:
                two_steps(i)
            x1_of(NT // 2 - 1, 1)
            normal2(NT // 2 - 2, 0)
            normal2(NT // 2 - 1, 1)

            V = nc.vector
            dve.wait_ge(consts_ok, 2)
            V.tensor_copy(part1[:, :], part_i[:, :])
            link(V.tensor_copy(count[:, :], count_i[:, :]))

            def bc_t(ap):
                return ap.unsqueeze(2).to_broadcast([P, NT, NX])

            dve.wait_ge(logit_ps, NT // 2)
            link(V.tensor_tensor(score[:, :, :], ps_logit[:, 0:NT * NX].rearrange("p (t e) -> p t e", e=NX),
                                 bg_b[:, :].unsqueeze(1).to_broadcast([P, NT, NX]), ALU.add))
            link(V.tensor_reduce(red[:, :], score[:, :, :], AX.X, ALU.max))
            V.tensor_tensor(score[:, :, :], score[:, :, :], bc_t(red[:, :]), ALU.subtract).then_inc(shift_ok, 1)
            dve.wait_ge(exp2_ok, 1)
            link(V.tensor_reduce(red[:, :], pr[:, :, :], AX.X, ALU.add))
            link(V.reciprocal(red[:, :], red[:, :]))
            link(V.tensor_tensor(pr[:, :, :], pr[:, :, :], bc_t(red[:, :]), ALU.mult))
            expert_id = count[:, 0:NX].unsqueeze(1).to_broadcast([P, NT, NX])
            for c in range(2):
                link(V.tensor_reduce(prob[:, c, :], pr[:, :, :], AX.X, ALU.max))
                link(V.tensor_tensor(pick[:, :, :], pr[:, :, :], bc_t(prob[:, c, :]), ALU.is_equal))
                link(V.scalar_tensor_tensor(out=pick[:, :, :], in0=pick[:, :, :], scalar=-float(NX), in1=expert_id,
                                            op0=ALU.mult, op1=ALU.add))
                link(V.tensor_reduce(red[:, :], pick[:, :, :], AX.X, ALU.min))
                link(V.tensor_single_scalar(red[:, :], red[:, :], float(NX), ALU.add))
                link(V.tensor_tensor(pick[:, :, :], expert_id, bc_t(red[:, :]), ALU.is_equal))
                link(V.tensor_tensor(choice[:, :, c, :], pick[:, :, :].rearrange("p t e -> p e t"),
                                     valid[:, c, :].unsqueeze(1).to_broadcast([P, NX, NT]), ALU.mult))
                if c == 0:
                    link(V.scalar_tensor_tensor(out=pr[:, :, :], in0=pick[:, :, :], scalar=-2.0, in1=pr[:, :, :],
                                                op0=ALU.mult, op1=ALU.add))
            flat = choice[:, :, :, :].rearrange("p e c t -> p (e c t)")
            by_item = choice[:, :, :, :].rearrange("p e c t -> p e (c t)")
            V.tensor_reduce(per[:, 0, :], by_item, AX.X, ALU.add).then_inc(cnt_ok, 1)
            link(V.tensor_tensor_scan(rank[:, :, :].rearrange("p e i -> p (e i)"), flat, zeros[:, :], 0.0,
                                      ALU.add, ALU.add))
            dve.wait_ge(cnt_ok, 1)
            link(V.tensor_tensor(per[:, 1, :], rank[:, :, ITEMS - 1], per[:, 0, :], ALU.subtract))
            dve.wait_ge(cnt_ps, 1)
            link(V.tensor_single_scalar(per_i[:, :], ps_sum[:, NX:2 * NX], float(P - 1), ALU.add))
            link(V.tensor_single_scalar(per_i[:, :], per_i[:, :], P.bit_length() - 1, ALU.arith_shift_right))
            link(V.tensor_copy(per[:, 2, :], per_i[:, :]))
            link(V.tensor_tensor_scan(per[:, 3, :], per[:, 2, :], zeros[:, 0:NX], 0.0, ALU.add, ALU.add))
            link(V.tensor_tensor(per[:, 5, :], per[:, 3, :], per[:, 2, :], ALU.subtract))
            link(V.scalar_tensor_tensor(out=per[:, 4, :], in0=per[:, 5, :], scalar=float(P), in1=ps_sum[:, 0:NX],
                                        op0=ALU.mult, op1=ALU.add))
            link(V.scalar_tensor_tensor(out=per[:, 6, :], in0=per[:, 4, :], scalar=-1.0, in1=per[:, 1, :],
                                        op0=ALU.add, op1=ALU.subtract))
            link(V.tensor_tensor(rank[:, :, :], rank[:, :, :], per[:, 6, :].unsqueeze(2).to_broadcast([P, NX, ITEMS]),
                                 ALU.add))
            link(V.tensor_tensor(rank[:, :, :], rank[:, :, :], by_item, ALU.mult))
            link(V.tensor_reduce(pos[:, :], rank[:, :, :].rearrange("p e i -> p i e"), AX.X, ALU.add))
            vflat = valid[:, :, :].rearrange("p c t -> p (c t)")
            link(V.scalar_tensor_tensor(out=pos[:, :], in0=vflat, scalar=float(TILES * P), in1=pos[:, :],
                                        op0=ALU.mult, op1=ALU.add))
            link(V.tensor_single_scalar(pos_i[:, 0, :], pos[:, :], -float(TILES * P), ALU.add))
            link(V.tensor_single_scalar(pos_i[:, 1, :], pos_i[:, 0, :], P.bit_length() - 1, ALU.arith_shift_right))
            link(V.tensor_single_scalar(pos_i[:, 2, :], pos_i[:, 0, :], P - 1, ALU.bitwise_and))
            link(V.tensor_copy(pos_f[:, :, :], pos_i[:, 1:3, :]))
            tile_id = count[:, 0:TILES].unsqueeze(1).to_broadcast([P, ITEMS, TILES])
            V.tensor_tensor(hot_r[:, :, :], pos_f[:, 1, :].unsqueeze(2).to_broadcast([P, ITEMS, P]),
                            count[:, :].unsqueeze(1).to_broadcast([P, ITEMS, P]), ALU.is_equal)
            link(V.tensor_tensor(hot_t[:, :, :], pos_f[:, 0, :].unsqueeze(2).to_broadcast([P, ITEMS, TILES]),
                                 tile_id, ALU.is_equal))
            V.tensor_scalar(hot_v[:, 0, :, :], hot_t[:, :, :], part1[:, :], None, ALU.mult)
            V.tensor_tensor(hot_v[:, 1, :, :], hot_t[:, :, :],
                            count[:, 1:ITEMS + 1].unsqueeze(2).to_broadcast([P, ITEMS, TILES]), ALU.mult)\
                .then_inc(hot_ok, 1)
            link(V.tensor_tensor(ends[:, :, :], per[0:1, 3, :].unsqueeze(1).to_broadcast([1, TILES, NX]),
                                 count[0:1, 0:TILES].unsqueeze(2).to_broadcast([1, TILES, NX]), ALU.is_le))
            link(V.tensor_reduce(end_n[:, :], ends[:, :, :], AX.X, ALU.add))
            V.tensor_single_scalar(expert_of[:, 2:TILES + 2], end_n[:, :], float(NX - 1), ALU.min)
            dve.wait_ge(inv_ps, 1)
            link(V.tensor_copy(inv[:, 0:2, :].rearrange("p v t -> p (v t)"), ps_inv[:, 0:2 * TILES]))
            link(V.scalar_tensor_tensor(out=inv[:, 2, :], in0=inv[:, 1, :], scalar=float(P), in1=inv[:, 0, :],
                                        op0=ALU.mult, op1=ALU.add))
            link(V.tensor_single_scalar(inv[:, 2, :], inv[:, 2, :], -float(P + 1), ALU.add))
            link(V.tensor_single_scalar(inv[:, 0, :], inv[:, 2, :], float(NTN), ALU.is_ge))
            link(V.scalar_tensor_tensor(out=inv[:, 0, :], in0=inv[:, 0, :], scalar=-float(NTN), in1=inv[:, 2, :],
                                        op0=ALU.mult, op1=ALU.add))
            V.tensor_single_scalar(src_row[:, :], inv[:, 0, :], 0.0, ALU.max)
            link(V.tensor_single_scalar(inv[:, 1, :], inv[:, 2, :], 0.0, ALU.is_lt))
            link(V.tensor_tensor(inv[:, 1, :], inv[:, 1, :], beyond[:, :], ALU.mult))
            link(V.tensor_tensor(dst_row[:, :], inv[:, 2, :], inv[:, 1, :], ALU.add))
            V.memset(spare[:, 0:1], 0.0).then_inc(routed, 1)

            def tile_step(i, n, e_new, e_old):
                s, r, peeled = i % 2, i % YR, isinstance(n, int)
                if e_old is not None:
                    dve.wait_ge(hidT_ps, n - 1)
                    if not (peeled and n < 4):
                        dve.wait_ge(y_ps, n - 3)
                    nc.vector.tensor_copy(hidT[:, s, :], ps_hT[:, 0:F]).then_inc(hidT_ok, 1)
                    e = expert_in(dve, e_old)
                    r2 = (i - 2) % YR
                    if not (peeled and n < 2 + YR):
                        dve.wait_ge(put_y[r2], 16 * ((n - 2) // YR) if peeled else 4 * (n - 2 - r2))
                    dve.wait_ge(y_ps, n - 1)
                    nc.vector.tensor_tensor(y[:, r2, :], ps_y[s][:, :],
                                            b2_b[:, bass.ds(e, 1), :].rearrange("p e d -> p (e d)"), ALU.add)\
                        .then_inc(y_ok, 1)
                if e_new is not None:
                    e = expert_in(dve, e_new)
                    if not (peeled and n < 2):
                        dve.wait_ge(gelu_ok, n - 1)
                    dve.wait_ge(hid_ps, n + 1)
                    nc.vector.tensor_tensor(hid[:, s, :], ps_hid[s][:, 0:F],
                                            b1_b[:, bass.ds(e, 1), :].rearrange("p e f -> p (e f)"), ALU.add)\
                        .then_inc(hid_ok, 1)

            dve.wait_ge(routed, 1)
            over_tiles(dve, regs[0:6], tile_step)

            def share(t, r, k, from_, ld, count_, done=0):
                a = features(t)
                dve.wait_ge(ld[r], k)
                if count_ is fin_b:
                    dve.wait_ge(fin_a, t + 1)
                nc.vector.scalar_tensor_tensor(out=a, in0=halves(from_[:, r, :]), scalar=prob[:, done, bass.ds(t, 1)], in1=a,
                                               op0=ALU.mult, op1=ALU.add).then_inc(count_, 1)

            with dve.Fori(0, NT // YR) as i:
                for r in range(YR):
                    share(YR * i + r, r, 16 * (i + 1), ya, ld_ya, fin_a)
                for r in range(YR):
                    share(YR * i + r, r, 16 * (i + 1), yb, ld_yb, fin_b, 1)


_INS = ["x", "src", "dst", "L0_gnn_W", "L0_gnn_b_w", "L0_gnn_a", "L0_gnn_b_a", "L0_ffn_Wg", "L0_ffn_bg",
        "L0_ffn_W1", "L0_ffn_b1", "L0_ffn_W2", "L0_ffn_b2"]


def kernel(**inputs):
    import numpy as _np
    import concourse.bacc as _bacc
    from concourse import mybir as _mybir
    from concourse.bass_utils import run_bass_kernel_spmd as _run

    nc = _bacc.Bacc("TRN2", target_bir_lowering=False, num_devices=1)
    arrays, args = {}, []
    for name in _INS:
        a = _np.ascontiguousarray(inputs[name])
        if a.ndim == 0:
            a = a.reshape(1)
        arrays[f"in_{name}_dram"] = a
        args.append(nc.dram_tensor(f"in_{name}_dram", a.shape, _mybir.dt.from_np(a.dtype), kind="ExternalInput").ap())
    shape = _np.shape(inputs["x"])
    args.append(nc.dram_tensor("out_0_dram", shape, _mybir.dt.float32, kind="ExternalOutput").ap())
    gnn_moe_kernel(nc, *args)
    r = _run(nc, [arrays], core_ids=[0])
    return r.results[0]["out_0_dram"]
```

```python
from contextlib import ExitStack

import concourse.bass as bass
from concourse import mybir

P = 128
F32 = mybir.dt.float32
F32R = mybir.dt.float32r
BF16 = mybir.dt.bfloat16
I32 = mybir.dt.int32
I16 = mybir.dt.int16
ALU = mybir.AluOpType
ACT = mybir.ActivationFunctionType
AX = mybir.AxisListType

EPS = 1e-5
SLOPE = 0.2
FINITE = 3.0e38


def gnn_moe_kernel(nc, x, src, dst, gnn_W, gnn_b_w, gnn_a, gnn_b_a, Wg, bg, W1, b1, W2, b2, out):
    N, D = x.shape
    E = src.shape[0]
    KT = D // P
    NT = -(-N // P)
    LAST = N - (NT - 1) * P
    NTN = NT * P
    CH = -(-E // P)
    CJ = -(-CH // P)
    GC = 2
    RING = 10
    NG = -(-CH // (RING * GC)) * RING
    SR = 5
    BACK = 3
    HD = D // 2
    HALF = HD + 1
    ROW = 2 * HALF + 2
    ONE, S_SRC = HD, 2 * HALF - 1

    NX, F = W1.shape[0], W1.shape[2]
    HF = F // P
    ITEMS = 2 * NT
    TILES = (2 * N + NX * (P - 1)) // P
    YR = 4
    LAG = YR + 2

    table = nc.dram_tensor("node_table", [NTN, ROW], F32).ap()
    xn_table = nc.dram_tensor("xn_table", [NTN, D], F32).ap()
    result = nc.dram_tensor("result", [NTN + P, D], F32).ap()

    with ExitStack() as ctx:
        def sb(name, shape, dt):
            return ctx.enter_context(nc.sbuf_tensor(name, shape, dt))

        def sem(name):
            return ctx.enter_context(nc.semaphore(name))

        rden = sb("rden", [P, NT], F32)
        ident = sb("ident", [P, P], F32)
        stats = sb("stats", [P, 2, 2, 6], F32)
        mv = sb("mv", [P, 2, 2, 2], F32)
        std = sb("std", [P, 2, 2], F32)
        rstd = sb("rstd", [P, 2, 2], F32)
        shift = sb("shift", [P, 2, 2], F32)
        spare = sb("spare", [P, 3], F32)
        start = sb("start", [P, 5], F32)
        eps = sb("eps", [P, 1], F32)

        top = [0]

        def size(shape, dt):
            n = 1
            for k in shape[1:]:
                n *= k
            return -(-n * (2 if dt in (BF16, I16) else 4) // 32) * 32

        def sg(name, shape, dt, into=None):
            top[0] += size(shape, dt)
            return (into or ctx).enter_context(nc.sbuf_tensor(name, shape, dt))

        def reach(name, end):
            if end > top[0]:
                sg(name, [P, (end - top[0]) // 4], F32)
            assert top[0] <= end

        early = ctx.enter_context(ExitStack())
        acc = sg("acc", [P, NT, 2, HALF], F32, early)
        x_in = sg("x_in", [P, 2, 2, D], F32, early)
        xn = sg("xn", [P, 2, 2, D], F32, early)
        wa_rep = sg("wa_rep", [P, 2, KT, P], F32R, early)
        s_dot = sg("s_dot", [P, 2, 2], F32, early)
        cst = sg("cst", [P, 1], F32, early)
        cst2 = sg("cst2", [P, 2], F32, early)
        win_i = sg("win_i", [1, 2, NG], I32, early)
        region1 = top[0]
        rows = sg("rows", [P, RING, GC, ROW], F32, early)
        sdst_b = sg("sdst_b", [P, NTN], F32, early)
        node_id = sg("node_id", [P, NTN], I16, early)
        ba_b = sg("ba_b", [P, 1], F32, early)
        srcT = sg("srcT", [P, NG * GC], I32, early)
        dstT = sg("dstT", [P, NG * GC], F32, early)
        idx = sg("idx", [P, RING, GC], I32, early)
        ch_mm = sg("ch_mm", [P, 2, CJ], F32, early)
        window = sg("window", [1, NG + BACK], I32, early)
        E1 = sg("E1", [P, 3, GC, P], F32, early)
        E2 = sg("E2", [P, 3, GC, P], F32, early)
        Wt = sg("Wt", [P, 3, GC, P], F32, early)
        S = sg("S", [P, SR + 1, GC, P], F32, early)

        bw_b = sg("bw_b", [P, D], F32, early)
        win_f = sg("win_f", [1, 2, NG], F32, early)
        win_n = sg("win_n", [1, 3, NG], F32, early)
        zero_r = sg("zero_r", [1, NG], F32, early)
        win_w = sg("win_w", [1, 2, NG + BACK], F32, early)
        region2 = top[0]
        xT = sg("xT", [P, 2, 2, KT, 2 * P], F32R, early)
        Wb = sg("Wb", [P, 2, KT, D], F32R, early)
        Wf = sg("Wf", [P, KT, D], F32, early)
        a_b = sg("a_b", [P, 2, D], F32, early)
        junk = sg("junk", [P, 2, D], F32, early)
        edge_i = sg("edge_i", [P, 2, CJ, P], I32, early)
        edge_f = sg("edge_f", [P, 2, CJ, P], F32, early)
        wa = sg("wa", [P, KT], F32, early)
        wa_hl = sg("wa_hl", [P, 2, KT], F32R, early)
        region3 = region2 + max(top[0] - region2, NX * (KT * F + HF * D) * 4)
        early.close()

        top[0] = 0
        W1_hi = sg("W1_hi", [P, NX, KT, F], F32R)
        xg = sg("xg", [P, YR, D], F32)
        gi = sg("gi", [P, YR, 1], I32)
        si = sg("si", [P, YR, 1], I32)
        hot = ctx.enter_context(ExitStack())
        before_hot = top[0]
        hot_r = sg("hot_r", [P, ITEMS, P], BF16, hot)
        hot_t = sg("hot_t", [P, ITEMS, TILES], BF16, hot)
        hot_v = sg("hot_v", [P, 2, ITEMS, TILES], BF16, hot)
        assert top[0] <= region1
        hot.close()
        top[0] = before_hot
        xgT = sg("xgT", [P, 2, 2, KT * P], F32R)
        hid = sg("hid", [P, 2, F], F32)
        act_h = sg("act_h", [P, 2, F], F32)
        reach("gap1", region1)

        expert_of = sg("expert_of", [1, TILES + 4], I32)
        src_row = sg("src_row", [P, TILES], I32)
        dst_row = sg("dst_row", [P, TILES], I32)
        share = sg("share", [P, TILES], F32)
        b1_b = sg("b1_b", [P, NX, F], F32)
        b2_b = sg("b2_b", [P, NX, D], F32)
        W2_hi = sg("W2_hi", [P, NX, HF, D], F32R)
        routing = ctx.enter_context(ExitStack())
        before_routing = top[0]

        def sr(name, shape, dt):
            return sg(name, shape, dt, routing)

        Wg_sb = sr("Wg_sb", [P, KT, NX], F32)
        bg_c = sr("bg_c", [NX, 1], F32)
        count_i = sr("count_i", [P, P], I32)
        count = sr("count", [P, P], F32)
        count_b = sr("count_b", [P, P], BF16)
        part_i = sr("part_i", [P, 1], I32)
        part1 = sr("part1", [P, 1], F32)
        beyond = sr("beyond", [P, TILES], F32)
        beyond_i = sr("beyond_i", [P, TILES], I32)
        valid = sr("valid", [P, 2, NT], F32)
        below = sr("below", [P, P], F32)
        all_1 = sr("all_1", [P, P], F32)
        prob = sr("prob", [P, 2, NT], F32)
        score = sr("score", [P, NT, NX], F32)
        pr = sr("pr", [P, NT, NX], F32)
        pick = sr("pick", [P, NT, NX], F32)
        red = sr("red", [P, NT], F32)
        choice = sr("choice", [P, NX, 2, NT], F32)
        rank = sr("rank", [P, NX, ITEMS], F32)
        zeros = sr("zeros", [P, NX * ITEMS], F32)
        per = sr("per", [P, 7, NX], F32)
        per_i = sr("per_i", [P, NX], I32)
        pos = sr("pos", [P, ITEMS], F32)
        pos_i = sr("pos_i", [P, 3, ITEMS], I32)
        pos_f = sr("pos_f", [P, 2, ITEMS], F32)
        prob_b = sr("prob_b", [P, 3, ITEMS], BF16)
        prob_r = sr("prob_r", [P, 2, ITEMS], F32)
        inv = sr("inv", [P, 3, TILES], F32)
        ends = sr("ends", [1, TILES, NX], F32)
        end_n = sr("end_n", [1, TILES], F32)
        transposed = ctx.enter_context(ExitStack())
        before_xnT = top[0]
        xnT = sg("xnT", [P, 2, KT, 2, P], F32, transposed)
        logT = sg("logT", [NX, 2, 2 * P], F32, transposed)
        transposed.close()
        top[0] = before_xnT
        hot_p = sr("hot_p", [P, 3, ITEMS, TILES], BF16)
        assert top[0] <= region2
        routing.close()
        top[0] = before_routing
        hidT = sg("hidT", [P, 2, 2, HF * P], F32R)
        y_b = sg("y_b", [P, 2, D], F32)
        y = sg("y", [P, YR, D], F32)
        reach("gap2", region2)

        whole = ctx.enter_context(ExitStack())
        W1_e = sg("W1_e", [P, NX, KT, F], F32, whole)
        W2_e = sg("W2_e", [P, NX, HF, D], F32, whole)
        assert top[0] <= region3
        whole.close()
        W1_lo = sg("W1_lo", [P, NX, KT, F], F32R)
        W2_lo = sg("W2_lo", [P, NX, HF, D], F32R)

        pair = [ctx.enter_context(nc.psum_tensor(f"ps{i}", [P, 2, 512], F32)) for i in range(4)]
        ps = [pair[i // 2][:, i % 2, :] for i in range(8)]
        psT = [[ps[2 * s], ps[2 * s + 1]] for s in range(2)]
        ps_h, ps_edge, ps_d = [ps[4], ps[5]], ps[6], ps[7]
        ps_agg = pair[0:3]
        ps_logT = [ps[6], ps[7]]
        ps_logit, ps_sum, ps_inv, ps_share = ps[4], ps[5], ps[6], ps[7]
        ps_x, ps_hT, ps_hid, ps_y = ps[0], ps[1], [ps[2], ps[3]], [ps[4], ps[5]]

        def halves(ap):
            return ap.rearrange("p (a d) -> p a d", a=2)

        def features(t):
            return acc[:, bass.ds(t, 1), :, 0:HD].rearrange("p t a d -> p (t a) d")

        ld_x = [[sem(f"ld_x{s}{j}") for j in range(2)] for s in range(2)]
        ld_W, ld_edge, ld_par = sem("ld_W"), sem("ld_edge"), sem("ld_par")
        pads, ident_ok, ids_ok, zeros_ok = sem("pads"), sem("ident_ok"), sem("ids_ok"), sem("zeros_ok")
        dv = sem("dv_setup")
        W_hi, W_ok, wa_ok, edges_f, edges_ps, edges_ok = (sem(n) for n in (
            "W_hi", "W_ok", "wa_ok", "edges_f", "edges_ps", "edges_ok"))
        mm_ps, win_ok, mm_ok = sem("mm_ps"), sem("win_ok"), sem("mm_ok")
        stats_ok, std_ok, rstd_ok, xn_ok = (sem(n) for n in ("stats_ok", "std_ok", "rstd_ok", "xn_ok"))
        xT_ps, xT_hi, xT_lo = sem("xT_ps"), sem("xT_hi"), sem("xT_lo")
        h_ps, row_ok, d_ps, d_ok = (sem(n) for n in ("h_ps", "row_ok", "d_ps", "d_ok"))
        dot_ok, s_ok = sem("dot_ok"), sem("s_ok")
        st_row = [[sem(f"st_row{s}{j}") for j in range(2)] for s in range(2)]
        idx_ok = sem("idx_ok")
        got = [sem(f"got{r}") for r in range(RING)]
        exp_ok = sem("exp_ok")
        max_ok = [sem("max_ok0"), sem("max_ok1")]
        S_ok, agg_ok = sem("S_ok"), sem("agg_ok")
        xexp_ok, xmax_ok, xS_ok, xagg_ok = (sem(n) for n in ("xexp_ok", "xmax_ok", "xS_ok", "xagg_ok"))
        acc_ok, added, xadded = sem("acc_ok"), sem("added"), sem("xadded")
        ld_x2 = [[sem(f"ld_x2_{s}{j}") for j in range(2)] for s in range(2)]
        st_xn = [[sem(f"st_xn_{s}{j}") for j in range(2)] for s in range(2)]
        ld_b = sem("ld_b")
        ld_late, ld_W1, ld_W2 = sem("ld_late"), sem("ld_W1"), sem("ld_W2")
        x1_ok, stats2_ok, aggr2_ok, std2_ok, rstd2_ok, xn2_ok = (sem(n) for n in (
            "x1_ok", "stats2_ok", "aggr2_ok", "std2_ok", "rstd2_ok", "xn2_ok"))
        xnT_ps, xnT_ok, logT_ps, logT_ok, logit_ps = (sem(n) for n in (
            "xnT_ps", "xnT_ok", "logT_ps", "logT_ok", "logit_ps"))
        shift_ok, exp2_ok, cnt_ok, cnt_ps = sem("shift_ok"), sem("exp2_ok"), sem("cnt_ok"), sem("cnt_ps")
        hot_ok, inv_ps, routed = sem("hot_ok"), sem("inv_ps"), sem("routed")
        consts_ok, share_ok = sem("consts_ok"), sem("share_ok")
        st_x1 = sem("st_x1")
        W1_hi_ok, W2_hi_ok, W1_lo_ok, W2_lo_ok = (sem(n) for n in ("W1_hi_ok", "W2_hi_ok", "W1_lo_ok", "W2_lo_ok"))
        gi_ok, si_ok = sem("gi_ok"), sem("si_ok")
        got_x = [sem(f"got_x{r}") for r in range(YR)]
        put_y = sem("put_y")
        x_ps, x_hi, x_lo, hid_ps, hid_ok, gelu_ok, hidT_ps, hidT_hi, hidT_lo, y_ps, yb_ok, y_ok = (sem(n) for n in (
            "x_ps", "x_hi", "x_lo", "hid_ps", "hid_ok", "gelu_ok", "hidT_ps", "hidT_hi", "hidT_lo", "y_ps", "yb_ok",
            "y_ok"))
        st_out = sem("st_out")

        def experts(eng, regs, i):
            eng.load(regs, expert_of[0:1, bass.ds(i, len(regs))])

        def expert_in(eng, reg):
            return nc.s_assert_within(eng.snap(reg), 0, NX - 1,
                                      skip_runtime_bounds_check_because="the table's words are built so")

        def over_steps(eng, step):
            for u in range(4):
                step(u, u % 2)
            with eng.Fori(2, NT // 4 - 1) as i:
                for s in range(2):
                    step(2 * i + s, s)
            for u in range(NT // 2 - 2, NT // 2 + 2):
                step(u, u % 2)

        def over_tiles(eng, regs, step):
            def some(i, n, at):
                if regs:
                    experts(eng, regs[0:n + 1], i)
                for k in range(n):
                    step(at + k, i + k, regs[k + 1] if regs else None, regs[k] if regs else None)
            some(0, 4, 0)
            some(4, 4, 4)
            with eng.Fori(2, TILES // 4) as b:
                some(4 * b, 4, 4)
            for i in range(TILES // 4 * 4, TILES + 2):
                some(i, 1, i)

        def parts_of(i):
            return i < TILES, 1 <= i <= TILES, i >= 2

        def window_words(eng, regs, i, back=0):
            eng.load(regs, window[0:1, bass.ds(RING * i + BACK - back, len(regs))])

        def field(word, shift, mask, most):
            return nc.s_assert_within((word >> shift) & mask if shift else word & mask, 0, most,
                                      skip_runtime_bounds_check_because="the table's words are built so")

        def tile_in(word):
            return field(word, 0, 31, NT - 1)

        def extra_in(word):
            return field(word, 5, 31, NT - 1)

        def before_in(word):
            return field(word, 10, 4095, NG * NT)

        def tile_of(value):
            return nc.s_assert_within(value, 0, NT - 1, skip_runtime_bounds_check_because="a tile of the window")

        block = ctx.enter_context(nc.Block())

        @block.sync
        def _(sp):
            def load_x(u, s, j):
                if u is not None:
                    tile = x[0:(NT - 1) * P, :].rearrange("(t p) d -> t p d", p=P)[bass.ds(2 * u + j, 1)]
                    sp.dma_start(x_in[:, s, j, :], tile.rearrange("t p d -> (t p) d")).then_inc(ld_x[s][j], 16)
                else:
                    sp.dma_start(x_in[0:LAST, s, j, :], x[(NT - 1) * P:N, :]).then_inc(ld_x[s][j], 16)

            def store_rows(u, s, i):
                sp.wait_ge(s_ok, u + 1)
                for j in range(2):
                    sp.wait_ge(row_ok, 2 * u + j + 1)
                    sp.dma_start(table[bass.ds((2 * u + j) * P, P), :], rows[:, s, j, :])\
                        .then_inc(st_row[s][j], 16)

            load_x(0, 0, 0)
            load_x(0, 0, 1)
            sp.dma_start(Wf[:, :, :], gnn_W.rearrange("(k p) n -> p k n", p=P)).then_inc(ld_W, 16)
            load_x(1, 1, 0)
            load_x(1, 1, 1)
            full = (CH - 1) * P if E % P else E
            sp.wait_ge(pads, 1)
            for k, e in enumerate((src, dst)):
                jf = full // (P * P)
                sp.dma_start(edge_i[:, k, 0:jf, :], e[0:jf * P * P].rearrange("(j q i) -> q j i", q=P, i=P))\
                    .then_inc(ld_edge, 16)
                q = (full - jf * P * P) // P
                sp.dma_start(edge_i[0:q, k, jf, :], e[jf * P * P:full].rearrange("(q i) -> q i", i=P))\
                    .then_inc(ld_edge, 16)
                sp.dma_start(edge_i[q:q + 1, k, jf, 0:E - full], e[full:E].rearrange("(q i) -> q i", q=1))\
                    .then_inc(ld_edge, 16)
            sp.dma_start(bw_b[:, :], gnn_b_w.partition_broadcast(P)).then_inc(ld_par, 16)
            sp.dma_start(a_b[:, :, :].rearrange("p a d -> p (a d)"), gnn_a.partition_broadcast(P)).then_inc(ld_par, 16)
            sp.dma_start(ba_b[:, :], gnn_b_a.partition_broadcast(P)).then_inc(ld_par, 16)

            def step(u, s, i, ahead):
                if ahead:
                    for j in range(2):
                        sp.wait_ge(xn_ok, 2 * u + j + 1)
                        load_x(*((u + 2, s, j) if ahead == 1 or j == 0 else (None, s, j)))
                store_rows(u, s, i)

            with sp.Fori(0, 3) as i:
                for s in range(2):
                    step(2 * i + s, s, i, 1)
            step(6, 0, 3, 1)
            step(7, 1, 3, 2)
            step(8, 0, 4, 0)
            step(9, 1, 4, 0)

            sp.wait_ge(d_ok, NT // 2)
            sp.wait_ge(wa_ok, 1)
            sp.wait_ge(win_ok, 2)
            sp.wait_ge(row_ok, NT)
            sp.wait_ge(s_ok, NT // 2)
            with sp.Fori(0, NX) as e:
                sp.wait_ge(agg_ok, NG // (NX + 1) * e + 1)
                sp.dma_start(W1_e[:, bass.ds(e, 1), :, :].rearrange("p e k f -> p (e k) f"),
                             W1.rearrange("e (k p) f -> p e k f", p=P)[:, bass.ds(e, 1)]
                             .rearrange("p e k f -> p (e k) f")).then_inc(ld_W1, 16)
                sp.dma_start(W2_e[:, bass.ds(e, 1), :, :].rearrange("p e k d -> p (e k) d"),
                             W2.rearrange("e (k p) d -> p e k d", p=P)[:, bass.ds(e, 1)]
                             .rearrange("p e k d -> p (e k) d")).then_inc(ld_W2, 16)

            def load_x2(u, s, j, last=False):
                if last:
                    sp.dma_start(x_in[0:LAST, s, j, :], x[(NT - 1) * P:N, :]).then_inc(ld_x2[s][j], 16)
                else:
                    tile = x[0:(NT - 1) * P, :].rearrange("(t p) d -> t p d", p=P)[bass.ds(2 * u + j, 1)]
                    sp.dma_start(x_in[:, s, j, :], tile.rearrange("t p d -> (t p) d")).then_inc(ld_x2[s][j], 16)

            def store_xn(u, s):
                for j in range(2):
                    sp.wait_ge(xn2_ok, 2 * u + j + 1)
                    sp.dma_start(xn_table[bass.ds((2 * u + j) * P, P), :], xn[:, s, j, :]).then_inc(st_xn[s][j], 16)

            def x_step(u, s, last=False):
                for j in range(2):
                    sp.wait_ge(x1_ok, 2 * u + j + 1)
                    load_x2(u + 2, s, j, last and j == 1)
                sp.dma_start(halves(result[bass.ds(2 * u * P, P), :]), features(2 * u)).then_inc(st_x1, 16)
                store_xn(u, s)

            for u in range(2):
                for j in range(2):
                    load_x2(u, u, j)
            sp.wait_ge(acc_ok, 1)
            sp.dma_start(Wg_sb[:, :, :], Wg.rearrange("(k p) e -> p k e", p=P)).then_inc(ld_late, 16)
            sp.dma_start(bg_c[:, :], bg.rearrange("(e o) -> e o", o=1)).then_inc(ld_late, 16)
            with sp.Fori(0, 3) as i:
                for s in range(2):
                    x_step(2 * i + s, s)
            x_step(NT // 2 - 4, 0)
            x_step(NT // 2 - 3, 1, last=True)
            for s in range(2):
                u = NT // 2 - 2 + s
                store_xn(u, s)
            for t in [2 * u + 1 for u in range(NT // 2 - 2)] + list(range(NT - 4, NT)):
                sp.dma_start(halves(result[t * P:(t + 1) * P, :]), features(t)).then_inc(st_x1, 16)
            sp.dma_start(result[NTN:NTN + P, :].rearrange("p (a d) -> p a d", a=2), features(NT - 1)).then_inc(st_x1, 16)
            sp.dma_start(b1_b[:, :, :].rearrange("p e f -> p (e f)"),
                         b1.rearrange("e f -> (e f)").partition_broadcast(P)).then_inc(ld_b, 16)
            sp.dma_start(b2_b[:, :, :].rearrange("p e d -> p (e d)"),
                         b2.rearrange("e d -> (e d)").partition_broadcast(P)).then_inc(ld_b, 16)

            sp.wait_ge(put_y, 16 * TILES)
            sp.dma_start(out[0:N // 2, :], result[0:N // 2, :]).then_inc(st_out, 16)
            sp.wait_ge(st_out, 32)

        @block.gpsimd
        def _(pool):
            nc.gpsimd.memset(edge_i[:, 0, :, :], 0)
            nc.gpsimd.memset(edge_i[:, 1, :, :], 4095).then_inc(pads, 1)
            nc.gpsimd.memset(ident[:, :], 0.0).then_inc(zeros_ok, 1)
            pool.wait_ge(zeros_ok, 1)
            nc.gpsimd.affine_select(out=ident[:, :], in_=ident[:, :], compare_op=ALU.not_equal, fill=1.0, base=0,
                                    pattern=[[-1, P]], channel_multiplier=1).then_inc(ident_ok, 1)
            nc.gpsimd.memset(rows[:, 0:2, :, ONE:ONE + 1], 1.0)
            nc.gpsimd.memset(rows[:, 0:2, :, ROW - 1:ROW], 0.0).then_inc(pads, 1)
            nc.gpsimd.iota(node_id[:, :], pattern=[[1, NTN]], base=0, channel_multiplier=0)
            nc.gpsimd.memset(acc[:, :, :, :], 0.0).then_inc(ids_ok, 1)

            def copy_idx(g, r):
                nc.gpsimd.tensor_copy(idx[:, r, :], srcT[:, bass.ds(GC * g, GC)]).then_inc(idx_ok, 1)

            def gather(g, r, last=False):
                pool.wait_ge(idx_ok, g + 1)
                if not (isinstance(g, int) and g < RING):
                    pool.wait_ge(agg_ok, g - RING + 2)
                if not last:
                    copy_idx(g + 1, (r + 1) % RING)
                for c in range(GC):
                    nc.gpsimd.indirect_dma_start(
                        out=rows[:, r, c, :], out_offset=None, in_=table,
                        in_offset=bass.IndirectOffsetOnAxis(ap=idx[:, r, c:c + 1], axis=0)).then_inc(got[r], 16)

            pool.wait_ge(edges_ok, 2)
            for s in range(2):
                for j in range(2):
                    pool.wait_ge(st_row[s][j], 16 * NT // 4)
            copy_idx(0, 0)
            for r in range(RING):
                if r == RING - 1:
                    pool.wait_ge(agg_ok, 1)
                gather(r, r)
            with pool.Fori(1, NG // RING - 1) as i:
                for r in range(RING):
                    gather(RING * i + r, r)
            for r in range(RING):
                gather(NG - RING + r, r, last=r == RING - 1)

            pool.wait_ge(acc_ok, 1)
            nc.gpsimd.iota(count_i[:, :], pattern=[[1, P]], base=0, channel_multiplier=0)
            nc.gpsimd.iota(part_i[:, :], pattern=[[0, 1]], base=1, channel_multiplier=1)
            nc.gpsimd.iota(beyond_i[:, :], pattern=[[0, TILES]], base=NTN, channel_multiplier=1)
            nc.gpsimd.memset(all_1[:, :], 1.0)
            nc.gpsimd.memset(zeros[:, :], 0.0)
            nc.gpsimd.memset(below[:, :], 1.0)
            nc.gpsimd.memset(expert_of[:, :], 0)
            nc.gpsimd.memset(valid[:, :, :], 1.0).then_inc(consts_ok, 1)
            pool.wait_ge(consts_ok, 1)
            nc.gpsimd.affine_select(out=below[:, :], in_=below[:, :], compare_op=ALU.is_gt, fill=0.0, base=0,
                                    pattern=[[1, P]], channel_multiplier=-1)
            nc.gpsimd.affine_select(out=valid[:, :, :], in_=valid[:, :, :], compare_op=ALU.is_ge, fill=0.0,
                                    base=N - 1, pattern=[[0, 2], [-P, NT]], channel_multiplier=-1)\
                .then_inc(consts_ok, 1)

            for e in range(NX):
                pool.wait_ge(W2_hi_ok, e + 1)
                nc.gpsimd.tensor_tensor(W2_lo[:, e, :, :], W2_e[:, e, :, :], W2_hi[:, e, :, :].bitcast(F32),
                                        ALU.subtract).then_inc(W2_lo_ok, 1)
            for e in range(NX):
                pool.wait_ge(W1_hi_ok, e + 1)
                nc.gpsimd.tensor_tensor(W1_lo[:, e, :, :], W1_e[:, e, :, :], W1_hi[:, e, :, :].bitcast(F32),
                                        ALU.subtract).then_inc(W1_lo_ok, 1)

            def copy_gi(i, r):
                nc.gpsimd.tensor_copy(gi[:, r, :], src_row[:, bass.ds(i, 1)]).then_inc(gi_ok, 1)

            def copy_si(i, r):
                nc.gpsimd.tensor_copy(si[:, r, :], dst_row[:, bass.ds(i, 1)]).then_inc(si_ok, 1)

            def row_step(i, r):
                peeled = isinstance(i, int)
                has_gather, has_add = not (peeled and i >= TILES), not (peeled and i < LAG)
                if has_gather:
                    pool.wait_ge(gi_ok, i + 1)
                    if not (peeled and i < YR):
                        pool.wait_ge(x_ps, i + 1 - YR)
                if has_add:
                    pool.wait_ge(si_ok, i - LAG + 1)
                if not (peeled and (i + 1 < LAG or i + 1 >= TILES + LAG)):
                    copy_si(i + 1 - LAG, (r + 1 - LAG) % YR)
                if has_gather:
                    nc.gpsimd.indirect_dma_start(
                        out=xg[:, r, :], out_offset=None, in_=xn_table,
                        in_offset=bass.IndirectOffsetOnAxis(ap=gi[:, r, :], axis=0)).then_inc(got_x[r], 16)
                if has_add:
                    pool.wait_ge(y_ok, i - LAG + 1)
                    if not (peeled and i < LAG + 1):
                        pool.wait_ge(put_y, 16 * (i - LAG))
                if not (peeled and i + 1 >= TILES):
                    if not (peeled and i + 1 < YR):
                        pool.wait_ge(x_ps, i + 2 - YR)
                    copy_gi(i + 1, (r + 1) % YR)
                if has_add:
                    nc.gpsimd.indirect_dma_start(
                        out=result, out_offset=bass.IndirectOffsetOnAxis(ap=si[:, (r - LAG) % YR, :], axis=0),
                        in_=y[:, (r - LAG) % YR, :], in_offset=None, compute_op=ALU.add).then_inc(put_y, 16)

            pool.wait_ge(routed, 1)
            for s in range(2):
                for j in range(2):
                    pool.wait_ge(st_xn[s][j], 16 * NT // 4)
            pool.wait_ge(st_x1, 16 * (NT + 1))
            copy_gi(0, 0)
            first, body = 2 * YR, (TILES - 1 - 2 * YR) // YR
            for i in range(first):
                row_step(i, i % YR)
            with pool.Fori(2, 2 + body) as b:
                for r in range(YR):
                    row_step(YR * b + r, r)
            for i in range(first + YR * body, TILES + LAG):
                row_step(i, i % YR)

        @block.tensor
        def _(pe):
            regs = [pe.alloc_register(f"pe_window{k}") for k in range(RING)]
            pe.wait_ge(ident_ok, 1)

            def edge_columns(k):
                for j in range(CJ):
                    m = pe.transpose(ps_edge[:, j * P:(j + 1) * P], edge_f[:, k, j, :], ident[:, :])
                m.then_inc(edges_ps, 1)

            def transposes(u, s):
                for j in range(2):
                    pe.wait_ge(xn_ok, 2 * u + j + 1)
                    for k in range(KT):
                        m = pe.transpose(psT[s][k // 2][:, (k % 2) * 2 * P + j * P:(k % 2) * 2 * P + (j + 1) * P],
                                         xn[:, s, j, k * P:(k + 1) * P], ident[:, :])
                m.then_inc(xT_ps, 1)

            def products(u, s, first):
                pe.wait_ge(xT_lo, u + 1)
                three = [(0, 0), (1, 0), (0, 1)]
                for j in range(2):
                    if not first:
                        pe.wait_ge(row_ok, 2 * u + j - 1)
                    n = 0
                    for k in range(KT):
                        for a, b in three:
                            m = pe.matmul(ps_h[j][:, :], xT[:, s, a, k, j * P:(j + 1) * P], Wb[:, b, k, :],
                                          start=(n == 0), stop=(n == 3 * KT - 1))
                            n += 1
                    m.then_inc(h_ps, 1)
                if first:
                    pe.wait_ge(wa_ok, 1)
                else:
                    pe.wait_ge(d_ok, u)
                n = 0
                for k in range(KT):
                    for a, b in three:
                        m = pe.matmul(ps_d[:, 0:2 * P], wa_rep[:, b, k, :], xT[:, s, a, k, :],
                                      start=(n == 0), stop=(n == 3 * KT - 1))
                        n += 1
                m.then_inc(d_ps, 1)

            transposes(0, 0)
            transposes(1, 1)
            pe.wait_ge(W_ok, 1)
            products(0, 0, True)
            pe.wait_ge(edges_f, 1)
            edge_columns(0)
            transposes(2, 0)
            products(1, 1, False)
            pe.wait_ge(edges_ok, 1)
            edge_columns(1)
            with pe.Fori(1, NT // 4 - 1) as i:
                transposes(2 * i + 1, 1)
                products(2 * i, 0, False)
                transposes(2 * i + 2, 0)
                products(2 * i + 1, 1, False)
            transposes(NT // 2 - 1, 1)
            products(NT // 2 - 2, 0, False)
            pe.wait_ge(mm_ok, 1)
            for k in range(2):
                for j in range(CJ):
                    m = pe.transpose(psT[0][k][0:1, j * P:(j + 1) * P], ch_mm[:, k, j:j + 1], ident[:, :])
            m.then_inc(mm_ps, 1)
            products(NT // 2 - 1, 1, False)

            def sums(q, w, r):
                for c in range(GC):
                    for a in range(2):
                        m = pe.matmul(ps_agg[q][:, a, 0:HALF], S[:, w, c, :], rows[:, r, c, a * HALF:(a + 1) * HALF],
                                      start=(c == 0), stop=(c == GC - 1))
                return m

            def group(g, r, i):
                pe.wait_ge(S_ok, g + 1)
                if not (isinstance(g, int) and g < 2):
                    pe.wait_ge(added, g - 1)
                sums(r % 2, r % SR, r).then_inc(agg_ok, 1)
                word = pe.snap(regs[r])
                extra = pe.snap(extra_in(word))
                with pe.If(extra > 0):
                    before = pe.snap(before_in(word))
                    with pe.Fori(0, extra) as n:
                        pe.wait_ge(xS_ok, before + n + 2)
                        pe.wait_ge(xadded, before + n + 1)
                        sums(2, SR, r).then_inc(xagg_ok, 1)

            pe.wait_ge(row_ok, NT)
            pe.wait_ge(s_ok, NT // 2)
            pe.wait_ge(d_ok, NT // 2)
            pe.wait_ge(win_ok, 2)
            window_words(pe, regs, 0)
            for r in range(RING):
                group(r, r, 0)
            with pe.Fori(1, NG // RING) as i:
                window_words(pe, regs, i)
                for r in range(RING):
                    group(RING * i + r, r, i)

            def normal_T(u, s):
                for j in range(2):
                    pe.wait_ge(xn2_ok, 2 * u + j + 1)
                    if j == 0 and not (isinstance(u, int) and u < 2):
                        pe.wait_ge(xnT_ok, u - 1)
                    for k in range(KT):
                        m = pe.transpose(psT[s][j][:, k * P:(k + 1) * P], xn[:, s, j, k * P:(k + 1) * P], ident[:, :])
                m.then_inc(xnT_ps, 1)

            def logits(u, s):
                pe.wait_ge(xnT_ok, u + 1)
                if not (isinstance(u, int) and u < 2):
                    pe.wait_ge(logT_ok, u - 1)
                for k in range(KT):
                    m = pe.matmul(ps_logT[s][0:NX, 0:2 * P], Wg_sb[:, k, :],
                                  xnT[:, s, k, :, :].rearrange("p j n -> p (j n)"), start=(k == 0), stop=(k == KT - 1))
                m.then_inc(logT_ps, 1)

            def logits_of_nodes(u, s):
                pe.wait_ge(logT_ok, u + 1)
                for j in range(2):
                    m = pe.matmul(ps_logit[:, bass.ds((2 * u + j) * NX, NX)], logT[:, s, j * P:(j + 1) * P],
                                  ident[0:NX, 0:NX], start=True, stop=True)
                m.then_inc(logit_ps, 1)

            def route_step(u, s):
                peeled = isinstance(u, int)
                if not (peeled and u >= NT // 2):
                    normal_T(u, s)
                if not (peeled and (u < 1 or u > NT // 2)):
                    logits(u - 1, 1 - s)
                if not (peeled and u < 2):
                    logits_of_nodes(u - 2, s)

            pe.wait_ge(acc_ok, 1)
            pe.wait_ge(ld_late, 16 * 2)
            over_steps(pe, route_step)
            pe.wait_ge(cnt_ok, 1)
            pe.wait_ge(consts_ok, 2)
            pe.matmul(ps_sum[:, 0:NX], below[:, :], per[:, 0, :], start=True, stop=True)
            pe.matmul(ps_sum[:, NX:2 * NX], all_1[:, :], per[:, 0, :], start=True, stop=True).then_inc(cnt_ps, 1)
            pe.wait_ge(hot_ok, 1)
            for v in range(2):
                for t in range(ITEMS):
                    m = pe.matmul(ps_inv[:, v * TILES:(v + 1) * TILES], hot_r[:, t, :], hot_v[:, v, t, :],
                                  start=(t == 0), stop=(t == ITEMS - 1))
            m.then_inc(inv_ps, 1)
            for v in range(3):
                pe.wait_ge(hot_ok, 2 + v)
                for t in range(ITEMS):
                    m = pe.matmul(ps_share[:, 0:TILES], hot_r[:, t, :], hot_p[:, v, t, :],
                                  start=(t == 0 and v == 0), stop=(t == ITEMS - 1 and v == 2))
            m.then_inc(inv_ps, 1)

            def tile_step(i, n, e_mid, e_old):
                s, r, peeled = i % 2, i % YR, isinstance(n, int)
                new, mid, old = parts_of(i) if peeled else (True, True, True)
                three = [(0, 0), (1, 0), (0, 1)]
                if old:
                    pe.wait_ge(gelu_ok, n - 1)
                    if not (peeled and n < 3):
                        pe.wait_ge(hidT_lo, n - 2)
                    for k in range(HF):
                        m = pe.transpose(ps_hT[:, k * P:(k + 1) * P], act_h[:, s, k * P:(k + 1) * P], ident[:, :])
                    m.then_inc(hidT_ps, 1)
                if new:
                    pe.wait_ge(got_x[r], tile_count(n, i))
                    if not (peeled and n < 1):
                        pe.wait_ge(x_lo, n)
                    for k in range(KT):
                        m = pe.transpose(ps_x[:, k * P:(k + 1) * P], xg[:, r, k * P:(k + 1) * P], ident[:, :])
                    m.then_inc(x_ps, 1)
                if mid:
                    e = expert_in(pe, e_mid)
                    pe.wait_ge(x_lo, n)
                    if not (peeled and n < 3):
                        pe.wait_ge(hid_ok, n - 2)
                    for k in range(KT):
                        for a, b in three:
                            m = pe.matmul(ps_hid[1 - s][:, 0:F], xgT[:, 1 - s, a, k * P:(k + 1) * P],
                                          (W1_hi, W1_lo)[b][:, bass.ds(e, 1), k, :].rearrange("p e f -> p (e f)"),
                                          start=(k == 0 and (a, b) == (0, 0)), stop=(k == KT - 1 and b == 1))
                    m.then_inc(hid_ps, 1)
                if old:
                    e = expert_in(pe, e_old)
                    pe.wait_ge(hidT_lo, n - 1)
                    if not (peeled and n < 4):
                        pe.wait_ge(yb_ok, n - 3)
                    for k in range(HF):
                        for a, b in three:
                            m = pe.matmul(ps_y[s][:, :], hidT[:, s, a, k * P:(k + 1) * P],
                                          (W2_hi, W2_lo)[b][:, bass.ds(e, 1), k, :].rearrange("p e d -> p (e d)"),
                                          start=(k == 0 and (a, b) == (0, 0)), stop=(k == HF - 1 and b == 1))
                    m.then_inc(y_ps, 1)

            def tile_count(n, i):
                return 16 * (n // YR + 1) if isinstance(n, int) else 4 * (n - i % YR) + 16

            pe.wait_ge(routed, 1)
            pe.wait_ge(W1_lo_ok, NX)
            pe.wait_ge(W2_lo_ok, NX)
            pe_experts = [pe.alloc_register(f"pe_expert{k}") for k in range(5)]
            over_tiles(pe, pe_experts, tile_step)

        @block.scalar
        def _(act):
            regs = [act.alloc_register(f"act_window{k}") for k in range(RING + 1)]
            def std_of(u, s):
                act.wait_ge(stats_ok, u + 1)
                nc.scalar.activation(std[:, s, :], mv[:, s, :, 1], ACT.Sqrt, bias=eps[:, :]).then_inc(std_ok, 1)

            def high_xT(u, s):
                act.wait_ge(xT_ps, u + 1)
                if not (isinstance(u, int) and u < 2):
                    act.wait_ge(d_ps, u - 1)
                for b in range(2):
                    m = nc.scalar.activation(xT[:, s, 0, 2 * b:2 * b + 2, :].rearrange("p k n -> p (k n)"),
                                             psT[s][b][:, :], ACT.Copy)
                m.then_inc(xT_hi, 1)

            def s_dst(u):
                act.wait_ge(d_ps, u + 1)
                nc.scalar.activation(sdst_b[:, bass.ds(2 * P * u, 2 * P)], ps_d[:, 0:2 * P], ACT.Copy).then_inc(d_ok, 1)

            std_of(0, 0)
            act.wait_ge(ld_W, 16)
            nc.scalar.activation(Wb[:, 0, :, :], Wf[:, :, :], ACT.Copy).then_inc(W_hi, 1)
            high_xT(0, 0)
            std_of(1, 1)

            def step(u, s, i, ahead):
                if ahead:
                    high_xT(u + 1, 1 - s)
                    if ahead > 1:
                        std_of(u + 2, s)
                s_dst(u)

            step(0, 0, 0, 2)
            with act.Fori(0, NT // 4 - 2) as i:
                step(2 * i + 1, 1, i, 2)
                step(2 * i + 2, 0, i + 1, 2)
            step(NT // 2 - 3, 1, NT // 4 - 2, 2)
            step(NT // 2 - 2, 0, NT // 4 - 1, 1)
            step(NT // 2 - 1, 1, NT // 4 - 1, 0)

            def weights(q, r, tile):
                for k, (e, scale) in enumerate(((E1, 1.0), (E2, SLOPE))):
                    for c in range(GC):
                        bias = rows[:, r, c, S_SRC + k:S_SRC + k + 1]
                        m = nc.scalar.activation(e[:, q, c, :], sdst_b[:, bass.ds(tile * P, P)], ACT.Exp,
                                                 bias=bias, scale=scale)
                return m

            def extras(r):
                word = act.snap(regs[r])
                extra = act.snap(extra_in(word))
                with act.If(extra > 0):
                    tile, before = act.snap(tile_in(word)), act.snap(before_in(word))
                    with act.Fori(0, extra) as n:
                        act.wait_ge(xmax_ok, before + n + 1)
                        weights(2, (r - 1) % RING, tile_of(tile + n + 1)).then_inc(xexp_ok, 1)

            def group(r, i):
                tile = act.snap(tile_in(act.snap(regs[r + 1])))
                act.wait_ge(max_ok[r % 2], RING // 2 * i + r // 2 + 1)
                act.wait_ge(got[r], 16 * GC * (i + 1))
                weights(r % 2, r, tile).then_inc(exp_ok, 1)
                extras(r)

            act.wait_ge(d_ok, NT // 2)
            act.wait_ge(win_ok, 2)
            act.wait_ge(wa_ok, 1)
            nc.scalar.activation(spare[:, 2:3], cst2[:, 0:1], ACT.Exp)
            with act.Fori(0, NG // RING) as i:
                window_words(act, regs, i, 1)
                for r in range(RING):
                    group(r, i)
            extras(RING)

            def std2_of(u, s):
                act.wait_ge(aggr2_ok, u + 1)
                nc.scalar.activation(std[:, s, :], mv[:, s, :, 1], ACT.Sqrt, bias=eps[:, :]).then_inc(std2_ok, 1)

            def xn_of(u, s):
                act.wait_ge(rstd2_ok, 2 * u + 2)
                for j in range(2):
                    if not (isinstance(u, int) and u < 2):
                        if j == 0:
                            act.wait_ge(xnT_ps, u - 1)
                        act.wait_ge(st_xn[s][j], 16 * (u // 2) if isinstance(u, int) else u * 8 - 8 * s)
                    nc.scalar.activation(halves(xn[:, s, j, :]), features(2 * u + j), ACT.Identity,
                                         bias=shift[:, s, j:j + 1], scale=rstd[:, s, j:j + 1]).then_inc(xn2_ok, 1)

            def xnT_of(u, s):
                act.wait_ge(xnT_ps, u + 1)
                if not (isinstance(u, int) and u < 2):
                    act.wait_ge(logT_ps, u - 1)
                for j in range(2):
                    m = nc.scalar.activation(xnT[:, s, :, j, :], psT[s][j].rearrange("p (k n) -> p k n", k=KT), ACT.Copy)
                m.then_inc(xnT_ok, 1)

            def logT_of(u, s):
                act.wait_ge(logT_ps, u + 1)
                if not (isinstance(u, int) and u < 2):
                    act.wait_ge(logit_ps, u - 1)
                nc.scalar.activation(logT[:, s, :], ps_logT[s][0:NX, 0:2 * P], ACT.Identity, bias=bg_c[:, :])\
                    .then_inc(logT_ok, 1)

            def high_W2(e):
                nc.scalar.activation(W2_hi[:, bass.ds(e, 1), :, :].rearrange("p e k d -> p (e k d)"),
                                     W2_e[:, bass.ds(e, 1), :, :].rearrange("p e k d -> p (e k d)"),
                                     ACT.Copy).then_inc(W2_hi_ok, 1)

            def route_step(u, s):
                peeled = isinstance(u, int)
                if not (peeled and u >= NT // 2 - 1):
                    std2_of(u + 1, 1 - s)
                if not (peeled and u >= NT // 2):
                    xn_of(u, s)
                if not (peeled and (u < 1 or u > NT // 2)):
                    xnT_of(u - 1, 1 - s)
                if not (peeled and u < 2):
                    logT_of(u - 2, s)
                if not (peeled and not 4 <= u < NT // 2 - 2):
                    high_W2(u - 4)

            act.wait_ge(acc_ok, 1)
            act.wait_ge(ld_late, 16 * 2)
            act.wait_ge(ld_W1, 16 * NX)
            act.wait_ge(ld_W2, 16 * NX)
            std2_of(0, 0)
            over_steps(act, route_step)
            n_early = NT // 2 - 6
            act.wait_ge(shift_ok, 1)
            nc.scalar.activation(pr[:, :, :], score[:, :, :], ACT.Exp).then_inc(exp2_ok, 1)

            for e in range(n_early, NX):
                high_W2(e)
            act.wait_ge(xn2_ok, NT)
            act.wait_ge(st_x1, 16 * (NT + 1))
            for e in range(NX):
                nc.scalar.activation(W1_hi[:, e, :, :], W1_e[:, e, :, :], ACT.Copy).then_inc(W1_hi_ok, 1)

            def share_of(m, r):
                if not (isinstance(m, int) and m < YR):
                    act.wait_ge(put_y, 16 * (m + 1 - YR))
                act.wait_ge(yb_ok, m + 1)
                nc.scalar.activation(y[:, r, :], y_b[:, r % 2, :], ACT.Copy, scale=share[:, bass.ds(m, 1)])\
                    .then_inc(y_ok, 1)

            def tile_step(i, n, _, __):
                s, peeled = i % 2, isinstance(n, int)
                new, mid, old = parts_of(i) if peeled else (True, True, True)
                if old:
                    act.wait_ge(hidT_ps, n - 1)
                    if not (peeled and n < 4):
                        act.wait_ge(y_ps, n - 3)
                    nc.scalar.activation(hidT[:, s, 0, :], ps_hT[:, 0:F], ACT.Copy).then_inc(hidT_hi, 1)
                if new:
                    act.wait_ge(x_ps, n + 1)
                    if not (peeled and n < 2):
                        act.wait_ge(hid_ps, n - 1)
                    nc.scalar.activation(xgT[:, s, 0, :], ps_x[:, :], ACT.Copy).then_inc(x_hi, 1)
                if mid:
                    act.wait_ge(hid_ok, n)
                    if not (peeled and n < 3):
                        act.wait_ge(hidT_ps, n - 2)
                    nc.scalar.activation(act_h[:, 1 - s, :], hid[:, 1 - s, :], ACT.Gelu_apprx_tanh).then_inc(gelu_ok, 1)
                if not (peeled and n < 3):
                    share_of(n - 3, (i - 3) % YR)

            act.wait_ge(routed, 1)
            act.wait_ge(share_ok, 1)
            over_tiles(act, None, tile_step)
            share_of(TILES - 1, (TILES - 1) % YR)

            act.wait_ge(put_y, 16 * TILES)
            act.dma_start(out[N // 2:N, :], result[N // 2:N, :]).then_inc(st_out, 16)
            act.wait_ge(st_out, 32)

        @block.vector
        def _(dve):
            regs = [dve.alloc_register(f"dve_window{k}") for k in range(RING + BACK)]
            n_dv = [0]

            def link(ins):
                n_dv[0] += 1
                ins.then_inc(dv, 1)
                dve.wait_ge(dv, n_dv[0])

            nc.vector.memset(zero_r[:, :], 0.0)
            for k, count_ in enumerate((max_ok[0], max_ok[1], xmax_ok, xS_ok)):
                nc.vector.memset(start[:, k:k + 1], 0.0).then_inc(count_, 1)
            link(nc.vector.memset(eps[:, :], EPS))

            def normal(u, s):
                for j in range(2):
                    dve.wait_ge(ld_x[s][j], 16 * (u // 2 + 1) if isinstance(u, int) else u * 8 + 16 - 8 * s)
                    nc.vector.bn_stats(stats[:, s, j, :], x_in[:, s, j, :]).then_inc(rstd_ok, 1)
                dve.wait_ge(rstd_ok, 3 * u + 2)
                nc.vector.memset(spare[:, s:s + 1], 0.0)
                for j in range(2):
                    m = nc.vector.bn_aggr(mv[:, s, j, :], stats[:, s, j, :])
                m.then_inc(stats_ok, 1)
                dve.wait_ge(std_ok, u + 1)
                nc.vector.reciprocal(rstd[:, s, :], std[:, s, :]).then_inc(rstd_ok, 1)
                dve.wait_ge(rstd_ok, 3 * u + 3)
                for j in range(2):
                    if not (isinstance(u, int) and u < 2):
                        dve.wait_ge(xT_ps, u - 1)
                    nc.vector.tensor_scalar(xn[:, s, j, :], x_in[:, s, j, :], mv[:, s, j, 0:1], rstd[:, s, j:j + 1],
                                            ALU.subtract, ALU.mult).then_inc(xn_ok, 1)

            def low_xT(u, s):
                dve.wait_ge(xT_hi, u + 1)
                for b in range(2):
                    m = nc.vector.tensor_tensor(xT[:, s, 1, 2 * b:2 * b + 2, :].rearrange("p k n -> p (k n)"),
                                                psT[s][b][:, :],
                                                xT[:, s, 0, 2 * b:2 * b + 2, :].rearrange("p k n -> p (k n)").bitcast(F32),
                                                ALU.subtract)
                m.then_inc(xT_lo, 1)

            def node_rows(u, s, i):
                for j in range(2):
                    dve.wait_ge(h_ps, 2 * u + j + 1)
                    if not (isinstance(u, int) and u < 2):
                        dve.wait_ge(st_row[s][j], 16 * i)
                    nc.vector.tensor_tensor(halves(rows[:, s, j, 0:2 * HALF])[:, :, 0:HD], halves(ps_h[j]),
                                            halves(bw_b[:, :]), ALU.add).then_inc(row_ok, 1)
                for j in range(2):
                    dve.wait_ge(row_ok, 2 * u + j + 1)
                    m = nc.vector.tensor_tensor_reduce(halves(junk[:, j, :]), halves(rows[:, s, j, 0:2 * HALF])[:, :, 0:HD],
                                                       halves(a_b[:, 1, :]), 1.0, 0.0, ALU.mult, ALU.add,
                                                       s_dot[:, s, j:j + 1])
                m.then_inc(dot_ok, 1)
                dve.wait_ge(dot_ok, u + 1)
                for k, scale in enumerate((1.0, SLOPE)):
                    m = nc.vector.tensor_scalar(rows[:, s, :, S_SRC + k:S_SRC + k + 1],
                                                s_dot[:, s, :].unsqueeze(2), scale, cst2[:, k:k + 1], ALU.mult, ALU.add)
                m.then_inc(s_ok, 1)

            normal(0, 0)
            normal(1, 1)
            dve.wait_ge(W_hi, 1)
            nc.vector.tensor_tensor(Wb[:, 1, :, :], Wf[:, :, :], Wb[:, 0, :, :].bitcast(F32), ALU.subtract).then_inc(W_ok, 1)
            low_xT(0, 0)
            dve.wait_ge(ld_par, 48)
            for k in range(KT):
                link(nc.vector.tensor_tensor_reduce(junk[:, 0, :], Wf[:, k, :], a_b[:, 0, :], 1.0, 0.0, ALU.mult,
                                                    ALU.add, wa[:, k:k + 1]))
            link(nc.vector.tensor_copy(wa_hl[:, 0, :], wa[:, :]))
            link(nc.vector.tensor_tensor(wa_hl[:, 1, :], wa[:, :], wa_hl[:, 0, :].bitcast(F32), ALU.subtract))
            for a in range(2):
                m = nc.vector.tensor_copy(wa_rep[:, a, :, :],
                                          wa_hl[:, a, :].bitcast(F32).unsqueeze(2).to_broadcast([P, KT, P]))
            m.then_inc(wa_ok, 1)
            link(nc.vector.tensor_tensor_reduce(junk[:, 0, :], bw_b[:, :], a_b[:, 0, :], 1.0, 0.0, ALU.mult,
                                                ALU.add, cst[:, :]))
            link(nc.vector.tensor_tensor(cst2[:, 0:1], cst[:, :], ba_b[:, :], ALU.add))
            link(nc.vector.tensor_scalar(cst2[:, 1:2], cst2[:, 0:1], SLOPE, None, ALU.mult))
            dve.wait_ge(ld_edge, 16 * 6)
            nc.vector.tensor_copy(edge_f[:, :, :, :], edge_i[:, :, :, :]).then_inc(edges_f, 1)
            dve.wait_ge(pads, 2)

            def step(u, s, i, ahead):
                if ahead:
                    low_xT(u + 1, 1 - s)
                    if ahead > 1:
                        normal(u + 2, s)
                node_rows(u, s, i)

            step(0, 0, 0, 2)
            dve.wait_ge(edges_f, 1)
            nc.vector.tensor_reduce(ch_mm[:, 0, :], edge_f[:, 1, :, :], AX.X, ALU.min)
            nc.vector.tensor_reduce(ch_mm[:, 1, :], edge_f[:, 1, :, :], AX.X, ALU.max).then_inc(mm_ok, 1)
            dve.wait_ge(edges_ps, 1)
            nc.vector.tensor_copy(srcT[:, :], ps_edge[:, 0:NG * GC]).then_inc(edges_ok, 1)
            step(1, 1, 0, 2)
            dve.wait_ge(edges_ps, 2)
            nc.vector.tensor_copy(dstT[:, :], ps_edge[:, 0:NG * GC]).then_inc(edges_ok, 1)
            step(2, 0, 1, 2)
            with dve.Fori(1, NT // 4 - 2) as i:
                step(2 * i + 1, 1, i, 2)
                step(2 * i + 2, 0, i + 1, 2)
            step(NT // 2 - 3, 1, NT // 4 - 2, 2)
            step(NT // 2 - 2, 0, NT // 4 - 1, 1)
            dve.wait_ge(mm_ps, 1)
            for k in range(2):
                link(nc.vector.tensor_reduce(win_f[:, k, :],
                                             psT[0][k][0:1, 0:NG * GC].rearrange("o (g c) -> o g c", c=GC),
                                             AX.X, (ALU.min, ALU.max)[k]))
            link(nc.vector.tensor_scalar(win_i[:, :, :], win_f[:, :, :], float(N - 1), None, ALU.min))
            link(nc.vector.tensor_single_scalar(win_i[:, :, :], win_i[:, :, :], 7, ALU.arith_shift_right))
            link(nc.vector.tensor_tensor(win_n[:, 0, :], win_i[:, 1, :], win_i[:, 0, :], ALU.subtract))
            link(nc.vector.tensor_tensor_scan(win_n[:, 1, :], win_n[:, 0, :], zero_r[:, :], 0.0, ALU.add, ALU.add))
            link(nc.vector.memset(win_w[:, :, :], 0.0))
            nc.vector.scalar_tensor_tensor(out=win_w[:, 0, BACK:NG + BACK], in0=win_n[:, 0, :], scalar=32.0,
                                           in1=win_i[:, 0, :], op0=ALU.mult, op1=ALU.add)
            link(nc.vector.tensor_copy(win_w[:, 1, BACK + 1:NG + BACK], win_n[:, 1, 0:NG - 1]))
            nc.vector.scalar_tensor_tensor(out=window[:, :], in0=win_w[:, 1, :], scalar=1024.0, in1=win_w[:, 0, :],
                                           op0=ALU.mult, op1=ALU.add).then_inc(win_ok, 2)

            step(NT // 2 - 1, 1, NT // 4 - 1, 0)

            def largest(q):
                return nc.vector.scalar_tensor_tensor(out=Wt[:, q, :, :], in0=E1[:, q, :, :], scalar=FINITE,
                                                      in1=E2[:, q, :, :], op0=ALU.min, op1=ALU.max)

            def masked(q, w, g, tile):
                for c in range(GC):
                    m = nc.vector.scalar_tensor_tensor(
                        out=S[:, w, c, :], in0=node_id[:, bass.ds(tile * P, P)], scalar=dstT[:, bass.ds(GC * g + c, 1)],
                        in1=Wt[:, q, c, :], op0=ALU.is_equal, op1=ALU.mult)
                return m

            def add(q, tile, count):
                a = acc[:, bass.ds(tile, 1), :, :].rearrange("p t a d -> p (t a) d")
                nc.vector.tensor_tensor(a, a, ps_agg[q][:, :, 0:HALF], ALU.add).then_inc(count, 1)

            def settle(sem_, at):
                dve.wait_ge(sem_, at)
                nc.vector.memset(spare[:, 0:1], 0.0)

            def weigh_extra(g, tile, at):
                dve.wait_ge(xS_ok, at)
                dve.wait_ge(xexp_ok, at)
                largest(2).then_inc(xmax_ok, 1)
                dve.wait_ge(xmax_ok, at + 1)
                masked(2, SR, g, tile).then_inc(xS_ok, 1)

            def add_extra(n_added, tile, at):
                if n_added is not None:
                    dve.wait_ge(added, n_added)
                dve.wait_ge(xagg_ok, at + 1)
                add(2, tile, xadded)
                settle(xadded, at + 1)

            last_tile = dve.alloc_register("last_extra_tile")
            dve.reg_mov(last_tile, 0)

            def extras(g, n_added, word):
                extra = dve.snap(extra_in(word))
                with dve.If(extra > 0):
                    tile, before = dve.snap(tile_in(word)), dve.snap(before_in(word))
                    add_extra(n_added, tile_of(dve.snap(last_tile)), before)
                    weigh_extra(g, tile_of(tile + 1), before + 1)
                    with dve.If(extra > 1):
                        with dve.Fori(1, extra) as n:
                            add_extra(n_added, tile_of(tile + n), before + n)
                            weigh_extra(g, tile_of(tile + n + 1), before + n + 1)
                    dve.reg_mov(last_tile, tile + extra)

            def step_of_group(g, r, i, first=False, words=None):
                words_at = r + BACK
                word = lambda back: dve.snap(regs[words_at - back])
                r %= RING
                if words is None:
                    dve.wait_ge(exp_ok, g + 1)
                    if not (first and r < 2):
                        dve.wait_ge(S_ok, g - 1)
                    largest(r % 2).then_inc(max_ok[r % 2], 1)
                if not (first and r < 3):
                    tile = dve.snap(tile_in(word(3)))
                    if not (first and r < 4):
                        dve.wait_ge(added, g - 3)
                    dve.wait_ge(agg_ok, g - 2)
                    add((r - 3) % 2, tile, added)
                if words is None or words < 1:
                    if not (first and r < 1):
                        tile = dve.snap(tile_in(word(1)))
                        dve.wait_ge(max_ok[(r - 1) % 2], RING // 2 * i + (r + 1) // 2 + 1)
                        masked((r - 1) % 2, (r - 1) % SR, g - 1, tile).then_inc(S_ok, 1)
                if (words is None or words < 1) and not (first and r < 1):
                    extras(g - 1, None if first and r < 3 else g - 2, word(1))

            dve.wait_ge(row_ok, NT)
            nc.vector.memset(ps_agg[2][:, :, 0:HALF], 0.0).then_inc(xagg_ok, 1)
            dve.wait_ge(win_ok, 2)
            dve.wait_ge(ids_ok, 1)
            dve.wait_ge(edges_ok, 2)
            window_words(dve, regs, 0, BACK)
            for r in range(RING):
                step_of_group(r, r, 0, first=True)
            with dve.Fori(1, NG // RING) as i:
                window_words(dve, regs, i, BACK)
                for r in range(RING):
                    step_of_group(RING * i + r, r, i)
            for k in range(BACK):
                step_of_group(NG + k, RING + k, NG // RING, words=k)
            dve.wait_ge(added, NG)
            last_word = dve.snap(regs[RING + BACK - 1])
            add_extra(None, tile_of(dve.snap(last_tile)), before_in(last_word) + extra_in(last_word))
            dve.wait_ge(agg_ok, NG)
            den = acc[:, :, 0, ONE]
            link(nc.vector.tensor_single_scalar(rden[:, :], den, 0.0, ALU.is_equal))
            link(nc.vector.tensor_tensor(rden[:, :], rden[:, :], den, ALU.add))
            link(nc.vector.reciprocal(rden[:, :], rden[:, :]))
            nc.vector.memset(spare[:, 0:1], 0.0).then_inc(acc_ok, 1)

            def x1_of(u, s):
                for j in range(2):
                    a = features(2 * u + j)
                    dve.wait_ge(ld_x2[s][j], 16 * (u // 2 + 1) if isinstance(u, int) else u * 8 + 16 - 8 * s)
                    nc.vector.scalar_tensor_tensor(out=a, in0=a, scalar=rden[:, bass.ds(2 * u + j, 1)],
                                                   in1=halves(x_in[:, s, j, :]), op0=ALU.mult, op1=ALU.add).then_inc(x1_ok, 1)
                dve.wait_ge(x1_ok, 2 * u + 2)
                nc.vector.memset(spare[:, 0:1], 0.0)
                for j in range(2):
                    a = features(2 * u + j)
                    m = nc.vector.bn_stats(stats[:, s, j, :], a)
                m.then_inc(stats2_ok, 1)
                if not (isinstance(u, int) and u < 2):
                    dve.wait_ge(rstd2_ok, 2 * u - 2)
                dve.wait_ge(stats2_ok, u + 1)
                nc.vector.memset(spare[:, 1:2], 0.0)
                for j in range(2):
                    m = nc.vector.bn_aggr(mv[:, s, j, :], stats[:, s, j, :])
                m.then_inc(aggr2_ok, 1)

            def normal2(u, s):
                dve.wait_ge(std2_ok, u + 1)
                if not (isinstance(u, int) and u < 2):
                    dve.wait_ge(xn2_ok, 2 * u - 2)
                nc.vector.reciprocal(rstd[:, s, :], std[:, s, :]).then_inc(rstd2_ok, 1)
                dve.wait_ge(rstd2_ok, 2 * u + 1)
                nc.vector.scalar_tensor_tensor(out=shift[:, s, :], in0=mv[:, s, :, 0], scalar=-1.0, in1=rstd[:, s, :],
                                               op0=ALU.mult, op1=ALU.mult).then_inc(rstd2_ok, 1)

            x1_of(0, 0)

            def two_steps(i):
                x1_of(2 * i + 1, 1)
                normal2(2 * i, 0)
                x1_of(2 * i + 2, 0)
                normal2(2 * i + 1, 1)

            two_steps(0)
            with dve.Fori(1, NT // 4 - 1) as i:
                two_steps(i)
            x1_of(NT // 2 - 1, 1)
            normal2(NT // 2 - 2, 0)
            normal2(NT // 2 - 1, 1)

            V = nc.vector
            dve.wait_ge(consts_ok, 2)
            V.tensor_copy(part1[:, :], part_i[:, :])
            V.tensor_copy(count_b[:, :], count_i[:, :])
            V.tensor_copy(beyond[:, :], beyond_i[:, :])
            link(V.tensor_copy(count[:, :], count_i[:, :]))

            def bc_t(ap):
                return ap.unsqueeze(2).to_broadcast([P, NT, NX])

            dve.wait_ge(logit_ps, NT // 2)
            logit = ps_logit[:, 0:NT * NX].rearrange("p (t e) -> p t e", e=NX)
            link(V.tensor_reduce(red[:, :], logit, AX.X, ALU.max))
            V.tensor_tensor(score[:, :, :], logit, bc_t(red[:, :]), ALU.subtract).then_inc(shift_ok, 1)
            dve.wait_ge(exp2_ok, 1)
            link(V.tensor_reduce(red[:, :], pr[:, :, :], AX.X, ALU.add))
            link(V.reciprocal(red[:, :], red[:, :]))
            link(V.tensor_tensor(pr[:, :, :], pr[:, :, :], bc_t(red[:, :]), ALU.mult))
            expert_id = count[:, 0:NX].unsqueeze(1).to_broadcast([P, NT, NX])
            for c in range(2):
                link(V.tensor_reduce(prob[:, c, :], pr[:, :, :], AX.X, ALU.max))
                link(V.tensor_tensor(pick[:, :, :], pr[:, :, :], bc_t(prob[:, c, :]), ALU.is_equal))
                link(V.scalar_tensor_tensor(out=pick[:, :, :], in0=pick[:, :, :], scalar=-float(NX), in1=expert_id,
                                            op0=ALU.mult, op1=ALU.add))
                link(V.tensor_reduce(red[:, :], pick[:, :, :], AX.X, ALU.min))
                link(V.tensor_single_scalar(red[:, :], red[:, :], float(NX), ALU.add))
                link(V.tensor_tensor(pick[:, :, :], expert_id, bc_t(red[:, :]), ALU.is_equal))
                link(V.tensor_tensor(choice[:, :, c, :], pick[:, :, :].rearrange("p t e -> p e t"),
                                     valid[:, c, :].unsqueeze(1).to_broadcast([P, NX, NT]), ALU.mult))
                if c == 0:
                    link(V.scalar_tensor_tensor(out=pr[:, :, :], in0=pick[:, :, :], scalar=-2.0, in1=pr[:, :, :],
                                                op0=ALU.mult, op1=ALU.add))
            flat = choice[:, :, :, :].rearrange("p e c t -> p (e c t)")
            by_item = choice[:, :, :, :].rearrange("p e c t -> p e (c t)")
            V.tensor_reduce(per[:, 0, :], by_item, AX.X, ALU.add).then_inc(cnt_ok, 1)
            link(V.tensor_tensor_scan(rank[:, :, :].rearrange("p e i -> p (e i)"), flat, zeros[:, :], 0.0,
                                      ALU.add, ALU.add))
            dve.wait_ge(cnt_ok, 1)
            link(V.tensor_tensor(per[:, 1, :], rank[:, :, ITEMS - 1], per[:, 0, :], ALU.subtract))
            dve.wait_ge(cnt_ps, 1)
            link(V.tensor_single_scalar(per_i[:, :], ps_sum[:, NX:2 * NX], float(P - 1), ALU.add))
            link(V.tensor_single_scalar(per_i[:, :], per_i[:, :], P.bit_length() - 1, ALU.arith_shift_right))
            link(V.tensor_copy(per[:, 2, :], per_i[:, :]))
            link(V.tensor_tensor_scan(per[:, 3, :], per[:, 2, :], zeros[:, 0:NX], 0.0, ALU.add, ALU.add))
            link(V.tensor_tensor(per[:, 5, :], per[:, 3, :], per[:, 2, :], ALU.subtract))
            link(V.scalar_tensor_tensor(out=per[:, 4, :], in0=per[:, 5, :], scalar=float(P), in1=ps_sum[:, 0:NX],
                                        op0=ALU.mult, op1=ALU.add))
            link(V.scalar_tensor_tensor(out=per[:, 6, :], in0=per[:, 4, :], scalar=-1.0, in1=per[:, 1, :],
                                        op0=ALU.add, op1=ALU.subtract))
            link(V.tensor_tensor(rank[:, :, :], rank[:, :, :], per[:, 6, :].unsqueeze(2).to_broadcast([P, NX, ITEMS]),
                                 ALU.add))
            link(V.tensor_tensor(rank[:, :, :], rank[:, :, :], by_item, ALU.mult))
            link(V.tensor_reduce(pos[:, :], rank[:, :, :].rearrange("p e i -> p i e"), AX.X, ALU.add))
            vflat = valid[:, :, :].rearrange("p c t -> p (c t)")
            link(V.scalar_tensor_tensor(out=pos[:, :], in0=vflat, scalar=float(TILES * P), in1=pos[:, :],
                                        op0=ALU.mult, op1=ALU.add))
            link(V.tensor_single_scalar(pos_i[:, 0, :], pos[:, :], -float(TILES * P), ALU.add))
            link(V.tensor_single_scalar(pos_i[:, 1, :], pos_i[:, 0, :], P.bit_length() - 1, ALU.arith_shift_right))
            link(V.tensor_single_scalar(pos_i[:, 2, :], pos_i[:, 0, :], P - 1, ALU.bitwise_and))
            link(V.tensor_copy(pos_f[:, :, :], pos_i[:, 1:3, :]))
            dve.wait_ge(st_x1, 16 * (NT + 1))
            for s in range(2):
                for j in range(2):
                    dve.wait_ge(st_xn[s][j], 16 * NT // 4)
            dve.wait_ge(xnT_ps, NT // 2)
            tile_id = count_b[:, 0:TILES].unsqueeze(1).to_broadcast([P, ITEMS, TILES])
            V.tensor_tensor(hot_r[:, :, :], pos_f[:, 1, :].unsqueeze(2).to_broadcast([P, ITEMS, P]),
                            count_b[:, :].unsqueeze(1).to_broadcast([P, ITEMS, P]), ALU.is_equal)
            link(V.tensor_tensor(hot_t[:, :, :], pos_f[:, 0, :].unsqueeze(2).to_broadcast([P, ITEMS, TILES]),
                                 tile_id, ALU.is_equal))
            V.tensor_scalar(hot_v[:, 0, :, :], hot_t[:, :, :], part1[:, :], None, ALU.mult)
            V.tensor_tensor(hot_v[:, 1, :, :], hot_t[:, :, :],
                            count[:, 1:ITEMS + 1].unsqueeze(2).to_broadcast([P, ITEMS, TILES]), ALU.mult)\
                .then_inc(hot_ok, 1)
            prob_f = prob[:, :, :].rearrange("p c t -> p (c t)")
            link(V.tensor_copy(prob_b[:, 0, :], prob_f))
            link(V.tensor_tensor(prob_r[:, 0, :], prob_f, prob_b[:, 0, :], ALU.subtract))
            link(V.tensor_copy(prob_b[:, 1, :], prob_r[:, 0, :]))
            link(V.tensor_tensor(prob_r[:, 1, :], prob_r[:, 0, :], prob_b[:, 1, :], ALU.subtract))
            link(V.tensor_copy(prob_b[:, 2, :], prob_r[:, 1, :]))

            def hot_share(v):
                V.tensor_tensor(hot_p[:, v, :, :], hot_t[:, :, :],
                                prob_b[:, v, :].unsqueeze(2).to_broadcast([P, ITEMS, TILES]), ALU.mult)\
                    .then_inc(hot_ok, 1)

            hot_share(0)
            link(V.tensor_tensor(ends[:, :, :], per[0:1, 3, :].unsqueeze(1).to_broadcast([1, TILES, NX]),
                                 count[0:1, 0:TILES].unsqueeze(2).to_broadcast([1, TILES, NX]), ALU.is_le))
            link(V.tensor_reduce(end_n[:, :], ends[:, :, :], AX.X, ALU.add))
            V.tensor_single_scalar(expert_of[:, 2:TILES + 2], end_n[:, :], float(NX - 1), ALU.min)
            dve.wait_ge(inv_ps, 1)
            link(V.tensor_copy(inv[:, 0:2, :].rearrange("p v t -> p (v t)"), ps_inv[:, 0:2 * TILES]))
            link(V.scalar_tensor_tensor(out=inv[:, 2, :], in0=inv[:, 1, :], scalar=float(P), in1=inv[:, 0, :],
                                        op0=ALU.mult, op1=ALU.add))
            link(V.tensor_single_scalar(inv[:, 2, :], inv[:, 2, :], -float(P + 1), ALU.add))
            link(V.tensor_single_scalar(inv[:, 0, :], inv[:, 2, :], float(NTN), ALU.is_ge))
            link(V.scalar_tensor_tensor(out=inv[:, 0, :], in0=inv[:, 0, :], scalar=-float(NTN), in1=inv[:, 2, :],
                                        op0=ALU.mult, op1=ALU.add))
            link(V.tensor_single_scalar(inv[:, 0, :], inv[:, 0, :], 0.0, ALU.max))
            V.tensor_copy(src_row[:, :], inv[:, 0, :])
            link(V.tensor_single_scalar(inv[:, 1, :], inv[:, 2, :], 0.0, ALU.is_lt))
            link(V.tensor_tensor(inv[:, 1, :], inv[:, 1, :], beyond[:, :], ALU.mult))
            link(V.tensor_tensor(dst_row[:, :], inv[:, 0, :], inv[:, 1, :], ALU.add))
            V.memset(spare[:, 0:1], 0.0).then_inc(routed, 1)
            hot_share(1)
            hot_share(2)
            dve.wait_ge(inv_ps, 2)
            V.tensor_copy(share[:, :], ps_share[:, 0:TILES]).then_inc(share_ok, 1)

            def tile_step(i, n, e_mid, e_old):
                s, peeled = i % 2, isinstance(n, int)
                new, mid, old = parts_of(i) if peeled else (True, True, True)
                if old:
                    dve.wait_ge(hidT_hi, n - 1)
                    nc.vector.tensor_tensor(hidT[:, s, 1, :], ps_hT[:, 0:F], hidT[:, s, 0, :].bitcast(F32),
                                            ALU.subtract).then_inc(hidT_lo, 1)
                if new:
                    dve.wait_ge(x_hi, n + 1)
                    nc.vector.tensor_tensor(xgT[:, s, 1, :], ps_x[:, :], xgT[:, s, 0, :].bitcast(F32),
                                            ALU.subtract).then_inc(x_lo, 1)
                if mid:
                    e = expert_in(dve, e_mid)
                    if not (peeled and n < 3):
                        dve.wait_ge(gelu_ok, n - 2)
                    dve.wait_ge(hid_ps, n)
                    nc.vector.tensor_tensor(hid[:, 1 - s, :], ps_hid[1 - s][:, 0:F],
                                            b1_b[:, bass.ds(e, 1), :].rearrange("p e f -> p (e f)"), ALU.add)\
                        .then_inc(hid_ok, 1)
                if old:
                    e = expert_in(dve, e_old)
                    if not (peeled and n < 4):
                        dve.wait_ge(y_ok, n - 3)
                    dve.wait_ge(y_ps, n - 1)
                    nc.vector.tensor_tensor(y_b[:, s, :], ps_y[s][:, :],
                                            b2_b[:, bass.ds(e, 1), :].rearrange("p e d -> p (e d)"), ALU.add)\
                        .then_inc(yb_ok, 1)

            dve.wait_ge(ld_b, 32)
            over_tiles(dve, regs[0:5], tile_step)


_INS = ["x", "src", "dst", "L0_gnn_W", "L0_gnn_b_w", "L0_gnn_a", "L0_gnn_b_a", "L0_ffn_Wg", "L0_ffn_bg",
        "L0_ffn_W1", "L0_ffn_b1", "L0_ffn_W2", "L0_ffn_b2"]


def kernel(**inputs):
    import numpy as _np
    import concourse.bacc as _bacc
    from concourse import mybir as _mybir
    from concourse.bass_utils import run_bass_kernel_spmd as _run

    nc = _bacc.Bacc("TRN2", target_bir_lowering=False, num_devices=1)
    arrays, args = {}, []
    for name in _INS:
        a = _np.ascontiguousarray(inputs[name])
        if a.ndim == 0:
            a = a.reshape(1)
        arrays[f"in_{name}_dram"] = a
        args.append(nc.dram_tensor(f"in_{name}_dram", a.shape, _mybir.dt.from_np(a.dtype), kind="ExternalInput").ap())
    shape = _np.shape(inputs["x"])
    args.append(nc.dram_tensor("out_0_dram", shape, _mybir.dt.float32, kind="ExternalOutput").ap())
    gnn_moe_kernel(nc, *args)
    r = _run(nc, [arrays], core_ids=[0])
    return r.results[0]["out_0_dram"]
```

```python
from contextlib import ExitStack

import concourse.bass as bass
from concourse import mybir

P = 128
F32 = mybir.dt.float32
F32R = mybir.dt.float32r
BF16 = mybir.dt.bfloat16
I32 = mybir.dt.int32
I16 = mybir.dt.int16
ALU = mybir.AluOpType
ACT = mybir.ActivationFunctionType
AX = mybir.AxisListType

EPS = 1e-5
SLOPE = 0.2
FINITE = 3.0e38


def gnn_moe_kernel(nc, x, src, dst, gnn_W, gnn_b_w, gnn_a, gnn_b_a, Wg, bg, W1, b1, W2, b2, out):
    N, D = x.shape
    E = src.shape[0]
    KT = D // P
    NT = -(-N // P)
    LAST = N - (NT - 1) * P
    NTN = NT * P
    CH = -(-E // P)
    CJ = -(-CH // P)
    GC = 2
    RING = 10
    NG = -(-CH // (RING * GC)) * RING
    SR = 5
    BACK = 3
    HD = D // 2
    HALF = HD + 1
    ROW = 2 * HALF + 2
    ONE, S_SRC = HD, 2 * HALF - 1

    NX, F = W1.shape[0], W1.shape[2]
    HF = F // P
    ITEMS = 2 * NT
    TILES = (2 * N + NX * (P - 1)) // P
    ROUNDS = -(-TILES // 4)
    ROUNDS_MIN = -(-(-(-2 * N // P)) // 4)
    YR = 4
    LAG = YR + 2

    table = nc.dram_tensor("node_table", [NTN, ROW], F32).ap()
    xn_table = nc.dram_tensor("xn_table", [NTN, D], F32).ap()
    result = nc.dram_tensor("result", [NTN + P, D], F32).ap()

    with ExitStack() as ctx:
        def sb(name, shape, dt):
            return ctx.enter_context(nc.sbuf_tensor(name, shape, dt))

        def sem(name):
            return ctx.enter_context(nc.semaphore(name))

        rden = sb("rden", [P, NT], F32)
        ident = sb("ident", [P, P], F32)
        stats = sb("stats", [P, 2, 2, 6], F32)
        mv = sb("mv", [P, 2, 2, 2], F32)
        std = sb("std", [P, 2, 2], F32)
        rstd = sb("rstd", [P, 2, 2], F32)
        shift = sb("shift", [P, 2, 2], F32)
        spare = sb("spare", [P, 3], F32)
        start = sb("start", [P, 5], F32)
        eps = sb("eps", [P, 1], F32)

        top = [0]

        def size(shape, dt):
            n = 1
            for k in shape[1:]:
                n *= k
            return -(-n * (2 if dt in (BF16, I16) else 4) // 32) * 32

        def sg(name, shape, dt, into=None):
            top[0] += size(shape, dt)
            return (into or ctx).enter_context(nc.sbuf_tensor(name, shape, dt))

        def reach(name, end):
            if end > top[0]:
                sg(name, [P, (end - top[0]) // 4], F32)
            assert top[0] <= end

        early = ctx.enter_context(ExitStack())
        acc = sg("acc", [P, NT, 2, HALF], F32, early)
        x_in = sg("x_in", [P, 2, 2, D], F32, early)
        xn = sg("xn", [P, 2, 2, D], F32, early)
        win_i = sg("win_i", [1, 2, NG], I32, early)
        a_b = sg("a_b", [P, 2, D], F32, early)
        region1 = top[0]
        rows = sg("rows", [P, RING, GC, ROW], F32, early)
        sdst_b = sg("sdst_b", [P, NTN], F32, early)
        node_id = sg("node_id", [P, NTN], I16, early)
        ba_b = sg("ba_b", [P, 1], F32, early)
        srcT = sg("srcT", [P, NG * GC], I32, early)
        dstT = sg("dstT", [P, NG * GC], F32, early)
        idx = sg("idx", [P, RING, GC], I32, early)
        ch_mm = sg("ch_mm", [P, 2, CJ], F32, early)
        window = sg("window", [1, NG + BACK], I32, early)
        E1 = sg("E1", [P, 3, GC, P], F32, early)
        E2 = sg("E2", [P, 3, GC, P], F32, early)
        Wt = sg("Wt", [P, 3, GC, P], F32, early)
        S = sg("S", [P, SR + 1, GC, P], F32, early)

        bw_b = sg("bw_b", [P, D], F32, early)
        win_f = sg("win_f", [1, 2, NG], F32, early)
        win_n = sg("win_n", [1, 3, NG], F32, early)
        zero_r = sg("zero_r", [1, NG], F32, early)
        win_w = sg("win_w", [1, 2, NG + BACK], F32, early)
        s_dot = sg("s_dot", [P, 2, 2, 2], F32, early)
        s_dst = sg("s_dst", [P, NT], F32, early)
        cst2 = sg("cst2", [P, 2], F32, early)
        region2 = top[0]
        xT = sg("xT", [P, 2, 2, KT, 2 * P], F32R, early)
        Wb = sg("Wb", [P, 2, KT, D], F32R, early)
        Wf = sg("Wf", [P, KT, D], F32, early)
        junk = sg("junk", [P, 4, D], F32, early)
        edge_i = sg("edge_i", [P, 2, CJ, P], I32, early)
        edge_f = sg("edge_f", [P, 2, CJ, P], F32, early)
        region3 = region2 + max(top[0] - region2, NX * (KT * F + HF * D) * 4)
        early.close()

        top[0] = 0
        W1_hi = sg("W1_hi", [P, NX, KT, F], F32R)
        xg = sg("xg", [P, YR, D], F32)
        gi = sg("gi", [P, YR, 1], I32)
        si = sg("si", [P, YR, 1], I32)
        hot = ctx.enter_context(ExitStack())
        before_hot = top[0]
        hot_r = sg("hot_r", [P, ITEMS, P], BF16, hot)
        hot_t = sg("hot_t", [P, ITEMS, TILES], BF16, hot)
        hot_v = sg("hot_v", [P, 2, ITEMS, TILES], BF16, hot)
        assert top[0] <= region1
        hot.close()
        top[0] = before_hot
        xgT = sg("xgT", [P, 2, 2, KT * P], F32R)
        hid = sg("hid", [P, 2, F], F32)
        act_h = sg("act_h", [P, 2, F], F32)
        reach("gap1", region1)

        rounds = sg("rounds", [1, 2], I32)
        expert_of = sg("expert_of", [1, 4 * ROUNDS + 4], I32)
        src_row = sg("src_row", [P, 4 * ROUNDS + 1], I32)
        dst_row = sg("dst_row", [P, 4 * ROUNDS + 1], I32)
        share = sg("share", [P, 4 * ROUNDS], F32)
        b1_b = sg("b1_b", [P, NX, F], F32)
        b2_b = sg("b2_b", [P, NX, D], F32)
        W2_hi = sg("W2_hi", [P, NX, HF, D], F32R)
        routing = ctx.enter_context(ExitStack())
        before_routing = top[0]

        def sr(name, shape, dt):
            return sg(name, shape, dt, routing)

        Wg_sb = sr("Wg_sb", [P, KT, NX], F32)
        bg_c = sr("bg_c", [NX, 1], F32)
        count_i = sr("count_i", [P, P], I32)
        count = sr("count", [P, P], F32)
        count_b = sr("count_b", [P, P], BF16)
        part_i = sr("part_i", [P, 1], I32)
        part1 = sr("part1", [P, 1], F32)
        beyond = sr("beyond", [P, TILES], F32)
        beyond_i = sr("beyond_i", [P, TILES], I32)
        valid = sr("valid", [P, 2, NT], F32)
        below = sr("below", [P, P], F32)
        all_1 = sr("all_1", [P, P], F32)
        prob = sr("prob", [P, 2, NT], F32)
        score = sr("score", [P, NT, NX], F32)
        pr = sr("pr", [P, NT, NX], F32)
        pick = sr("pick", [P, NT, NX], F32)
        red = sr("red", [P, NT], F32)
        choice = sr("choice", [P, NX, 2, NT], F32)
        rank = sr("rank", [P, NX, ITEMS], F32)
        zeros = sr("zeros", [P, NX * ITEMS], F32)
        per = sr("per", [P, 7, NX], F32)
        per_i = sr("per_i", [P, NX], I32)
        pos = sr("pos", [P, ITEMS], F32)
        pos_i = sr("pos_i", [P, 3, ITEMS], I32)
        pos_f = sr("pos_f", [P, 2, ITEMS], F32)
        prob_b = sr("prob_b", [P, 3, ITEMS], BF16)
        prob_r = sr("prob_r", [P, 2, ITEMS], F32)
        inv = sr("inv", [P, 3, TILES], F32)
        ends = sr("ends", [1, TILES, NX], F32)
        end_n = sr("end_n", [1, TILES], F32)
        transposed = ctx.enter_context(ExitStack())
        before_xnT = top[0]
        xnT = sg("xnT", [P, 2, KT, 2, P], F32, transposed)
        logT = sg("logT", [NX, 2, 2 * P], F32, transposed)
        transposed.close()
        top[0] = before_xnT
        hot_p = sr("hot_p", [P, 3, ITEMS, TILES], BF16)
        assert top[0] <= region2
        routing.close()
        top[0] = before_routing
        hidT = sg("hidT", [P, 2, 2, HF * P], F32R)
        y_b = sg("y_b", [P, 2, D], F32)
        y = sg("y", [P, YR, D], F32)
        reach("gap2", region2)

        whole = ctx.enter_context(ExitStack())
        W1_e = sg("W1_e", [P, NX, KT, F], F32, whole)
        W2_e = sg("W2_e", [P, NX, HF, D], F32, whole)
        assert top[0] <= region3
        whole.close()
        W1_lo = sg("W1_lo", [P, NX, KT, F], F32R)
        W2_lo = sg("W2_lo", [P, NX, HF, D], F32R)

        pair = [ctx.enter_context(nc.psum_tensor(f"ps{i}", [P, 2, 512], F32)) for i in range(4)]
        ps = [pair[i // 2][:, i % 2, :] for i in range(8)]
        psT = [[ps[2 * s], ps[2 * s + 1]] for s in range(2)]
        ps_h = [[ps[4], ps[5]], [ps[6], ps[7]]]
        ps_edge = ps_h[1]
        ps_d = [ps[3], ps[2], ps[4], ps[5], ps[7]]
        assert 4 * len(ps_d) - 4 <= NT - 2 and NT <= 4 * len(ps_d)
        ps_agg = pair[0:3]
        ps_logT = [ps[6], ps[7]]
        ps_logit, ps_sum, ps_inv, ps_share = ps[4], ps[5], ps[6], ps[7]
        ps_x, ps_hT, ps_hid, ps_y = ps[0], ps[1], [ps[2], ps[3]], [ps[4], ps[5]]

        def halves(ap):
            return ap.rearrange("p (a d) -> p a d", a=2)

        def features(t):
            return acc[:, bass.ds(t, 1), :, 0:HD].rearrange("p t a d -> p (t a) d")

        ld_x = [[sem(f"ld_x{s}{j}") for j in range(2)] for s in range(2)]
        ld_W, ld_edge, ld_par = sem("ld_W"), sem("ld_edge"), sem("ld_par")
        pads, ident_ok, ids_ok, zeros_ok = sem("pads"), sem("ident_ok"), sem("ids_ok"), sem("zeros_ok")
        dv = sem("dv_setup")
        W_hi, W_ok, cst_ok, edges_f, edges_ps, edges_ok = (sem(n) for n in (
            "W_hi", "W_ok", "cst_ok", "edges_f", "edges_ps", "edges_ok"))
        mm_ps, win_ok, mm_ok = sem("mm_ps"), sem("win_ok"), sem("mm_ok")
        stats_ok, std_ok, rstd_ok, xn_ok = (sem(n) for n in ("stats_ok", "std_ok", "rstd_ok", "xn_ok"))
        xT_ps, xT_hi, xT_lo = sem("xT_ps"), sem("xT_hi"), sem("xT_lo")
        h_ps, row_ok, d_ps, d_ok = (sem(n) for n in ("h_ps", "row_ok", "d_ps", "d_ok"))
        dot_ok, s_ok, s_dst_ok = sem("dot_ok"), sem("s_ok"), sem("s_dst_ok")
        st_row = [[sem(f"st_row{s}{j}") for j in range(2)] for s in range(2)]
        idx_ok = sem("idx_ok")
        got = [sem(f"got{r}") for r in range(RING)]
        exp_ok = sem("exp_ok")
        max_ok = [sem("max_ok0"), sem("max_ok1")]
        S_ok, agg_ok = sem("S_ok"), sem("agg_ok")
        xexp_ok, xmax_ok, xS_ok, xagg_ok = (sem(n) for n in ("xexp_ok", "xmax_ok", "xS_ok", "xagg_ok"))
        acc_ok, added, xadded = sem("acc_ok"), sem("added"), sem("xadded")
        ld_x2 = [[sem(f"ld_x2_{s}{j}") for j in range(2)] for s in range(2)]
        st_xn = [[sem(f"st_xn_{s}{j}") for j in range(2)] for s in range(2)]
        ld_b = sem("ld_b")
        ld_late, ld_W1, ld_W2 = sem("ld_late"), sem("ld_W1"), sem("ld_W2")
        x1_ok, stats2_ok, aggr2_ok, std2_ok, rstd2_ok, xn2_ok = (sem(n) for n in (
            "x1_ok", "stats2_ok", "aggr2_ok", "std2_ok", "rstd2_ok", "xn2_ok"))
        xnT_ps, xnT_ok, logT_ps, logT_ok, logit_ps = (sem(n) for n in (
            "xnT_ps", "xnT_ok", "logT_ps", "logT_ok", "logit_ps"))
        shift_ok, exp2_ok, cnt_ok, cnt_ps = sem("shift_ok"), sem("exp2_ok"), sem("cnt_ok"), sem("cnt_ps")
        hot_ok, inv_ps, routed = sem("hot_ok"), sem("inv_ps"), sem("routed")
        consts_ok, share_ok = sem("consts_ok"), sem("share_ok")
        st_x1 = sem("st_x1")
        W1_hi_ok, W2_hi_ok, W1_lo_ok, W2_lo_ok = (sem(n) for n in ("W1_hi_ok", "W2_hi_ok", "W1_lo_ok", "W2_lo_ok"))
        gi_ok, si_ok = sem("gi_ok"), sem("si_ok")
        got_x = [sem(f"got_x{r}") for r in range(YR)]
        put_y = sem("put_y")
        x_ps, x_hi, x_lo, hid_ps, hid_ok, gelu_ok, hidT_ps, hidT_hi, hidT_lo, y_ps, yb_ok, y_ok = (sem(n) for n in (
            "x_ps", "x_hi", "x_lo", "hid_ps", "hid_ok", "gelu_ok", "hidT_ps", "hidT_hi", "hidT_lo", "y_ps", "yb_ok",
            "y_ok"))
        st_out = sem("st_out")

        def experts(eng, regs, i):
            eng.load(regs, expert_of[0:1, bass.ds(i, len(regs))])

        def expert_in(eng, reg):
            return nc.s_assert_within(eng.snap(reg), 0, NX - 1,
                                      skip_runtime_bounds_check_because="the table's words are built so")

        def over_steps(eng, step):
            for u in range(4):
                step(u, u % 2)
            with eng.Fori(2, NT // 4 - 1) as i:
                for s in range(2):
                    step(2 * i + s, s)
            for u in range(NT // 2 - 2, NT // 2 + 2):
                step(u, u % 2)

        def over_tiles(eng, regs, step):
            def some(i, n, at):
                if regs:
                    experts(eng, regs[0:n + 1], i)
                for k in range(n):
                    step(at + k, i + k, regs[k + 1] if regs else None, regs[k] if regs else None,
                         (True, at + k >= 1, at + k >= 2))
            some(0, 4, 0)
            some(4, 4, 4)
            n_rounds = rounds_in(eng)
            with eng.Fori(2, n_rounds) as b:
                some(4 * b, 4, 4)
            if regs:
                experts(eng, regs[0:3], 4 * n_rounds)
            for k in range(2):
                step(k, 4 * n_rounds + k, regs[k + 1] if regs else None, regs[k] if regs else None,
                     (False, k == 0, True))
            return n_rounds

        def rounds_in(eng):
            reg = eng.alloc_register("rounds")
            eng.load([reg], rounds[0:1, 0:1])
            more = nc.s_assert_within(eng.snap(reg) & 7, 0, ROUNDS - ROUNDS_MIN,
                                      skip_runtime_bounds_check_because="so many items there are")
            return eng.snap(more + ROUNDS_MIN)

        def window_words(eng, regs, i, back=0):
            eng.load(regs, window[0:1, bass.ds(RING * i + BACK - back, len(regs))])

        def field(word, shift, mask, most):
            return nc.s_assert_within((word >> shift) & mask if shift else word & mask, 0, most,
                                      skip_runtime_bounds_check_because="the table's words are built so")

        def tile_in(word):
            return field(word, 0, 31, NT - 1)

        def extra_in(word):
            return field(word, 5, 31, NT - 1)

        def before_in(word):
            return field(word, 10, 4095, NG * NT)

        def tile_of(value):
            return nc.s_assert_within(value, 0, NT - 1, skip_runtime_bounds_check_because="a tile of the window")

        block = ctx.enter_context(nc.Block())

        @block.sync
        def _(sp):
            def load_x(u, s, j):
                if u is not None:
                    tile = x[0:(NT - 1) * P, :].rearrange("(t p) d -> t p d", p=P)[bass.ds(2 * u + j, 1)]
                    sp.dma_start(x_in[:, s, j, :], tile.rearrange("t p d -> (t p) d")).then_inc(ld_x[s][j], 16)
                else:
                    sp.dma_start(x_in[0:LAST, s, j, :], x[(NT - 1) * P:N, :]).then_inc(ld_x[s][j], 16)

            def store_rows(u, s, i):
                sp.wait_ge(s_ok, u + 1)
                for j in range(2):
                    sp.wait_ge(row_ok, 2 * u + j + 1)
                    sp.dma_start(table[bass.ds((2 * u + j) * P, P), :], rows[:, s, j, :])\
                        .then_inc(st_row[s][j], 16)

            load_x(0, 0, 0)
            load_x(0, 0, 1)
            sp.dma_start(Wf[:, :, :], gnn_W.rearrange("(k p) n -> p k n", p=P)).then_inc(ld_W, 16)
            load_x(1, 1, 0)
            load_x(1, 1, 1)
            full = (CH - 1) * P if E % P else E
            sp.wait_ge(pads, 1)
            for k, e in enumerate((src, dst)):
                jf = full // (P * P)
                sp.dma_start(edge_i[:, k, 0:jf, :], e[0:jf * P * P].rearrange("(j q i) -> q j i", q=P, i=P))\
                    .then_inc(ld_edge, 16)
                q = (full - jf * P * P) // P
                sp.dma_start(edge_i[0:q, k, jf, :], e[jf * P * P:full].rearrange("(q i) -> q i", i=P))\
                    .then_inc(ld_edge, 16)
                sp.dma_start(edge_i[q:q + 1, k, jf, 0:E - full], e[full:E].rearrange("(q i) -> q i", q=1))\
                    .then_inc(ld_edge, 16)
            sp.dma_start(bw_b[:, :], gnn_b_w.partition_broadcast(P)).then_inc(ld_par, 16)
            sp.dma_start(a_b[:, :, :].rearrange("p a d -> p (a d)"), gnn_a.partition_broadcast(P)).then_inc(ld_par, 16)
            sp.dma_start(ba_b[:, :], gnn_b_a.partition_broadcast(P)).then_inc(ld_par, 16)

            def load_ahead(u, s, last=False):
                for j in range(2):
                    sp.wait_ge(xn_ok, 2 * (u - 2) + j + 1)
                    load_x(*((None, s, j) if last and j == 1 else (u, s, j)))

            load_ahead(2, 0)
            with sp.Fori(0, 3) as i:
                for s in range(2):
                    load_ahead(2 * i + s + 3, 1 - s)
                    store_rows(2 * i + s, s, i)
            load_ahead(9, 1, True)
            for u in range(6, NT // 2):
                store_rows(u, u % 2, u // 2)

            sp.wait_ge(d_ok, len(ps_d))
            sp.wait_ge(cst_ok, 1)
            sp.wait_ge(win_ok, 2)
            sp.wait_ge(row_ok, NT)
            sp.wait_ge(s_ok, NT // 2)
            with sp.Fori(0, NX) as e:
                sp.wait_ge(agg_ok, NG // (NX + 1) * e + 1)
                sp.dma_start(W1_e[:, bass.ds(e, 1), :, :].rearrange("p e k f -> p (e k) f"),
                             W1.rearrange("e (k p) f -> p e k f", p=P)[:, bass.ds(e, 1)]
                             .rearrange("p e k f -> p (e k) f")).then_inc(ld_W1, 16)
                sp.dma_start(W2_e[:, bass.ds(e, 1), :, :].rearrange("p e k d -> p (e k) d"),
                             W2.rearrange("e (k p) d -> p e k d", p=P)[:, bass.ds(e, 1)]
                             .rearrange("p e k d -> p (e k) d")).then_inc(ld_W2, 16)

            def load_x2(u, s, j, last=False):
                if last:
                    sp.dma_start(x_in[0:LAST, s, j, :], x[(NT - 1) * P:N, :]).then_inc(ld_x2[s][j], 16)
                else:
                    tile = x[0:(NT - 1) * P, :].rearrange("(t p) d -> t p d", p=P)[bass.ds(2 * u + j, 1)]
                    sp.dma_start(x_in[:, s, j, :], tile.rearrange("t p d -> (t p) d")).then_inc(ld_x2[s][j], 16)

            def store_xn(u, s):
                for j in range(2):
                    sp.wait_ge(xn2_ok, 2 * u + j + 1)
                    sp.dma_start(xn_table[bass.ds((2 * u + j) * P, P), :], xn[:, s, j, :]).then_inc(st_xn[s][j], 16)

            def x_step(u, s, last=False):
                for j in range(2):
                    sp.wait_ge(x1_ok, 2 * u + j + 1)
                    load_x2(u + 2, s, j, last and j == 1)
                sp.dma_start(halves(result[bass.ds(2 * u * P, P), :]), features(2 * u)).then_inc(st_x1, 16)
                store_xn(u, s)

            for u in range(2):
                for j in range(2):
                    load_x2(u, u, j)
            sp.wait_ge(acc_ok, 1)
            sp.dma_start(Wg_sb[:, :, :], Wg.rearrange("(k p) e -> p k e", p=P)).then_inc(ld_late, 16)
            sp.dma_start(bg_c[:, :], bg.rearrange("(e o) -> e o", o=1)).then_inc(ld_late, 16)
            with sp.Fori(0, 3) as i:
                for s in range(2):
                    x_step(2 * i + s, s)
            x_step(NT // 2 - 4, 0)
            x_step(NT // 2 - 3, 1, last=True)
            for s in range(2):
                u = NT // 2 - 2 + s
                store_xn(u, s)
            for t in [2 * u + 1 for u in range(NT // 2 - 2)] + list(range(NT - 4, NT)):
                sp.dma_start(halves(result[t * P:(t + 1) * P, :]), features(t)).then_inc(st_x1, 16)
            sp.dma_start(result[NTN:NTN + P, :].rearrange("p (a d) -> p a d", a=2), features(NT - 1)).then_inc(st_x1, 16)
            sp.dma_start(b1_b[:, :, :].rearrange("p e f -> p (e f)"),
                         b1.rearrange("e f -> (e f)").partition_broadcast(P)).then_inc(ld_b, 16)
            sp.dma_start(b2_b[:, :, :].rearrange("p e d -> p (e d)"),
                         b2.rearrange("e d -> (e d)").partition_broadcast(P)).then_inc(ld_b, 16)

            sp.wait_ge(routed, 1)
            sp.wait_ge(put_y, 16 * 4 * rounds_in(sp))
            sp.dma_start(out[0:N // 2, :], result[0:N // 2, :]).then_inc(st_out, 16)
            sp.wait_ge(st_out, 32)

        @block.gpsimd
        def _(pool):
            nc.gpsimd.memset(edge_i[:, 0, :, :], 0)
            nc.gpsimd.memset(edge_i[:, 1, :, :], 4095).then_inc(pads, 1)
            nc.gpsimd.memset(ident[:, :], 0.0).then_inc(zeros_ok, 1)
            pool.wait_ge(zeros_ok, 1)
            nc.gpsimd.affine_select(out=ident[:, :], in_=ident[:, :], compare_op=ALU.not_equal, fill=1.0, base=0,
                                    pattern=[[-1, P]], channel_multiplier=1).then_inc(ident_ok, 1)
            nc.gpsimd.memset(rows[:, 0:2, :, ONE:ONE + 1], 1.0)
            nc.gpsimd.memset(rows[:, 0:2, :, ROW - 1:ROW], 0.0).then_inc(pads, 1)
            nc.gpsimd.iota(node_id[:, :], pattern=[[1, NTN]], base=0, channel_multiplier=0)
            nc.gpsimd.memset(acc[:, :, :, :], 0.0).then_inc(ids_ok, 1)

            def copy_idx(g, r):
                nc.gpsimd.tensor_copy(idx[:, r, :], srcT[:, bass.ds(GC * g, GC)]).then_inc(idx_ok, 1)

            def gather(g, r, last=False):
                pool.wait_ge(idx_ok, g + 1)
                if not (isinstance(g, int) and g < RING):
                    pool.wait_ge(agg_ok, g - RING + 2)
                if not last:
                    copy_idx(g + 1, (r + 1) % RING)
                for c in range(GC):
                    nc.gpsimd.indirect_dma_start(
                        out=rows[:, r, c, :], out_offset=None, in_=table,
                        in_offset=bass.IndirectOffsetOnAxis(ap=idx[:, r, c:c + 1], axis=0)).then_inc(got[r], 16)

            pool.wait_ge(edges_ok, 2)
            for s in range(2):
                for j in range(2):
                    pool.wait_ge(st_row[s][j], 16 * NT // 4)
            copy_idx(0, 0)
            for r in range(RING):
                if r == RING - 1:
                    pool.wait_ge(agg_ok, 1)
                gather(r, r)
            with pool.Fori(1, NG // RING - 1) as i:
                for r in range(RING):
                    gather(RING * i + r, r)
            for r in range(RING):
                gather(NG - RING + r, r, last=r == RING - 1)

            pool.wait_ge(acc_ok, 1)
            nc.gpsimd.iota(count_i[:, :], pattern=[[1, P]], base=0, channel_multiplier=0)
            nc.gpsimd.iota(part_i[:, :], pattern=[[0, 1]], base=1, channel_multiplier=1)
            nc.gpsimd.iota(beyond_i[:, :], pattern=[[0, TILES]], base=NTN, channel_multiplier=1)
            nc.gpsimd.memset(all_1[:, :], 1.0)
            nc.gpsimd.memset(zeros[:, :], 0.0)
            nc.gpsimd.memset(below[:, :], 1.0)
            nc.gpsimd.memset(expert_of[:, :], 0)
            nc.gpsimd.memset(src_row[:, TILES:4 * ROUNDS + 1], 0)
            nc.gpsimd.iota(dst_row[:, TILES:4 * ROUNDS + 1], pattern=[[0, 4 * ROUNDS + 1 - TILES]], base=NTN,
                           channel_multiplier=1)
            if TILES < 4 * ROUNDS:
                nc.gpsimd.memset(share[:, TILES:4 * ROUNDS], 0.0)
            nc.gpsimd.memset(valid[:, :, :], 1.0).then_inc(consts_ok, 1)
            pool.wait_ge(consts_ok, 1)
            nc.gpsimd.affine_select(out=below[:, :], in_=below[:, :], compare_op=ALU.is_gt, fill=0.0, base=0,
                                    pattern=[[1, P]], channel_multiplier=-1)
            nc.gpsimd.affine_select(out=valid[:, :, :], in_=valid[:, :, :], compare_op=ALU.is_ge, fill=0.0,
                                    base=N - 1, pattern=[[0, 2], [-P, NT]], channel_multiplier=-1)\
                .then_inc(consts_ok, 1)

            for e in range(NX):
                pool.wait_ge(W2_hi_ok, e + 1)
                nc.gpsimd.tensor_tensor(W2_lo[:, e, :, :], W2_e[:, e, :, :], W2_hi[:, e, :, :].bitcast(F32),
                                        ALU.subtract).then_inc(W2_lo_ok, 1)
            for e in range(NX):
                pool.wait_ge(W1_hi_ok, e + 1)
                nc.gpsimd.tensor_tensor(W1_lo[:, e, :, :], W1_e[:, e, :, :], W1_hi[:, e, :, :].bitcast(F32),
                                        ALU.subtract).then_inc(W1_lo_ok, 1)

            def copy_gi(i, r):
                nc.gpsimd.tensor_copy(gi[:, r, :], src_row[:, bass.ds(i, 1)]).then_inc(gi_ok, 1)

            def copy_si(i, r):
                nc.gpsimd.tensor_copy(si[:, r, :], dst_row[:, bass.ds(i, 1)]).then_inc(si_ok, 1)

            def row_step(i, r, has_gather=True):
                peeled = isinstance(i, int)
                has_add = not (peeled and i < LAG)

                def wait_to_add():
                    pool.wait_ge(y_ok, i - LAG + 1)
                    if not (peeled and i < LAG + 1):
                        pool.wait_ge(put_y, 16 * (i - LAG))

                if has_gather:
                    pool.wait_ge(gi_ok, i + 1)
                    if not (peeled and i < YR):
                        pool.wait_ge(x_ps, i + 1 - YR)
                if has_add:
                    pool.wait_ge(si_ok, i - LAG + 1)
                    if not has_gather:
                        wait_to_add()
                if not (peeled and i + 1 < LAG):
                    copy_si(i + 1 - LAG, (r + 1 - LAG) % YR)
                if has_gather:
                    nc.gpsimd.indirect_dma_start(
                        out=xg[:, r, :], out_offset=None, in_=xn_table,
                        in_offset=bass.IndirectOffsetOnAxis(ap=gi[:, r, :], axis=0)).then_inc(got_x[r], 16)
                    if has_add:
                        wait_to_add()
                    if not (peeled and i + 1 < YR):
                        pool.wait_ge(x_ps, i + 2 - YR)
                    copy_gi(i + 1, (r + 1) % YR)
                if has_add:
                    nc.gpsimd.indirect_dma_start(
                        out=result, out_offset=bass.IndirectOffsetOnAxis(ap=si[:, (r - LAG) % YR, :], axis=0),
                        in_=y[:, (r - LAG) % YR, :], in_offset=None, compute_op=ALU.add).then_inc(put_y, 16)

            pool.wait_ge(routed, 1)
            for s in range(2):
                for j in range(2):
                    pool.wait_ge(st_xn[s][j], 16 * NT // 4)
            pool.wait_ge(st_x1, 16 * (NT + 1))
            copy_gi(0, 0)
            for i in range(2 * YR):
                row_step(i, i % YR)
            n_rounds = rounds_in(pool)
            with pool.Fori(2, n_rounds) as b:
                for r in range(YR):
                    row_step(YR * b + r, r)
            for k in range(LAG):
                row_step(YR * n_rounds + k, k % YR, has_gather=False)

        @block.tensor
        def _(pe):
            regs = [pe.alloc_register(f"pe_window{k}") for k in range(RING)]
            pe.wait_ge(ident_ok, 1)

            def edge_columns(k):
                for j in range(CJ):
                    m = pe.transpose(ps_edge[k][:, j * P:(j + 1) * P], edge_f[:, k, j, :], ident[:, :])
                m.then_inc(edges_ps, 1)

            def transposes(u, s):
                for j in range(2):
                    pe.wait_ge(xn_ok, 2 * u + j + 1)
                    for k in range(KT):
                        m = pe.transpose(psT[s][k // 2][:, (k % 2) * 2 * P + j * P:(k % 2) * 2 * P + (j + 1) * P],
                                         xn[:, s, j, k * P:(k + 1) * P], ident[:, :])
                m.then_inc(xT_ps, 1)

            def products(u, s, first):
                pe.wait_ge(xT_lo, u + 1)
                three = [(0, 0), (1, 0), (0, 1)]
                for j in range(2):
                    if not first:
                        pe.wait_ge(row_ok, 2 * u + j - 3)
                    n = 0
                    for k in range(KT):
                        for a, b in three:
                            m = pe.matmul(ps_h[s][j][:, :], xT[:, s, a, k, j * P:(j + 1) * P], Wb[:, b, k, :],
                                          start=(n == 0), stop=(n == 3 * KT - 1))
                            n += 1
                    m.then_inc(h_ps, 1)

            transposes(0, 0)
            transposes(1, 1)
            pe.wait_ge(W_ok, 1)
            products(0, 0, True)
            pe.wait_ge(edges_f, 1)
            edge_columns(0)
            edge_columns(1)
            transposes(2, 0)
            pe.wait_ge(edges_ok, 2)
            products(1, 1, True)
            with pe.Fori(1, NT // 4 - 1) as i:
                transposes(2 * i + 1, 1)
                products(2 * i, 0, False)
                transposes(2 * i + 2, 0)
                products(2 * i + 1, 1, False)
            transposes(NT // 2 - 1, 1)
            products(NT // 2 - 2, 0, False)
            pe.wait_ge(mm_ok, 1)
            for k in range(2):
                for j in range(CJ):
                    m = pe.transpose(psT[0][k][0:1, j * P:(j + 1) * P], ch_mm[:, k, j:j + 1], ident[:, :])
            m.then_inc(mm_ps, 1)
            products(NT // 2 - 1, 1, False)
            pe.wait_ge(xT_lo, NT // 2)
            pe.wait_ge(row_ok, NT - 2)
            for b in range(len(ps_d)):
                last = b == len(ps_d) - 1
                pe.wait_ge(s_dst_ok, NT // 2 if last else NT // 2 - 1)
                if last:
                    pe.wait_ge(row_ok, NT)
                for t in range(4 * b, min(4 * b + 4, NT)):
                    m = pe.matmul(ps_d[b][:, (t - 4 * b) * P:(t - 4 * b + 1) * P],
                                  s_dst[:, t:t + 1].to_broadcast([P, P]), ident[:, :], start=True, stop=True)
                m.then_inc(d_ps, 1)

            def sums(q, w, r):
                for c in range(GC):
                    for a in range(2):
                        m = pe.matmul(ps_agg[q][:, a, 0:HALF], S[:, w, c, :], rows[:, r, c, a * HALF:(a + 1) * HALF],
                                      start=(c == 0), stop=(c == GC - 1))
                return m

            def group(g, r, i):
                pe.wait_ge(S_ok, g + 1)
                if not (isinstance(g, int) and g < 2):
                    pe.wait_ge(added, g - 1)
                sums(r % 2, r % SR, r).then_inc(agg_ok, 1)
                word = pe.snap(regs[r])
                extra = pe.snap(extra_in(word))
                with pe.If(extra > 0):
                    before = pe.snap(before_in(word))
                    with pe.Fori(0, extra) as n:
                        pe.wait_ge(xS_ok, before + n + 2)
                        pe.wait_ge(xadded, before + n + 1)
                        sums(2, SR, r).then_inc(xagg_ok, 1)

            pe.wait_ge(row_ok, NT)
            pe.wait_ge(s_ok, NT // 2)
            pe.wait_ge(d_ok, len(ps_d))
            pe.wait_ge(win_ok, 2)
            window_words(pe, regs, 0)
            for r in range(RING):
                group(r, r, 0)
            with pe.Fori(1, NG // RING) as i:
                window_words(pe, regs, i)
                for r in range(RING):
                    group(RING * i + r, r, i)

            def normal_T(u, s):
                for j in range(2):
                    pe.wait_ge(xn2_ok, 2 * u + j + 1)
                    if j == 0 and not (isinstance(u, int) and u < 2):
                        pe.wait_ge(xnT_ok, u - 1)
                    for k in range(KT):
                        m = pe.transpose(psT[s][j][:, k * P:(k + 1) * P], xn[:, s, j, k * P:(k + 1) * P], ident[:, :])
                m.then_inc(xnT_ps, 1)

            def logits(u, s):
                pe.wait_ge(xnT_ok, u + 1)
                if not (isinstance(u, int) and u < 2):
                    pe.wait_ge(logT_ok, u - 1)
                for k in range(KT):
                    m = pe.matmul(ps_logT[s][0:NX, 0:2 * P], Wg_sb[:, k, :],
                                  xnT[:, s, k, :, :].rearrange("p j n -> p (j n)"), start=(k == 0), stop=(k == KT - 1))
                m.then_inc(logT_ps, 1)

            def logits_of_nodes(u, s):
                pe.wait_ge(logT_ok, u + 1)
                for j in range(2):
                    m = pe.matmul(ps_logit[:, bass.ds((2 * u + j) * NX, NX)], logT[:, s, j * P:(j + 1) * P],
                                  ident[0:NX, 0:NX], start=True, stop=True)
                m.then_inc(logit_ps, 1)

            def route_step(u, s):
                peeled = isinstance(u, int)
                if not (peeled and u >= NT // 2):
                    normal_T(u, s)
                if not (peeled and (u < 1 or u > NT // 2)):
                    logits(u - 1, 1 - s)
                if not (peeled and u < 2):
                    logits_of_nodes(u - 2, s)

            pe.wait_ge(acc_ok, 1)
            pe.wait_ge(ld_late, 16 * 2)
            over_steps(pe, route_step)
            pe.wait_ge(cnt_ok, 1)
            pe.wait_ge(consts_ok, 2)
            pe.matmul(ps_sum[:, 0:NX], below[:, :], per[:, 0, :], start=True, stop=True)
            pe.matmul(ps_sum[:, NX:2 * NX], all_1[:, :], per[:, 0, :], start=True, stop=True).then_inc(cnt_ps, 1)
            pe.wait_ge(hot_ok, 1)
            for v in range(2):
                for t in range(ITEMS):
                    m = pe.matmul(ps_inv[:, v * TILES:(v + 1) * TILES], hot_r[:, t, :], hot_v[:, v, t, :],
                                  start=(t == 0), stop=(t == ITEMS - 1))
            m.then_inc(inv_ps, 1)
            for v in range(3):
                pe.wait_ge(hot_ok, 2 + v)
                for t in range(ITEMS):
                    m = pe.matmul(ps_share[:, 0:TILES], hot_r[:, t, :], hot_p[:, v, t, :],
                                  start=(t == 0 and v == 0), stop=(t == ITEMS - 1 and v == 2))
            m.then_inc(inv_ps, 1)

            def tile_step(i, n, e_mid, e_old, parts):
                s, r, peeled = i % 2, i % YR, isinstance(n, int)
                new, mid, old = parts
                three = [(0, 0), (1, 0), (0, 1)]
                if old:
                    pe.wait_ge(gelu_ok, n - 1)
                    if not (peeled and n < 3):
                        pe.wait_ge(hidT_lo, n - 2)
                    for k in range(HF):
                        m = pe.transpose(ps_hT[:, k * P:(k + 1) * P], act_h[:, s, k * P:(k + 1) * P], ident[:, :])
                    m.then_inc(hidT_ps, 1)
                if new:
                    pe.wait_ge(got_x[r], tile_count(n, i))
                    if not (peeled and n < 1):
                        pe.wait_ge(x_lo, n)
                    for k in range(KT):
                        m = pe.transpose(ps_x[:, k * P:(k + 1) * P], xg[:, r, k * P:(k + 1) * P], ident[:, :])
                    m.then_inc(x_ps, 1)
                if mid:
                    e = expert_in(pe, e_mid)
                    pe.wait_ge(x_lo, n)
                    if not (peeled and n < 3):
                        pe.wait_ge(hid_ok, n - 2)
                    for k in range(KT):
                        for a, b in three:
                            m = pe.matmul(ps_hid[1 - s][:, 0:F], xgT[:, 1 - s, a, k * P:(k + 1) * P],
                                          (W1_hi, W1_lo)[b][:, bass.ds(e, 1), k, :].rearrange("p e f -> p (e f)"),
                                          start=(k == 0 and (a, b) == (0, 0)), stop=(k == KT - 1 and b == 1))
                    m.then_inc(hid_ps, 1)
                if old:
                    e = expert_in(pe, e_old)
                    pe.wait_ge(hidT_lo, n - 1)
                    if not (peeled and n < 4):
                        pe.wait_ge(yb_ok, n - 3)
                    for k in range(HF):
                        for a, b in three:
                            m = pe.matmul(ps_y[s][:, :], hidT[:, s, a, k * P:(k + 1) * P],
                                          (W2_hi, W2_lo)[b][:, bass.ds(e, 1), k, :].rearrange("p e d -> p (e d)"),
                                          start=(k == 0 and (a, b) == (0, 0)), stop=(k == HF - 1 and b == 1))
                    m.then_inc(y_ps, 1)

            def tile_count(n, i):
                return 16 * (n // YR + 1) if isinstance(n, int) else 4 * (n - i % YR) + 16

            pe.wait_ge(routed, 1)
            pe.wait_ge(W1_lo_ok, NX)
            pe.wait_ge(W2_lo_ok, NX)
            pe_experts = [pe.alloc_register(f"pe_expert{k}") for k in range(5)]
            over_tiles(pe, pe_experts, tile_step)

        @block.scalar
        def _(act):
            regs = [act.alloc_register(f"act_window{k}") for k in range(RING + 1)]
            def std_of(u, s):
                act.wait_ge(stats_ok, u + 1)
                nc.scalar.activation(std[:, s, :], mv[:, s, :, 1], ACT.Sqrt, bias=eps[:, :]).then_inc(std_ok, 1)

            def high_xT(u, s):
                act.wait_ge(xT_ps, u + 1)
                if not (isinstance(u, int) and u < 2):
                    act.wait_ge(h_ps, 2 * u - 2)
                for b in range(2):
                    m = nc.scalar.activation(xT[:, s, 0, 2 * b:2 * b + 2, :].rearrange("p k n -> p (k n)"),
                                             psT[s][b][:, :], ACT.Copy)
                m.then_inc(xT_hi, 1)

            def normal(u, s):
                for j in range(2):
                    act.wait_ge(rstd_ok, 4 * u + 4)
                    if not (isinstance(u, int) and u < 2):
                        act.wait_ge(xT_ps, u - 1)
                    nc.scalar.activation(xn[:, s, j, :], x_in[:, s, j, :], ACT.Identity, bias=shift[:, s, j:j + 1],
                                         scale=rstd[:, s, j:j + 1]).then_inc(xn_ok, 1)

            std_of(0, 0)
            normal(0, 0)
            act.wait_ge(ld_W, 16)
            nc.scalar.activation(Wb[:, 0, :, :], Wf[:, :, :], ACT.Copy).then_inc(W_hi, 1)
            std_of(1, 1)
            normal(1, 1)
            high_xT(0, 0)

            def step(u, s, ahead):
                high_xT(u + 1, 1 - s)
                if ahead > 1:
                    std_of(u + 2, s)
                    normal(u + 2, s)

            step(0, 0, 2)
            with act.Fori(0, NT // 4 - 2) as i:
                step(2 * i + 1, 1, 2)
                step(2 * i + 2, 0, 2)
            step(NT // 2 - 3, 1, 2)
            step(NT // 2 - 2, 0, 1)
            for b in range(len(ps_d)):
                act.wait_ge(d_ps, b + 1)
                n = min(4, NT - 4 * b) * P
                nc.scalar.activation(sdst_b[:, 4 * b * P:4 * b * P + n], ps_d[b][:, 0:n], ACT.Copy).then_inc(d_ok, 1)

            def weights(q, r, tile):
                for k, (e, scale) in enumerate(((E1, 1.0), (E2, SLOPE))):
                    for c in range(GC):
                        bias = rows[:, r, c, S_SRC + k:S_SRC + k + 1]
                        m = nc.scalar.activation(e[:, q, c, :], sdst_b[:, bass.ds(tile * P, P)], ACT.Exp,
                                                 bias=bias, scale=scale)
                return m

            def extras(r):
                word = act.snap(regs[r])
                extra = act.snap(extra_in(word))
                with act.If(extra > 0):
                    tile, before = act.snap(tile_in(word)), act.snap(before_in(word))
                    with act.Fori(0, extra) as n:
                        act.wait_ge(xmax_ok, before + n + 1)
                        weights(2, (r - 1) % RING, tile_of(tile + n + 1)).then_inc(xexp_ok, 1)

            def group(r, i):
                tile = act.snap(tile_in(act.snap(regs[r + 1])))
                act.wait_ge(max_ok[r % 2], RING // 2 * i + r // 2 + 1)
                act.wait_ge(got[r], 16 * GC * (i + 1))
                weights(r % 2, r, tile).then_inc(exp_ok, 1)
                extras(r)

            act.wait_ge(d_ok, len(ps_d))
            act.wait_ge(win_ok, 2)
            act.wait_ge(cst_ok, 1)
            nc.scalar.activation(spare[:, 2:3], cst2[:, 0:1], ACT.Exp)
            with act.Fori(0, NG // RING) as i:
                window_words(act, regs, i, 1)
                for r in range(RING):
                    group(r, i)
            extras(RING)

            def std2_of(u, s):
                act.wait_ge(aggr2_ok, u + 1)
                nc.scalar.activation(std[:, s, :], mv[:, s, :, 1], ACT.Sqrt, bias=eps[:, :]).then_inc(std2_ok, 1)

            def xn_of(u, s):
                act.wait_ge(rstd2_ok, 2 * u + 2)
                for j in range(2):
                    if not (isinstance(u, int) and u < 2):
                        if j == 0:
                            act.wait_ge(xnT_ps, u - 1)
                        act.wait_ge(st_xn[s][j], 16 * (u // 2) if isinstance(u, int) else u * 8 - 8 * s)
                    nc.scalar.activation(halves(xn[:, s, j, :]), features(2 * u + j), ACT.Identity,
                                         bias=shift[:, s, j:j + 1], scale=rstd[:, s, j:j + 1]).then_inc(xn2_ok, 1)

            def xnT_of(u, s):
                act.wait_ge(xnT_ps, u + 1)
                if not (isinstance(u, int) and u < 2):
                    act.wait_ge(logT_ps, u - 1)
                for j in range(2):
                    m = nc.scalar.activation(xnT[:, s, :, j, :], psT[s][j].rearrange("p (k n) -> p k n", k=KT), ACT.Copy)
                m.then_inc(xnT_ok, 1)

            def logT_of(u, s):
                act.wait_ge(logT_ps, u + 1)
                if not (isinstance(u, int) and u < 2):
                    act.wait_ge(logit_ps, u - 1)
                nc.scalar.activation(logT[:, s, :], ps_logT[s][0:NX, 0:2 * P], ACT.Identity, bias=bg_c[:, :])\
                    .then_inc(logT_ok, 1)

            def high_W2(e):
                nc.scalar.activation(W2_hi[:, bass.ds(e, 1), :, :].rearrange("p e k d -> p (e k d)"),
                                     W2_e[:, bass.ds(e, 1), :, :].rearrange("p e k d -> p (e k d)"),
                                     ACT.Copy).then_inc(W2_hi_ok, 1)

            def route_step(u, s):
                peeled = isinstance(u, int)
                if not (peeled and u >= NT // 2 - 1):
                    std2_of(u + 1, 1 - s)
                if not (peeled and u >= NT // 2):
                    xn_of(u, s)
                if not (peeled and (u < 1 or u > NT // 2)):
                    xnT_of(u - 1, 1 - s)
                if not (peeled and u < 2):
                    logT_of(u - 2, s)
                if not (peeled and not 4 <= u < NT // 2 - 2):
                    high_W2(u - 4)

            act.wait_ge(acc_ok, 1)
            act.wait_ge(ld_late, 16 * 2)
            act.wait_ge(ld_W1, 16 * NX)
            act.wait_ge(ld_W2, 16 * NX)
            std2_of(0, 0)
            over_steps(act, route_step)
            n_early = NT // 2 - 6
            act.wait_ge(shift_ok, 1)
            nc.scalar.activation(pr[:, :, :], score[:, :, :], ACT.Exp).then_inc(exp2_ok, 1)

            for e in range(n_early, NX):
                high_W2(e)
            act.wait_ge(xn2_ok, NT)
            act.wait_ge(st_x1, 16 * (NT + 1))
            for e in range(NX):
                nc.scalar.activation(W1_hi[:, e, :, :], W1_e[:, e, :, :], ACT.Copy).then_inc(W1_hi_ok, 1)

            def share_of(m, r):
                if not (isinstance(m, int) and m < YR):
                    act.wait_ge(put_y, 16 * (m + 1 - YR))
                act.wait_ge(yb_ok, m + 1)
                nc.scalar.activation(y[:, r, :], y_b[:, r % 2, :], ACT.Copy, scale=share[:, bass.ds(m, 1)])\
                    .then_inc(y_ok, 1)

            def tile_step(i, n, _, __, parts):
                s, peeled = i % 2, isinstance(n, int)
                new, mid, old = parts
                if old:
                    act.wait_ge(hidT_ps, n - 1)
                    if not (peeled and n < 4):
                        act.wait_ge(y_ps, n - 3)
                    nc.scalar.activation(hidT[:, s, 0, :], ps_hT[:, 0:F], ACT.Copy).then_inc(hidT_hi, 1)
                if new:
                    act.wait_ge(x_ps, n + 1)
                    if not (peeled and n < 2):
                        act.wait_ge(hid_ps, n - 1)
                    nc.scalar.activation(xgT[:, s, 0, :], ps_x[:, :], ACT.Copy).then_inc(x_hi, 1)
                if mid:
                    act.wait_ge(hid_ok, n)
                    if not (peeled and n < 3):
                        act.wait_ge(hidT_ps, n - 2)
                    nc.scalar.activation(act_h[:, 1 - s, :], hid[:, 1 - s, :], ACT.Gelu_apprx_tanh).then_inc(gelu_ok, 1)
                if not (peeled and n < 3):
                    share_of(n - 3, (i - 3) % YR)

            nc.scalar.activation(spare[:, 2:3], eps[:, :], ACT.Gelu_apprx_tanh)
            act.wait_ge(routed, 1)
            act.wait_ge(share_ok, 1)
            n_rounds = over_tiles(act, None, tile_step)
            share_of(4 * n_rounds - 1, YR - 1)

            act.wait_ge(put_y, 16 * 4 * n_rounds)
            act.dma_start(out[N // 2:N, :], result[N // 2:N, :]).then_inc(st_out, 16)
            act.wait_ge(st_out, 32)

        @block.vector
        def _(dve):
            regs = [dve.alloc_register(f"dve_window{k}") for k in range(RING + BACK)]
            n_dv = [0]

            def link(ins):
                n_dv[0] += 1
                ins.then_inc(dv, 1)
                dve.wait_ge(dv, n_dv[0])

            nc.vector.memset(zero_r[:, :], 0.0)
            for k, count_ in enumerate((max_ok[0], max_ok[1], xmax_ok, xS_ok)):
                nc.vector.memset(start[:, k:k + 1], 0.0).then_inc(count_, 1)
            link(nc.vector.memset(eps[:, :], EPS))

            def normal(u, s):
                for j in range(2):
                    dve.wait_ge(ld_x[s][j], 16 * (u // 2 + 1) if isinstance(u, int) else u * 8 + 16 - 8 * s)
                    nc.vector.bn_stats(stats[:, s, j, :], x_in[:, s, j, :]).then_inc(rstd_ok, 1)
                dve.wait_ge(rstd_ok, 4 * u + 2)
                nc.vector.memset(spare[:, s:s + 1], 0.0)
                for j in range(2):
                    m = nc.vector.bn_aggr(mv[:, s, j, :], stats[:, s, j, :])
                m.then_inc(stats_ok, 1)

            def rstd_of(u, s):
                if not (isinstance(u, int) and u < 2):
                    dve.wait_ge(xn_ok, 2 * u - 2)
                dve.wait_ge(std_ok, u + 1)
                nc.vector.reciprocal(rstd[:, s, :], std[:, s, :]).then_inc(rstd_ok, 1)
                dve.wait_ge(rstd_ok, 4 * u + 3)
                nc.vector.scalar_tensor_tensor(out=shift[:, s, :], in0=mv[:, s, :, 0], scalar=-1.0, in1=rstd[:, s, :],
                                               op0=ALU.mult, op1=ALU.mult).then_inc(rstd_ok, 1)

            def low_xT(u, s):
                dve.wait_ge(xT_hi, u + 1)
                for b in range(2):
                    m = nc.vector.tensor_tensor(xT[:, s, 1, 2 * b:2 * b + 2, :].rearrange("p k n -> p (k n)"),
                                                psT[s][b][:, :],
                                                xT[:, s, 0, 2 * b:2 * b + 2, :].rearrange("p k n -> p (k n)").bitcast(F32),
                                                ALU.subtract)
                m.then_inc(xT_lo, 1)

            def node_rows(u, s, i):
                for j in range(2):
                    dve.wait_ge(h_ps, 2 * u + j + 1)
                    if not (isinstance(u, int) and u < 2):
                        dve.wait_ge(st_row[s][j], 16 * i)
                    nc.vector.tensor_tensor(halves(rows[:, s, j, 0:2 * HALF])[:, :, 0:HD], halves(ps_h[s][j]),
                                            halves(bw_b[:, :]), ALU.add).then_inc(row_ok, 1)
                    dve.wait_ge(row_ok, 2 * u + j + 1)
                    for k in range(2):
                        nc.vector.tensor_tensor_reduce(
                            halves(junk[:, 2 * k + j, :]), halves(rows[:, s, j, 0:2 * HALF])[:, :, 0:HD],
                            halves(a_b[:, 1 - k, :]), 1.0, 0.0, ALU.mult, ALU.add,
                            s_dot[:, s, k, j:j + 1]).then_inc(dot_ok, 1)
                dve.wait_ge(dot_ok, 4 * u + 3)
                for k, scale in enumerate((1.0, SLOPE)):
                    m = nc.vector.tensor_scalar(rows[:, s, :, S_SRC + k:S_SRC + k + 1],
                                                s_dot[:, s, 0, :].unsqueeze(2), scale, cst2[:, k:k + 1], ALU.mult, ALU.add)
                m.then_inc(s_ok, 1)
                dve.wait_ge(dot_ok, 4 * u + 4)
                nc.vector.tensor_copy(s_dst[:, bass.ds(2 * u, 2)], s_dot[:, s, 1, :]).then_inc(s_dst_ok, 1)

            normal(0, 0)
            rstd_of(0, 0)
            normal(1, 1)
            rstd_of(1, 1)
            dve.wait_ge(W_hi, 1)
            nc.vector.tensor_tensor(Wb[:, 1, :, :], Wf[:, :, :], Wb[:, 0, :, :].bitcast(F32), ALU.subtract).then_inc(W_ok, 1)
            low_xT(0, 0)
            dve.wait_ge(ld_par, 48)
            nc.vector.tensor_copy(cst2[:, 0:1], ba_b[:, :])
            nc.vector.tensor_scalar(cst2[:, 1:2], ba_b[:, :], SLOPE, None, ALU.mult).then_inc(cst_ok, 1)
            dve.wait_ge(cst_ok, 1)
            dve.wait_ge(ld_edge, 16 * 6)
            nc.vector.tensor_copy(edge_f[:, :, :, :], edge_i[:, :, :, :]).then_inc(edges_f, 1)
            dve.wait_ge(pads, 2)

            def step(u, s, i, ahead):
                if ahead > 1:
                    normal(u + 2, s)
                if ahead:
                    low_xT(u + 1, 1 - s)
                if ahead > 1:
                    rstd_of(u + 2, s)
                node_rows(u, s, i)

            step(0, 0, 0, 2)
            dve.wait_ge(edges_f, 1)
            for k, column in enumerate((srcT, dstT)):
                dve.wait_ge(edges_ps, k + 1)
                nc.vector.tensor_copy(column[:, :], ps_edge[k][:, 0:NG * GC]).then_inc(edges_ok, 1)
            for k in range(2):
                m = nc.vector.tensor_reduce(ch_mm[:, k, :], edge_f[:, 1, :, :], AX.X, (ALU.min, ALU.max)[k])
            m.then_inc(mm_ok, 1)
            step(1, 1, 0, 2)
            step(2, 0, 1, 2)
            with dve.Fori(1, NT // 4 - 2) as i:
                step(2 * i + 1, 1, i, 2)
                step(2 * i + 2, 0, i + 1, 2)
            step(NT // 2 - 3, 1, NT // 4 - 2, 2)
            step(NT // 2 - 2, 0, NT // 4 - 1, 1)
            step(NT // 2 - 1, 1, NT // 4 - 1, 0)
            dve.wait_ge(mm_ps, 1)
            for k in range(2):
                link(nc.vector.tensor_reduce(win_f[:, k, :],
                                             psT[0][k][0:1, 0:NG * GC].rearrange("o (g c) -> o g c", c=GC),
                                             AX.X, (ALU.min, ALU.max)[k]))
            link(nc.vector.tensor_scalar(win_i[:, :, :], win_f[:, :, :], float(N - 1), None, ALU.min))
            link(nc.vector.tensor_single_scalar(win_i[:, :, :], win_i[:, :, :], 7, ALU.arith_shift_right))
            link(nc.vector.tensor_tensor(win_n[:, 0, :], win_i[:, 1, :], win_i[:, 0, :], ALU.subtract))
            link(nc.vector.tensor_tensor_scan(win_n[:, 1, :], win_n[:, 0, :], zero_r[:, :], 0.0, ALU.add, ALU.add))
            link(nc.vector.memset(win_w[:, :, :], 0.0))
            nc.vector.scalar_tensor_tensor(out=win_w[:, 0, BACK:NG + BACK], in0=win_n[:, 0, :], scalar=32.0,
                                           in1=win_i[:, 0, :], op0=ALU.mult, op1=ALU.add)
            link(nc.vector.tensor_copy(win_w[:, 1, BACK + 1:NG + BACK], win_n[:, 1, 0:NG - 1]))
            nc.vector.scalar_tensor_tensor(out=window[:, :], in0=win_w[:, 1, :], scalar=1024.0, in1=win_w[:, 0, :],
                                           op0=ALU.mult, op1=ALU.add).then_inc(win_ok, 2)


            def largest(q):
                return nc.vector.scalar_tensor_tensor(out=Wt[:, q, :, :], in0=E1[:, q, :, :], scalar=FINITE,
                                                      in1=E2[:, q, :, :], op0=ALU.min, op1=ALU.max)

            def masked(q, w, g, tile):
                for c in range(GC):
                    m = nc.vector.scalar_tensor_tensor(
                        out=S[:, w, c, :], in0=node_id[:, bass.ds(tile * P, P)], scalar=dstT[:, bass.ds(GC * g + c, 1)],
                        in1=Wt[:, q, c, :], op0=ALU.is_equal, op1=ALU.mult)
                return m

            def add(q, tile, count):
                a = acc[:, bass.ds(tile, 1), :, :].rearrange("p t a d -> p (t a) d")
                nc.vector.tensor_tensor(a, a, ps_agg[q][:, :, 0:HALF], ALU.add).then_inc(count, 1)

            def settle(sem_, at):
                dve.wait_ge(sem_, at)
                nc.vector.memset(spare[:, 0:1], 0.0)

            def weigh_extra(g, tile, at):
                dve.wait_ge(xS_ok, at)
                dve.wait_ge(xexp_ok, at)
                largest(2).then_inc(xmax_ok, 1)
                dve.wait_ge(xmax_ok, at + 1)
                masked(2, SR, g, tile).then_inc(xS_ok, 1)

            def add_extra(n_added, tile, at):
                if n_added is not None:
                    dve.wait_ge(added, n_added)
                dve.wait_ge(xagg_ok, at + 1)
                add(2, tile, xadded)
                settle(xadded, at + 1)

            last_tile = dve.alloc_register("last_extra_tile")
            dve.reg_mov(last_tile, 0)

            def extras(g, n_added, word):
                extra = dve.snap(extra_in(word))
                with dve.If(extra > 0):
                    tile, before = dve.snap(tile_in(word)), dve.snap(before_in(word))
                    add_extra(n_added, tile_of(dve.snap(last_tile)), before)
                    weigh_extra(g, tile_of(tile + 1), before + 1)
                    with dve.If(extra > 1):
                        with dve.Fori(1, extra) as n:
                            add_extra(n_added, tile_of(tile + n), before + n)
                            weigh_extra(g, tile_of(tile + n + 1), before + n + 1)
                    dve.reg_mov(last_tile, tile + extra)

            def step_of_group(g, r, i, first=False, words=None):
                words_at = r + BACK
                word = lambda back: dve.snap(regs[words_at - back])
                r %= RING
                if words is None:
                    dve.wait_ge(exp_ok, g + 1)
                    if not (first and r < 2):
                        dve.wait_ge(S_ok, g - 1)
                    largest(r % 2).then_inc(max_ok[r % 2], 1)
                if not (first and r < 3):
                    tile = dve.snap(tile_in(word(3)))
                    if not (first and r < 4):
                        dve.wait_ge(added, g - 3)
                    dve.wait_ge(agg_ok, g - 2)
                    add((r - 3) % 2, tile, added)
                if words is None or words < 1:
                    if not (first and r < 1):
                        tile = dve.snap(tile_in(word(1)))
                        dve.wait_ge(max_ok[(r - 1) % 2], RING // 2 * i + (r + 1) // 2 + 1)
                        masked((r - 1) % 2, (r - 1) % SR, g - 1, tile).then_inc(S_ok, 1)
                if (words is None or words < 1) and not (first and r < 1):
                    extras(g - 1, None if first and r < 3 else g - 2, word(1))

            dve.wait_ge(row_ok, NT)
            dve.wait_ge(d_ok, len(ps_d))
            nc.vector.memset(ps_agg[2][:, :, 0:HALF], 0.0).then_inc(xagg_ok, 1)
            dve.wait_ge(win_ok, 2)
            dve.wait_ge(ids_ok, 1)
            dve.wait_ge(edges_ok, 2)
            window_words(dve, regs, 0, BACK)
            for r in range(RING):
                step_of_group(r, r, 0, first=True)
            with dve.Fori(1, NG // RING) as i:
                window_words(dve, regs, i, BACK)
                for r in range(RING):
                    step_of_group(RING * i + r, r, i)
            for k in range(BACK):
                step_of_group(NG + k, RING + k, NG // RING, words=k)
            dve.wait_ge(added, NG)
            last_word = dve.snap(regs[RING + BACK - 1])
            add_extra(None, tile_of(dve.snap(last_tile)), before_in(last_word) + extra_in(last_word))
            dve.wait_ge(agg_ok, NG)
            den = acc[:, :, 0, ONE]
            link(nc.vector.tensor_single_scalar(rden[:, :], den, 0.0, ALU.is_equal))
            link(nc.vector.tensor_tensor(rden[:, :], rden[:, :], den, ALU.add))
            link(nc.vector.reciprocal(rden[:, :], rden[:, :]))
            nc.vector.memset(spare[:, 0:1], 0.0).then_inc(acc_ok, 1)

            def x1_of(u, s):
                for j in range(2):
                    a = features(2 * u + j)
                    dve.wait_ge(ld_x2[s][j], 16 * (u // 2 + 1) if isinstance(u, int) else u * 8 + 16 - 8 * s)
                    nc.vector.scalar_tensor_tensor(out=a, in0=a, scalar=rden[:, bass.ds(2 * u + j, 1)],
                                                   in1=halves(x_in[:, s, j, :]), op0=ALU.mult, op1=ALU.add).then_inc(x1_ok, 1)
                dve.wait_ge(x1_ok, 2 * u + 2)
                nc.vector.memset(spare[:, 0:1], 0.0)
                for j in range(2):
                    a = features(2 * u + j)
                    m = nc.vector.bn_stats(stats[:, s, j, :], a)
                m.then_inc(stats2_ok, 1)
                if not (isinstance(u, int) and u < 2):
                    dve.wait_ge(rstd2_ok, 2 * u - 2)
                dve.wait_ge(stats2_ok, u + 1)
                nc.vector.memset(spare[:, 1:2], 0.0)
                for j in range(2):
                    m = nc.vector.bn_aggr(mv[:, s, j, :], stats[:, s, j, :])
                m.then_inc(aggr2_ok, 1)

            def normal2(u, s):
                dve.wait_ge(std2_ok, u + 1)
                if not (isinstance(u, int) and u < 2):
                    dve.wait_ge(xn2_ok, 2 * u - 2)
                nc.vector.reciprocal(rstd[:, s, :], std[:, s, :]).then_inc(rstd2_ok, 1)
                dve.wait_ge(rstd2_ok, 2 * u + 1)
                nc.vector.scalar_tensor_tensor(out=shift[:, s, :], in0=mv[:, s, :, 0], scalar=-1.0, in1=rstd[:, s, :],
                                               op0=ALU.mult, op1=ALU.mult).then_inc(rstd2_ok, 1)

            x1_of(0, 0)

            def two_steps(i):
                x1_of(2 * i + 1, 1)
                normal2(2 * i, 0)
                x1_of(2 * i + 2, 0)
                normal2(2 * i + 1, 1)

            two_steps(0)
            with dve.Fori(1, NT // 4 - 1) as i:
                two_steps(i)
            x1_of(NT // 2 - 1, 1)
            normal2(NT // 2 - 2, 0)
            normal2(NT // 2 - 1, 1)

            V = nc.vector
            dve.wait_ge(consts_ok, 2)
            V.tensor_copy(part1[:, :], part_i[:, :])
            V.tensor_copy(count_b[:, :], count_i[:, :])
            V.tensor_copy(beyond[:, :], beyond_i[:, :])
            link(V.tensor_copy(count[:, :], count_i[:, :]))

            def bc_t(ap):
                return ap.unsqueeze(2).to_broadcast([P, NT, NX])

            dve.wait_ge(logit_ps, NT // 2)
            logit = ps_logit[:, 0:NT * NX].rearrange("p (t e) -> p t e", e=NX)
            link(V.tensor_reduce(red[:, :], logit, AX.X, ALU.max))
            V.tensor_tensor(score[:, :, :], logit, bc_t(red[:, :]), ALU.subtract).then_inc(shift_ok, 1)
            dve.wait_ge(exp2_ok, 1)
            link(V.tensor_reduce(red[:, :], pr[:, :, :], AX.X, ALU.add))
            link(V.reciprocal(red[:, :], red[:, :]))
            link(V.tensor_tensor(pr[:, :, :], pr[:, :, :], bc_t(red[:, :]), ALU.mult))
            expert_id = count[:, 0:NX].unsqueeze(1).to_broadcast([P, NT, NX])
            for c in range(2):
                link(V.tensor_reduce(prob[:, c, :], pr[:, :, :], AX.X, ALU.max))
                link(V.tensor_tensor(pick[:, :, :], pr[:, :, :], bc_t(prob[:, c, :]), ALU.is_equal))
                link(V.scalar_tensor_tensor(out=pick[:, :, :], in0=pick[:, :, :], scalar=-float(NX), in1=expert_id,
                                            op0=ALU.mult, op1=ALU.add))
                link(V.tensor_reduce(red[:, :], pick[:, :, :], AX.X, ALU.min))
                link(V.tensor_single_scalar(red[:, :], red[:, :], float(NX), ALU.add))
                link(V.tensor_tensor(pick[:, :, :], expert_id, bc_t(red[:, :]), ALU.is_equal))
                link(V.tensor_tensor(choice[:, :, c, :], pick[:, :, :].rearrange("p t e -> p e t"),
                                     valid[:, c, :].unsqueeze(1).to_broadcast([P, NX, NT]), ALU.mult))
                if c == 0:
                    link(V.scalar_tensor_tensor(out=pr[:, :, :], in0=pick[:, :, :], scalar=-2.0, in1=pr[:, :, :],
                                                op0=ALU.mult, op1=ALU.add))
            flat = choice[:, :, :, :].rearrange("p e c t -> p (e c t)")
            by_item = choice[:, :, :, :].rearrange("p e c t -> p e (c t)")
            V.tensor_reduce(per[:, 0, :], by_item, AX.X, ALU.add).then_inc(cnt_ok, 1)
            link(V.tensor_tensor_scan(rank[:, :, :].rearrange("p e i -> p (e i)"), flat, zeros[:, :], 0.0,
                                      ALU.add, ALU.add))
            dve.wait_ge(cnt_ok, 1)
            link(V.tensor_tensor(per[:, 1, :], rank[:, :, ITEMS - 1], per[:, 0, :], ALU.subtract))
            dve.wait_ge(cnt_ps, 1)
            link(V.tensor_single_scalar(per_i[:, :], ps_sum[:, NX:2 * NX], float(P - 1), ALU.add))
            link(V.tensor_single_scalar(per_i[:, :], per_i[:, :], P.bit_length() - 1, ALU.arith_shift_right))
            link(V.tensor_copy(per[:, 2, :], per_i[:, :]))
            link(V.tensor_tensor_scan(per[:, 3, :], per[:, 2, :], zeros[:, 0:NX], 0.0, ALU.add, ALU.add))
            link(V.tensor_tensor(per[:, 5, :], per[:, 3, :], per[:, 2, :], ALU.subtract))
            link(V.scalar_tensor_tensor(out=per[:, 4, :], in0=per[:, 5, :], scalar=float(P), in1=ps_sum[:, 0:NX],
                                        op0=ALU.mult, op1=ALU.add))
            link(V.scalar_tensor_tensor(out=per[:, 6, :], in0=per[:, 4, :], scalar=-1.0, in1=per[:, 1, :],
                                        op0=ALU.add, op1=ALU.subtract))
            link(V.tensor_tensor(rank[:, :, :], rank[:, :, :], per[:, 6, :].unsqueeze(2).to_broadcast([P, NX, ITEMS]),
                                 ALU.add))
            link(V.tensor_tensor(rank[:, :, :], rank[:, :, :], by_item, ALU.mult))
            link(V.tensor_reduce(pos[:, :], rank[:, :, :].rearrange("p e i -> p i e"), AX.X, ALU.add))
            vflat = valid[:, :, :].rearrange("p c t -> p (c t)")
            link(V.scalar_tensor_tensor(out=pos[:, :], in0=vflat, scalar=float(TILES * P), in1=pos[:, :],
                                        op0=ALU.mult, op1=ALU.add))
            link(V.tensor_single_scalar(pos_i[:, 0, :], pos[:, :], -float(TILES * P), ALU.add))
            link(V.tensor_single_scalar(pos_i[:, 1, :], pos_i[:, 0, :], P.bit_length() - 1, ALU.arith_shift_right))
            link(V.tensor_single_scalar(pos_i[:, 2, :], pos_i[:, 0, :], P - 1, ALU.bitwise_and))
            link(V.tensor_copy(pos_f[:, :, :], pos_i[:, 1:3, :]))
            dve.wait_ge(st_x1, 16 * (NT + 1))
            for s in range(2):
                for j in range(2):
                    dve.wait_ge(st_xn[s][j], 16 * NT // 4)
            dve.wait_ge(xnT_ps, NT // 2)
            tile_id = count_b[:, 0:TILES].unsqueeze(1).to_broadcast([P, ITEMS, TILES])
            V.tensor_tensor(hot_r[:, :, :], pos_f[:, 1, :].unsqueeze(2).to_broadcast([P, ITEMS, P]),
                            count_b[:, :].unsqueeze(1).to_broadcast([P, ITEMS, P]), ALU.is_equal)
            link(V.tensor_tensor(hot_t[:, :, :], pos_f[:, 0, :].unsqueeze(2).to_broadcast([P, ITEMS, TILES]),
                                 tile_id, ALU.is_equal))
            V.tensor_scalar(hot_v[:, 0, :, :], hot_t[:, :, :], part1[:, :], None, ALU.mult)
            V.tensor_tensor(hot_v[:, 1, :, :], hot_t[:, :, :],
                            count[:, 1:ITEMS + 1].unsqueeze(2).to_broadcast([P, ITEMS, TILES]), ALU.mult)\
                .then_inc(hot_ok, 1)
            prob_f = prob[:, :, :].rearrange("p c t -> p (c t)")
            link(V.tensor_copy(prob_b[:, 0, :], prob_f))
            link(V.tensor_tensor(prob_r[:, 0, :], prob_f, prob_b[:, 0, :], ALU.subtract))
            link(V.tensor_copy(prob_b[:, 1, :], prob_r[:, 0, :]))
            link(V.tensor_tensor(prob_r[:, 1, :], prob_r[:, 0, :], prob_b[:, 1, :], ALU.subtract))
            link(V.tensor_copy(prob_b[:, 2, :], prob_r[:, 1, :]))

            def hot_share(v):
                V.tensor_tensor(hot_p[:, v, :, :], hot_t[:, :, :],
                                prob_b[:, v, :].unsqueeze(2).to_broadcast([P, ITEMS, TILES]), ALU.mult)\
                    .then_inc(hot_ok, 1)

            hot_share(0)
            link(V.tensor_tensor(ends[:, :, :], per[0:1, 3, :].unsqueeze(1).to_broadcast([1, TILES, NX]),
                                 count[0:1, 0:TILES].unsqueeze(2).to_broadcast([1, TILES, NX]), ALU.is_le))
            link(V.tensor_reduce(end_n[:, :], ends[:, :, :], AX.X, ALU.add))
            link(V.tensor_single_scalar(rounds[:, 1:2], per[0:1, 3, NX - 1:NX], 3.0 - 4 * ROUNDS_MIN, ALU.add))
            V.tensor_single_scalar(rounds[:, 0:1], rounds[:, 1:2], 2, ALU.arith_shift_right)
            V.tensor_single_scalar(expert_of[:, 2:TILES + 2], end_n[:, :], float(NX - 1), ALU.min)
            dve.wait_ge(inv_ps, 1)
            link(V.tensor_copy(inv[:, 0:2, :].rearrange("p v t -> p (v t)"), ps_inv[:, 0:2 * TILES]))
            link(V.scalar_tensor_tensor(out=inv[:, 2, :], in0=inv[:, 1, :], scalar=float(P), in1=inv[:, 0, :],
                                        op0=ALU.mult, op1=ALU.add))
            link(V.tensor_single_scalar(inv[:, 2, :], inv[:, 2, :], -float(P + 1), ALU.add))
            link(V.tensor_single_scalar(inv[:, 0, :], inv[:, 2, :], float(NTN), ALU.is_ge))
            link(V.scalar_tensor_tensor(out=inv[:, 0, :], in0=inv[:, 0, :], scalar=-float(NTN), in1=inv[:, 2, :],
                                        op0=ALU.mult, op1=ALU.add))
            link(V.tensor_single_scalar(inv[:, 0, :], inv[:, 0, :], 0.0, ALU.max))
            V.tensor_copy(src_row[:, 0:TILES], inv[:, 0, :])
            link(V.tensor_single_scalar(inv[:, 1, :], inv[:, 2, :], 0.0, ALU.is_lt))
            link(V.tensor_tensor(inv[:, 1, :], inv[:, 1, :], beyond[:, :], ALU.mult))
            link(V.tensor_tensor(dst_row[:, 0:TILES], inv[:, 0, :], inv[:, 1, :], ALU.add))
            V.memset(spare[:, 0:1], 0.0).then_inc(routed, 1)
            hot_share(1)
            hot_share(2)
            dve.wait_ge(inv_ps, 2)
            V.tensor_copy(share[:, 0:TILES], ps_share[:, 0:TILES]).then_inc(share_ok, 1)

            def tile_step(i, n, e_mid, e_old, parts):
                s, peeled = i % 2, isinstance(n, int)
                new, mid, old = parts
                if old:
                    dve.wait_ge(hidT_hi, n - 1)
                    nc.vector.tensor_tensor(hidT[:, s, 1, :], ps_hT[:, 0:F], hidT[:, s, 0, :].bitcast(F32),
                                            ALU.subtract).then_inc(hidT_lo, 1)
                if new:
                    dve.wait_ge(x_hi, n + 1)
                    nc.vector.tensor_tensor(xgT[:, s, 1, :], ps_x[:, :], xgT[:, s, 0, :].bitcast(F32),
                                            ALU.subtract).then_inc(x_lo, 1)
                if mid:
                    e = expert_in(dve, e_mid)
                    if not (peeled and n < 3):
                        dve.wait_ge(gelu_ok, n - 2)
                    dve.wait_ge(hid_ps, n)
                    nc.vector.tensor_tensor(hid[:, 1 - s, :], ps_hid[1 - s][:, 0:F],
                                            b1_b[:, bass.ds(e, 1), :].rearrange("p e f -> p (e f)"), ALU.add)\
                        .then_inc(hid_ok, 1)
                if old:
                    e = expert_in(dve, e_old)
                    if not (peeled and n < 4):
                        dve.wait_ge(y_ok, n - 3)
                    dve.wait_ge(y_ps, n - 1)
                    nc.vector.tensor_tensor(y_b[:, s, :], ps_y[s][:, :],
                                            b2_b[:, bass.ds(e, 1), :].rearrange("p e d -> p (e d)"), ALU.add)\
                        .then_inc(yb_ok, 1)

            dve.wait_ge(ld_b, 32)
            over_tiles(dve, regs[0:5], tile_step)


_INS = ["x", "src", "dst", "L0_gnn_W", "L0_gnn_b_w", "L0_gnn_a", "L0_gnn_b_a", "L0_ffn_Wg", "L0_ffn_bg",
        "L0_ffn_W1", "L0_ffn_b1", "L0_ffn_W2", "L0_ffn_b2"]


def kernel(**inputs):
    import numpy as _np
    import concourse.bacc as _bacc
    from concourse import mybir as _mybir
    from concourse.bass_utils import run_bass_kernel_spmd as _run

    nc = _bacc.Bacc("TRN2", target_bir_lowering=False, num_devices=1)
    arrays, args = {}, []
    for name in _INS:
        a = _np.ascontiguousarray(inputs[name])
        if a.ndim == 0:
            a = a.reshape(1)
        arrays[f"in_{name}_dram"] = a
        args.append(nc.dram_tensor(f"in_{name}_dram", a.shape, _mybir.dt.from_np(a.dtype), kind="ExternalInput").ap())
    shape = _np.shape(inputs["x"])
    args.append(nc.dram_tensor("out_0_dram", shape, _mybir.dt.float32, kind="ExternalOutput").ap())
    gnn_moe_kernel(nc, *args)
    r = _run(nc, [arrays], core_ids=[0])
    return r.results[0]["out_0_dram"]
```
